# Optimizing a Trainium2 kernel written in Bass

```python
import numpy as np
import jax
import jax.numpy as jnp

def _softmax(x, axis=-1):
    return jax.nn.softmax(x, axis=axis)

def _gelu(x):
    return jax.nn.gelu(x, approximate=True)

def _silu(x):
    return jax.nn.silu(x)

def _sigmoid(x):
    return jax.nn.sigmoid(x)

def _layernorm(x, axis=-1, eps=1e-05):
    m = jnp.mean(x, axis=axis, keepdims=True)
    v = jnp.var(x, axis=axis, keepdims=True)
    return (x - m) / jnp.sqrt(v + eps)

def _scatter_add(tgt, idx, src, axis=0):
    return tgt.at[idx].add(src)

def _segment_sum(src, seg, n):
    return jax.ops.segment_sum(src, seg, n)
kernel_name = 'mk_conv_attn_hybrid_d2_conv_nhwc256_r4_ce2d47'

def setup_inputs(seed: int=0):
    np.random.seed(seed)
    _w = jnp.asarray

    def _rec_inputs():
        import jax
        import jax.numpy as jnp
        _gk = jax.random.key(seed)
        x = -0.0002091 + 1 * jax.random.normal(jax.random.fold_in(_gk, 1), (32, 56, 56, 64), jnp.float32)
        return x
    x = _rec_inputs()

    def _L0_conv_setup():
        import jax, jax.numpy as jnp
        import numpy as np
        WS = 7
        NH = 4
        HD = 16
        ALPHA = 0.1
        BETA = 0.2
        THETA = 0.5
        EPS = 1e-05

        def dwconv(x, w):
            return jax.lax.conv_general_dilated(x, w, window_strides=(1, 1), padding='SAME', feature_group_count=x.shape[1], dimension_numbers=('NCHW', 'OIHW', 'NCHW'))
        key = jax.random.key(seed)
        ks = jax.random.split(key, 8)
        B, H, W, C = (32, 56, 56, 64)
        s = 0.02
        return {'x': jax.random.normal(ks[0], (B, H, W, C), jnp.float32), 'qkv_w': jax.random.normal(ks[1], (3 * C, C), jnp.float32) * s, 'qkv_b': jnp.zeros((3 * C,), jnp.float32), 'conv3_w': jax.random.normal(ks[2], (C, 1, 3, 3), jnp.float32) * s, 'conv5_w': jax.random.normal(ks[3], (C, 1, 5, 5), jnp.float32) * s, 'conv7_w': jax.random.normal(ks[4], (C, 1, 7, 7), jnp.float32) * s, 'ffn_in_w': jax.random.normal(ks[5], (C, C), jnp.float32) * s, 'ffn_out_w': jax.random.normal(ks[6], (C, C), jnp.float32) * s, 'ln_g': jnp.ones((C,), jnp.float32), 'ln_b': jnp.zeros((C,), jnp.float32)}
    _L0_conv_all = _L0_conv_setup()
    _L0_conv_in = {k: v for k, v in _L0_conv_all.items() if k in ('qkv_w', 'qkv_b', 'conv3_w', 'conv5_w', 'conv7_w', 'ffn_in_w', 'ffn_out_w', 'ln_g', 'ln_b')}
    del _L0_conv_all

    def _L1_attn_setup():
        import jax, jax.numpy as jnp
        import numpy as np
        SEQ, BATCH, IN, HID = (512, 16, 64, 64)
        key = jax.random.key(seed)
        k1, k2, k3, k4, k5 = jax.random.split(key, 5)
        s = 1.0 / np.sqrt(HID)
        return {'x_in': jax.random.normal(k1, (SEQ, BATCH, IN), dtype=jnp.float32), 'W_ih': jax.random.uniform(k2, (HID, IN), jnp.float32, -s, s), 'W_hh': jax.random.uniform(k3, (HID, HID), jnp.float32, -s, s), 'b_ih': jax.random.uniform(k4, (HID,), jnp.float32, -s, s), 'b_hh': jax.random.uniform(k5, (HID,), jnp.float32, -s, s)}
    _L1_attn_all = _L1_attn_setup()
    _L1_attn_in = {k: v for k, v in _L1_attn_all.items() if k in ('W_ih', 'W_hh', 'b_ih', 'b_hh')}
    del _L1_attn_all

    def _L1_ffn_setup():
        import jax, jax.numpy as jnp
        import numpy as np
        TOP_K = 2
        LN_EPS = 1e-05
        key = jax.random.key(seed)
        ks = jax.random.split(key, 8)
        B, S, D, E, H = (16, 256, 64, 8, 256)
        x = jax.random.normal(ks[0], (B, S, D), dtype=jnp.float32)
        Wr = jax.random.normal(ks[1], (D, E), dtype=jnp.float32) * 0.1
        br = jnp.zeros((E,), dtype=jnp.float32)
        ln_g = jnp.ones((E, D), dtype=jnp.float32)
        ln_b = jnp.zeros((E, D), dtype=jnp.float32)
        W1 = jax.random.normal(ks[2], (E, D, H), dtype=jnp.float32) * (1.0 / np.sqrt(D))
        b1 = jnp.zeros((E, H), dtype=jnp.float32)
        W2 = jax.random.normal(ks[3], (E, H, D), dtype=jnp.float32) * (1.0 / np.sqrt(H))
        b2 = jnp.zeros((E, D), dtype=jnp.float32)
        return {'x': x, 'Wr': Wr, 'br': br, 'ln_g': ln_g, 'ln_b': ln_b, 'W1': W1, 'b1': b1, 'W2': W2, 'b2': b2}
    _L1_ffn_all = _L1_ffn_setup()
    _L1_ffn_in = {k: v for k, v in _L1_ffn_all.items() if k in ('Wr', 'br', 'ln_g', 'ln_b', 'W1', 'b1', 'W2', 'b2')}
    del _L1_ffn_all
    return {'x': x, 'L0_conv_qkv_w': _L0_conv_in['qkv_w'], 'L0_conv_qkv_b': _L0_conv_in['qkv_b'], 'L0_conv_conv3_w': _L0_conv_in['conv3_w'], 'L0_conv_conv5_w': _L0_conv_in['conv5_w'], 'L0_conv_conv7_w': _L0_conv_in['conv7_w'], 'L0_conv_ffn_in_w': _L0_conv_in['ffn_in_w'], 'L0_conv_ffn_out_w': _L0_conv_in['ffn_out_w'], 'L0_conv_ln_g': _L0_conv_in['ln_g'], 'L0_conv_ln_b': _L0_conv_in['ln_b'], 'L1_attn_W_ih': _L1_attn_in['W_ih'], 'L1_attn_W_hh': _L1_attn_in['W_hh'], 'L1_attn_b_ih': _L1_attn_in['b_ih'], 'L1_attn_b_hh': _L1_attn_in['b_hh'], 'L1_ffn_Wr': _L1_ffn_in['Wr'], 'L1_ffn_br': _L1_ffn_in['br'], 'L1_ffn_ln_g': _L1_ffn_in['ln_g'], 'L1_ffn_ln_b': _L1_ffn_in['ln_b'], 'L1_ffn_W1': _L1_ffn_in['W1'], 'L1_ffn_b1': _L1_ffn_in['b1'], 'L1_ffn_W2': _L1_ffn_in['W2'], 'L1_ffn_b2': _L1_ffn_in['b2']}

def reference(x, L0_conv_qkv_w, L0_conv_qkv_b, L0_conv_conv3_w, L0_conv_conv5_w, L0_conv_conv7_w, L0_conv_ffn_in_w, L0_conv_ffn_out_w, L0_conv_ln_g, L0_conv_ln_b, L1_attn_W_ih, L1_attn_W_hh, L1_attn_b_ih, L1_attn_b_hh, L1_ffn_Wr, L1_ffn_br, L1_ffn_ln_g, L1_ffn_ln_b, L1_ffn_W1, L1_ffn_b1, L1_ffn_W2, L1_ffn_b2):
    import jax
    import jax.numpy as jnp

    def _L0_conv_ref(x, qkv_w, qkv_b, conv3_w, conv5_w, conv7_w, ffn_in_w, ffn_out_w, ln_g, ln_b):
        import jax, jax.numpy as jnp
        import numpy as np
        WS = 7
        NH = 4
        HD = 16
        ALPHA = 0.1
        BETA = 0.2
        THETA = 0.5
        EPS = 1e-05

        def dwconv(x, w):
            return jax.lax.conv_general_dilated(x, w, window_strides=(1, 1), padding='SAME', feature_group_count=x.shape[1], dimension_numbers=('NCHW', 'OIHW', 'NCHW'))
        B, H, W, C = x.shape
        n1, n2 = (H // WS, W // WS)
        xw = x.reshape(B, WS, n1, WS, n2, C).transpose(0, 2, 4, 1, 3, 5)
        xw = xw.reshape(B * n1 * n2, WS, WS, C)
        b, hw = (B * n1 * n2, WS * WS)
        shortcut = xw.reshape(b, hw, NH, HD).transpose(0, 2, 1, 3)
        qkv = xw.reshape(b, hw, C) @ qkv_w.T + qkv_b
        qkv = qkv.reshape(b, hw, 3, NH, HD).transpose(2, 0, 3, 1, 4)
        q, k, v = (qkv[0], qkv[1], qkv[2])
        v = ALPHA * v + shortcut
        shortcut2 = v.transpose(0, 2, 1, 3).reshape(b, WS, WS, C)
        attn = jax.nn.softmax(jnp.einsum('bnqd,bnkd->bnqk', q, k) * HD ** (-0.5), axis=-1)
        x_spa = jnp.einsum('bnqk,bnkd->bnqd', attn, v)
        x_spa = x_spa.transpose(0, 2, 1, 3).reshape(b, WS, WS, C)
        xc = v.transpose(0, 1, 3, 2).reshape(b, C, WS, WS)
        c3 = dwconv(xc, conv3_w).transpose(0, 2, 3, 1)
        c5 = dwconv(xc, conv5_w).transpose(0, 2, 3, 1)
        c7 = dwconv(xc, conv7_w).transpose(0, 2, 3, 1)
        x_spa = 0.25 * (x_spa + c3 + c5 + c7)
        xw = BETA * x_spa + shortcut2
        xo = xw.reshape(B, n1, n2, WS, WS, C).transpose(0, 3, 1, 4, 2, 5).reshape(B, H, W, C)
        y = jax.nn.silu(xo @ ffn_in_w.T) @ ffn_out_w.T
        xo = THETA * y + xo
        mu = jnp.mean(xo, axis=-1, keepdims=True)
        var = jnp.var(xo, axis=-1, keepdims=True)
        return (xo - mu) / jnp.sqrt(var + EPS) * ln_g + ln_b

    def _L1_attn_ref(x_in, W_ih, W_hh, b_ih, b_hh):
        import jax, jax.numpy as jnp
        import numpy as np
        SEQ, BATCH, IN, HID = (512, 16, 64, 64)
        xp = jnp.einsum('tbi,hi->tbh', x_in, W_ih) + b_ih + b_hh
        h0 = jnp.zeros((x_in.shape[1], W_hh.shape[0]), dtype=x_in.dtype)

        def step(h, xp_t):
            h_new = jnp.tanh(xp_t + h @ W_hh.T)
            return (h_new, h_new)
        _, hiddens = jax.lax.scan(step, h0, xp)
        return hiddens

    def _L1_ffn_ref(x, Wr, br, ln_g, ln_b, W1, b1, W2, b2):
        import jax, jax.numpy as jnp
        import numpy as np
        TOP_K = 2
        LN_EPS = 1e-05
        B, S, D = x.shape
        N = B * S
        xt = x.reshape(N, D)
        logits = xt @ Wr + br
        probs = jax.nn.softmax(logits, axis=-1)
        top_p, top_idx = jax.lax.top_k(probs, TOP_K)
        weights = top_p / top_p.sum(axis=-1, keepdims=True)
        mu = xt.mean(axis=-1, keepdims=True)
        var = ((xt - mu) ** 2).mean(axis=-1, keepdims=True)
        xn = (xt - mu) * jax.lax.rsqrt(var + LN_EPS)
        xe = xn[None, :, :] * ln_g[:, None, :] + ln_b[:, None, :]
        h = jax.nn.gelu(jnp.einsum('end,edh->enh', xe, W1) + b1[:, None, :], approximate=False)
        y = jnp.einsum('enh,ehd->end', h, W2) + b2[:, None, :]
        y_tok = jnp.transpose(y, (1, 0, 2))
        sel = jnp.take_along_axis(y_tok, top_idx[:, :, None], axis=1)
        out = (weights[:, :, None] * sel).sum(axis=1)
        return out.reshape(B, S, D)

    def _gn(v, G=32, eps=1e-05):
        B_, H_, W_, C_ = v.shape
        g = v.reshape(B_, H_, W_, G, C_ // G)
        m = jnp.mean(g, axis=(1, 2, 4), keepdims=True)
        s = jnp.var(g, axis=(1, 2, 4), keepdims=True)
        return ((g - m) / jnp.sqrt(s + eps)).reshape(v.shape)

    def _ln_c(v, eps=1e-06):
        m = jnp.mean(v, axis=-1, keepdims=True)
        s = jnp.var(v, axis=-1, keepdims=True)
        return (v - m) / jnp.sqrt(s + eps)

    def _ln_t(v, eps=1e-05):
        m = jnp.mean(v, axis=-1, keepdims=True)
        s = jnp.var(v, axis=-1, keepdims=True)
        return (v - m) / jnp.sqrt(s + eps)

    def _to_tokens(v):
        B_, H_, W_, C_ = v.shape
        return v.reshape(B_, H_ * W_, C_)

    def _from_tokens(t, like):
        return t.reshape(like.shape)
    x = _L0_conv_ref(x, L0_conv_qkv_w, L0_conv_qkv_b, L0_conv_conv3_w, L0_conv_conv5_w, L0_conv_conv7_w, L0_conv_ffn_in_w, L0_conv_ffn_out_w, L0_conv_ln_g, L0_conv_ln_b)
    t = _to_tokens(x)
    t = t + _L1_attn_ref(_ln_t(t), L1_attn_W_ih, L1_attn_W_hh, L1_attn_b_ih, L1_attn_b_hh)
    t = t + _L1_ffn_ref(_ln_t(t), L1_ffn_Wr, L1_ffn_br, L1_ffn_ln_g, L1_ffn_ln_b, L1_ffn_W1, L1_ffn_b1, L1_ffn_W2, L1_ffn_b2)
    x = _from_tokens(t, x)
    return x

_drawn_inputs = setup_inputs


def setup_inputs(seed=0):
    import zlib

    import numpy as np

    out = dict(_drawn_inputs(seed))
    spreads = {'L0_conv_qkv_b': (0.0, 0.1),
     'L0_conv_ln_g': (1.0, 0.2),
     'L0_conv_ln_b': (0.0, 0.1),
     'L1_ffn_br': (0.0, 0.1),
     'L1_ffn_ln_g': (1.0, 0.2),
     'L1_ffn_ln_b': (0.0, 0.1),
     'L1_ffn_b1': (0.0, 0.1),
     'L1_ffn_b2': (0.0, 0.1)}
    factors = {'L0_conv_conv3_w': 3.724, 'L0_conv_conv5_w': 3.151}
    for name, (base, spread) in spreads.items():
        noise = np.random.default_rng([zlib.crc32(name.encode()), seed]).standard_normal(out[name].shape)
        drawn = base * np.exp(spread * noise) if base else spread * noise
        out[name] = jnp.asarray(drawn.astype(out[name].dtype))
    for name, factor in factors.items():
        out[name] = (out[name] * factor).astype(out[name].dtype)
    return out
```

```python
from contextlib import ExitStack

import concourse.bass as bass
from concourse import mybir

F32 = mybir.dt.float32
F32R = mybir.dt.float32r
BF16 = mybir.dt.bfloat16
ALU = mybir.AluOpType
ACT = mybir.ActivationFunctionType
AX = mybir.AxisListType

IMAGES, SIDE, CH = 32, 56, 64
WS = 7
NWIN = SIDE // WS
TOK = WS * WS
HEADS, HD = 4, 16
EXPERTS, HID = 8, 256
LN_EPS = 1e-5
PAD = 64
GROUP = 2
CHUNKS = 4 * GROUP
CW = 8 * TOK
UNITS = 4 * CHUNKS
PAIRS = 2 * UNITS
ROWS2 = 2 * TOK
HW2 = CW * 2
HALVES = IMAGES * 2
BIG = 3.0e38
OFF = 2 * WS - 1
ITERS = IMAGES // GROUP
WLOADS = 32
MLOADS = 12
PREP_STEPS = 9
M_STEPS = 5
ROUTER_STEPS = 19
PARTS = 3
GROWS = PARTS * 2 * EXPERTS
PRIME = 40


class Sem:

    def __init__(self, handle, per, step=1):
        self.h, self.per, self.step = handle, per, step

    def upto(self, i, n):
        return i * (self.per * self.step) + (PRIME + n) * self.step


def constants():
    import numpy as np

    c = np.zeros((128, 3 * 128 + HEADS + EXPERTS), np.float32)
    eye = np.eye(128, dtype=np.float32)
    mean = np.kron(np.eye(2), np.full((CH, CH), 1.0 / CH)).astype(np.float32)
    c[:, 0:128] = eye
    c[:, 128:256] = eye - mean
    c[:, 256:384] = mean
    for h in range(HEADS):
        c[:, 384 + h] = (np.arange(128) % CH) // HD == h
    c[:, 388:396] = EXPERTS - np.arange(EXPERTS)
    return c


def selectors():
    import numpy as np

    c = np.zeros((PARTS, 2, EXPERTS, EXPERTS, 2, CH), np.float32)
    for j in range(2):
        for e in range(EXPERTS):
            c[:, j, e, e, j, :] = 1
    return c.reshape(GROWS, EXPERTS, 128)


def build(nc, A):
    with ExitStack() as ctx:
        program(nc, A, ctx)


def program(nc, A, ctx):
    def sb(name, shape, dt=F32, to=ctx):
        return to.enter_context(nc.sbuf_tensor(name, shape, dt))

    all_sems = []

    def sem(name, per=1, step=1):
        s = Sem(ctx.enter_context(nc.semaphore(name)), per, step)
        all_sems.append(s)
        return s

    PS = ctx.enter_context(nc.psum_tensor("banks", [128, 8, 512], F32))

    def bank(b):
        return PS[:, b, :]

    t2_dram = nc.dram_tensor("t2_scratch", (HALVES, 128, HW2), F32, kind="Internal").ap()
    xn_dram = nc.dram_tensor("xn_scratch", (HALVES, 128, HW2), F32, kind="Internal").ap()
    gate_dram = nc.dram_tensor("gate_scratch", (HALVES, GROWS, HW2), BF16, kind="Internal").ap()
    taps_dram = nc.dram_tensor("taps_scratch", (WS, CH, OFF * WS), F32, kind="Internal").ap()

    const = sb("const", [128, 396])
    ident = const[:, 0:128]
    centre = const[:, 128:256]
    meanm = const[:, 256:384]
    headmask = const[:, 384:388]
    rank = const[0:ROWS2, 388:396]

    phase1 = ExitStack()

    def sa(name, shape, dt=F32):
        return sb(name, shape, dt, phase1)

    small = sa("small", [128, 16])
    bq, bk, lng, lnb, brnn, brnn2, eps_c, eps2_c = (small[:, k:k + 1] for k in range(8))
    wq = sa("wq", [128, 128])
    wk = sa("wk", [128, 128])
    wv = sa("wv", [128, CH])
    bv = sa("bv", [128, CH])
    w_in = sa("w_in", [128, 128])
    w_out = sa("w_out", [128, 128])
    w_outc = sa("w_outc", [128, 128])
    w_ih = sa("w_ih", [128, 128])
    w_hh = sa("w_hh", [128, 128])
    w_r = sa("w_r", [128, 2 * EXPERTS])
    b_r = sa("b_r", [ROWS2, 2 * EXPERTS])
    conv_m = sa("conv_m", [128, CH, 2, PAD])
    x_in = sa("x_in", [ROWS2, GROUP, 2, 2, 8, CH])
    xT = sa("xT", [128, GROUP, 4, 8, TOK])
    x_diag = sa("x_diag", [128, 2, 8, 3, PAD])
    q_diag = sa("q_diag", [128, 2, 8, 2, PAD])
    k_sb = sa("k_sb", [128, 1, 8, TOK])
    k_heads = sa("k_heads", [128, 2, 8, HEADS, TOK])
    v_swap = sa("v_swap", [128, 1, 8, CH])
    v_all = sa("v_all", [128, CH, PAIRS])
    v_heads = sa("v_heads", [128, 2, 8, 2, 2, 2, HD + 1])
    probs = sa("probs", [128, 3, 2, HEADS, PAD])
    probsT = sa("probsT", [128, 2, 512])
    rden = sa("rden", [128, 2, 4, 2])
    xo = sa("xo", [128, PAIRS, CH])
    xoT = sa("xoT", [128, CHUNKS * CW])
    ffn_u = sa("ffn_u", [128, CHUNKS * CW])
    hid = sa("hid", [128, 4 * CW])
    tmp = sa("tmp", [128, 2, CW])
    sq = sa("sq", [128, 2, CW])
    sd = sa("sd", [128, 2, CW])
    rs = sa("rs", [128, 2, CW])
    xn = sa("xn", [128, 2, CW])
    lg = sa("lg", [ROWS2, 2 * UNITS, EXPERTS])
    oh1 = sa("oh1", [ROWS2, 2 * UNITS, EXPERTS])
    gate3 = sa("gate3", [ROWS2, UNITS, PARTS, 2 * EXPERTS], BF16)
    ident_b = sa("ident_b", [128, 128], BF16)
    r_small = sa("r_small", [128, 8, 2 * UNITS])
    mx = sa("mx", [128, 2, 8])
    tT = xT[:].rearrange("p g r w t -> p (g r w t)")
    z1 = xoT
    t2 = ffn_u
    zz = tmp
    gate_rest = oh1
    gate = lg
    x_rows = xo[0:ROWS2].rearrange("p (m u w s) k -> p m u w s k", m=GROUP, u=2, w=8)
    gateT = k_heads[0:GROWS].rearrange("p a w h t -> p (a w h t)")[:, 0:CHUNKS * CW // 2].bitcast(BF16)
    oh2 = xo[0:ROWS2, 0:2 * UNITS * EXPERTS // CH, :].rearrange("p a b -> p (a b)").rearrange(
        "p (g e) -> p g e", e=EXPERTS)
    taps = xo[0:CH, 0:3, :].rearrange("p a b -> p (a b)")[:, 0:OFF * OFF]
    spread = xo[0:CH, 3:13, :].rearrange("p a b -> p (a b)")[:, 0:WS * OFF * WS].rearrange(
        "p (x u v) -> p x u v", x=WS, u=OFF)
    raw3, raw5, raw7 = lg[0:CH, 0:2, :], lg[0:CH, 8:12, :], lg[0:CH, 16:23, :]
    raw3 = raw3.rearrange("p a b -> p (a b)")[:, 0:9]
    raw5 = raw5.rearrange("p a b -> p (a b)")[:, 0:25]
    raw7 = raw7.rearrange("p a b -> p (a b)")[:, 0:49]
    phase1.close()

    phase2 = ExitStack()

    def sm(name, shape, dt=F32):
        return sb(name, shape, dt, phase2)

    w1 = sm("w1", [128, EXPERTS, HID])
    w1hi = sm("w1hi", [128, EXPERTS, HID], F32R)
    w1lo = sm("w1lo", [128, EXPERTS, HID], F32R)
    w2 = sm("w2", [128, EXPERTS, 2, CH])
    b1 = sm("b1", [128, EXPERTS, 2])
    b2 = sm("b2", [128, EXPERTS])
    ge = sm("ge", [128, EXPERTS])
    be = sm("be", [128, EXPERTS])
    xnl = sm("xnl", [128, 2, HW2])
    t2l = sm("t2l", [128, 2, HW2])
    gatel = sm("gatel", [GROWS, 2, HW2], BF16)
    sel = sm("sel", [GROWS, EXPERTS, 128])
    sel_b = sm("sel_b", [GROWS, EXPERTS, 128], BF16)
    xs = sm("xs", [128, 2, 2, CW], F32R)
    g = sm("g", [128, 4, 2, CW])
    wrep = sm("wrep", [128, 2, CW])
    yw = sm("yw", [128, 2, CW])
    acc = sm("acc", [128, 2, CW])
    ot = sm("ot", [ROWS2, 2, 512])
    phase2.close()

    zeroed = sem("zeroed")
    passed = sem("passed")
    wloaded = sem("wloaded")
    taps_in = sem("taps_in")
    taps_step = sem("taps_step")
    taps_saved = sem("taps_saved")
    conv_w = sem("conv_w")
    prepared = sem("prepared")
    outc_mm = sem("outc_mm")
    phase1_end = sem("phase1_end")

    x_loaded = sem("x_loaded", 8 * GROUP, 16)
    rows_done = sem("rows_done", 1)
    xt_mm = sem("xt_mm", 8)
    xt_done = sem("xt_done", 8)
    q_mm = sem("q_mm", CHUNKS)
    k_mm = sem("k_mm", CHUNKS)
    v_mm = sem("v_mm", CHUNKS)
    vs_mm = sem("vs_mm", CHUNKS)
    xd_done = sem("xd_done", CHUNKS)
    q_done = sem("q_done", CHUNKS)
    k_done = sem("k_done", CHUNKS)
    kh_done = sem("kh_done", CHUNKS)
    v_done = sem("v_done", CHUNKS)
    vs_done = sem("vs_done", CHUNKS)
    vh_done = sem("vh_done", CHUNKS)
    s_mm = sem("s_mm", UNITS)
    max_done = sem("max_done", UNITS)
    sub_done = sem("sub_done", UNITS)
    exp_done = sem("exp_done", UNITS)
    pt_mm = sem("pt_mm", UNITS)
    pt_done = sem("pt_done", UNITS)
    o_mm = sem("o_mm", UNITS)
    rden_done = sem("rden_done", UNITS)
    o_done = sem("o_done", UNITS)
    conv_mm = sem("conv_mm", 8)
    conv_done = sem("conv_done", 8)
    xot_mm = sem("xot_mm", CHUNKS)
    xot_done = sem("xot_done", CHUNKS)
    f_mm = sem("f_mm", CHUNKS)
    th_done = sem("th_done", CHUNKS)
    u_done = sem("u_done", CHUNKS)
    d_mm = [sem(f"d_mm{n}", CHUNKS) for n in range(3)]
    sq_done = [sem(f"sq_done{n}", CHUNKS) for n in range(3)]
    var_mm = [sem(f"var_mm{n}", CHUNKS) for n in range(3)]
    sd_done = [sem(f"sd_done{n}", CHUNKS) for n in range(3)]
    rs_done = [sem(f"rs_done{n}", CHUNKS) for n in range(3)]
    mul_done = [sem(f"mul_done{n}", CHUNKS) for n in range(3)]
    t_done = sem("t_done", CHUNKS)
    sd2_done = sem("sd2_done", CHUNKS)
    rs2_done = sem("rs2_done", CHUNKS)
    xn_done = sem("xn_done", CHUNKS)
    h_mm = sem("h_mm", CHUNKS)
    h_done = sem("h_done", CHUNKS)
    t2_done = sem("t2_done", CHUNKS)
    lg_mm = sem("lg_mm", CHUNKS)
    lg_done = sem("lg_done", CHUNKS)
    r_step = sem("r_step", ROUTER_STEPS)
    dl_done = sem("dl_done", 1)
    gth_done = sem("gth_done", 1)
    gate_done = sem("gate_done", 1)
    gt_mm = sem("gt_mm", CHUNKS)
    gt_done = sem("gt_done", CHUNKS)
    t2_stored = sem("t2_stored", CHUNKS, 16)
    xn_stored = [sem(f"xn_stored{k}", CHUNKS // 2, 16) for k in range(2)]
    gate_stored = sem("gate_stored", 4, 16)

    E = EXPERTS
    C2 = 4
    m_wloaded = sem("m_wloaded")
    m_step = sem("m_step")
    m_bias_mm = sem("m_bias_mm")
    half_in = [sem(f"half_in{k}", 3, 16) for k in range(2)]
    hi_done = sem("hi_done", C2)
    xs_done = sem("xs_done", C2)
    wr_mm = sem("wr_mm", C2 * E)
    wr_done = sem("wr_done", C2 * E)
    a_mm = sem("a_mm", C2 * E * 2)
    g_done = sem("g_done", C2 * E * 2)
    y_mm = sem("y_mm", C2 * E)
    yw_done = sem("yw_done", C2 * E)
    acc_done = sem("acc_done", C2 * E)
    ot_mm = sem("ot_mm", C2)
    ot_done = sem("ot_done", C2)
    out_stored = [sem(f"out_stored{k}", C2, 16) for k in range(2)]

    x_v = A["x"].rearrange("b (a s r u) (c w) k -> b s r u a c (w k)", a=WS, s=2, r=2, u=2, c=WS, w=8)
    out_v = A["out"].rearrange("b (a s r) (c w) k -> b r s a c (w k)", a=WS, s=2, r=4, c=WS, w=8)

    block = ctx.enter_context(nc.Block())

    def end_of_phase1(eng):
        eng.drain().then_inc(phase1_end.h, 1)
        eng.wait_ge(phase1_end.h, PRIME + 5)

    @block.sync
    def _(sp):
        count = [0]

        def load(dst, src):
            sp.dma_start(dst, src).then_inc(wloaded.h, 16)
            count[0] += 1

        load(const[:], A["const"])
        sp.wait_ge(zeroed.h, PRIME + 2)
        for s in range(2):
            lo, hi = 64 * s, 64 * s + 64
            load(wq[lo:hi, lo:hi], A["qkv_wT"][:, 0:64])
            load(wk[lo:hi, lo:hi], A["qkv_wT"][:, 64:128])
            load(wv[lo:hi, :], A["qkv_wT"][:, 128:192])
            load(w_in[lo:hi, lo:hi], A["ffn_in_wT"])
            load(w_out[lo:hi, lo:hi], A["ffn_out_w"])
            load(w_ih[lo:hi, lo:hi], A["W_ihT"])
            load(w_hh[lo:hi, lo:hi], A["W_hhT"])
            load(w_r[lo:hi, E * s:E * s + E], A["Wr"])
            load(b_r[:, E * s:E * s + E], A["br"].partition_broadcast(ROWS2))
            load(bq[lo:hi], A["qkv_b"][0:64].unsqueeze(1))
            load(bk[lo:hi], A["qkv_b"][64:128].unsqueeze(1))
            load(lng[lo:hi], A["ln_g"].unsqueeze(1))
            load(lnb[lo:hi], A["ln_b"].unsqueeze(1))
            load(brnn[lo:hi], A["b_ih"].unsqueeze(1))
            load(brnn2[lo:hi], A["b_hh"].unsqueeze(1))
        load(bv[:], A["qkv_b"][128:192].partition_broadcast(128))
        assert count[0] == WLOADS
        for dst, name in ((raw3, "conv3f"), (raw5, "conv5f"), (raw7, "conv7f")):
            sp.dma_start(dst, A[name]).then_inc(taps_in.h, 16)

        def load_x(image0):
            for m in range(GROUP):
                for s in range(2):
                    for r in range(2):
                        for u in range(2):
                            sp.dma_start(x_in[TOK * r:TOK * r + TOK, m, s, u].rearrange("p w k -> p (w k)"),
                                         x_v[image0 + m, s, r, u]).then_inc(x_loaded.h, 16)

        load_x(0)
        sp.wait_ge(taps_step.h, PRIME + 6)
        sp.dma_start(taps_dram.rearrange("x c n -> c x n"), spread.rearrange("p x u v -> p x (u v)")
                     ).then_inc(taps_saved.h, 16)
        sp.wait_ge(taps_saved.h, PRIME + 16)
        sp.wait_ge(zeroed.h, PRIME + 2)
        for s in range(2):
            for y in range(WS):
                p = 64 * s + WS * y
                sp.dma_start(conv_m[p:p + WS, :, s, 0:TOK],
                             taps_dram[:, :, WS * (WS - 1 - y):WS * (WS - 1 - y) + TOK]).then_inc(conv_w.h, 16)

        def iteration(i, following):
            if following:
                sp.wait_ge(rows_done.h, rows_done.upto(i, 1))
                load_x((i + 1) * GROUP)
            for c in range(CHUNKS):
                sp.wait_ge(t2_done.h, t2_done.upto(i, c + 1))
                sp.dma_start(t2_dram[i * 4 + c // 2, :, (c % 2) * CW:(c % 2) * CW + CW],
                             t2[:, c * CW:c * CW + CW]).then_inc(t2_stored.h, 16)
            for c in range(CHUNKS):
                sp.wait_ge(xn_done.h, xn_done.upto(i, c + 1))
                sp.dma_start(xn_dram[i * 4 + c // 2, :, (c % 2) * CW:(c % 2) * CW + CW],
                             xn[:, c % 2, :]).then_inc(xn_stored[c % 2].h, 16)
            for q in range(4):
                sp.wait_ge(gt_done.h, gt_done.upto(i, 2 * q + 2))
                sp.dma_start(gate_dram[i * 4 + q], gateT[:, q * HW2:q * HW2 + HW2]).then_inc(gate_stored.h, 16)

        with sp.Fori(0, ITERS - 1) as i:
            iteration(i, True)
        iteration(ITERS - 1, False)
        sp.wait_ge(t2_stored.h, t2_stored.upto(ITERS, 0))
        for k in range(2):
            sp.wait_ge(xn_stored[k].h, xn_stored[k].upto(ITERS, 0))
        sp.wait_ge(gate_stored.h, gate_stored.upto(ITERS, 0))
        end_of_phase1(sp)

        count[0] = 0

        def mload(dst, src):
            sp.dma_start(dst, src).then_inc(m_wloaded.h, 16)
            count[0] += 1

        for s in range(2):
            lo, hi = 64 * s, 64 * s + 64
            mload(w1[lo:hi], A["W1"].rearrange("e k h -> k e h"))
            mload(b2[lo:hi], A["b2T"])
            mload(ge[lo:hi], A["ln_geT"])
            mload(be[lo:hi], A["ln_beT"])
        for m in range(2):
            mload(w2[:, :, m, :], A["W2"].rearrange("e (m h) k -> m h e k", m=2)[m])
        mload(b1[:], A["b1P"])
        mload(sel[:], A["sel"])
        assert count[0] == MLOADS

        def load_half(image, k):
            half = image * 2 + k
            sp.dma_start(xnl[:, k, :], xn_dram[half]).then_inc(half_in[k].h, 16)
            sp.dma_start(gatel[:, k, :], gate_dram[half]).then_inc(half_in[k].h, 16)
            sp.dma_start(t2l[:, k, :], t2_dram[half]).then_inc(half_in[k].h, 16)

        for k in range(2):
            load_half(0, k)

        def m_iteration(i, following):
            for c in range(C2):
                sp.wait_ge(ot_done.h, ot_done.upto(i, c + 1))
                for s in range(2):
                    sp.dma_start(out_v[i, c, s], ot[TOK * s:TOK * s + TOK, c % 2, :]).then_inc(out_stored[c % 2].h, 16)
                if following and c % 2 == 1:
                    sp.wait_ge(wr_mm.h, wr_mm.upto(i, (c + 1) * E))
                    sp.wait_ge(xs_done.h, xs_done.upto(i, c + 1))
                    load_half(i + 1, c // 2)

        with sp.Fori(0, IMAGES - 1) as i:
            m_iteration(i, True)
        m_iteration(IMAGES - 1, False)
        for k in range(2):
            sp.wait_ge(out_stored[k].h, out_stored[k].upto(IMAGES, 0))

    @block.gpsimd
    def _(pool):
        for s in all_sems:
            pool.sem_inc(s.h, PRIME * s.step)
        for t in (wq, wk, w_in, w_out, w_ih, w_hh, w_r):
            nc.gpsimd.memset(t[:], 0.0)
        nc.gpsimd.memset(conv_m[:], 0.0).then_inc(zeroed.h, 1)
        nc.gpsimd.memset(x_diag[:], 0.0)
        nc.gpsimd.memset(q_diag[:], 0.0)
        nc.gpsimd.memset(probs[:], 0.0)
        nc.gpsimd.memset(hid[:], 0.0)
        nc.gpsimd.memset(v_heads[:], 0.0).then_inc(zeroed.h, 1)
        pool.wait_ge(zeroed.h, PRIME + 2)
        for k in range(2):
            part = v_heads[64 * k:64 * k + 64].rearrange("p a w h s i d -> p (a w h s) i d")
            last = nc.gpsimd.memset(part[:, :, k, HD:HD + 1], 20.0)
        last.then_inc(zeroed.h, 1)
        pool.wait_ge(zeroed.h, PRIME + 3)

        def settle():
            pool.sem_inc(passed.h, 1)

        def heads_of_k(i, c):
            pool.wait_ge(xd_done.h, xd_done.upto(i, c + 1))
            pool.wait_ge(k_done.h, k_done.upto(i, c + 1))
            pool.wait_ge(gate_stored.h, gate_stored.upto(i, 0))
            pool.wait_ge(s_mm.h, s_mm.upto(i, 4 * (c - 1)))
            settle()
            for h in range(HEADS):
                last = nc.gpsimd.tensor_scalar(k_heads[:, c % 2, :, h, :], k_sb[:, 0], headmask[:, h:h + 1], 1.0,
                                               ALU.mult, ALU.mult)
            last.then_inc(kh_done.h, 1)

        def diagonal_x(i, c):
            m, rq = c // 4, c % 4
            pool.wait_ge(xt_done.h, xt_done.upto(i, 4 * m + 4))
            pool.wait_ge(vh_done.h, vh_done.upto(i, c))
            pool.wait_ge(v_mm.h, v_mm.upto(i, c - 1))
            pool.wait_ge(vs_mm.h, vs_mm.upto(i, c - 1))
            settle()
            for s, blk in ((0, 0), (1, 1), (0, 2)):
                last = nc.gpsimd.tensor_copy(x_diag[64 * s:64 * s + 64, c % 2, :, blk, 0:TOK],
                                             xT[64 * s:64 * s + 64, m, rq])
            last.then_inc(xd_done.h, 1)

        def heads_of_v(i, c):
            pool.wait_ge(kh_done.h, kh_done.upto(i, c + 1))
            pool.wait_ge(v_done.h, v_done.upto(i, c + 1))
            pool.wait_ge(vs_done.h, vs_done.upto(i, c + 1))
            pool.wait_ge(o_mm.h, o_mm.upto(i, 4 * (c - 1)))
            settle()
            for k in range(2):
                p = slice(64 * k, 64 * k + 64)
                for s in range(2):
                    if s == k:
                        src = v_all[p].rearrange("p (h i d) n -> p i n h d", h=2, i=2)[:, k, 8 * c:8 * c + 8]
                    else:
                        src = v_swap[p, 0].rearrange("p w (h i d) -> p i w h d", h=2, i=2)[:, k]
                    last = nc.gpsimd.tensor_copy(v_heads[p, c % 2, :, :, s, k, 0:HD], src)
            last.then_inc(vh_done.h, 1)

        def regroup_x(i):
            pool.wait_ge(vh_done.h, vh_done.upto(i, 0))
            pool.wait_ge(x_loaded.h, x_loaded.upto(i, 8 * GROUP))
            pool.wait_ge(xot_mm.h, xot_mm.upto(i, 0))
            pool.wait_ge(gate_done.h, gate_done.upto(i, 0))
            settle()
            for m in range(GROUP):
                for s in range(2):
                    last = nc.gpsimd.tensor_copy(x_rows[:, m, :, :, s, :], x_in[:, m, s])
            last.then_inc(rows_done.h, 1)

        pool.wait_ge(taps_saved.h, PRIME + 16)
        with pool.Fori(0, ITERS) as i:
            regroup_x(i)
            diagonal_x(i, 0)
            heads_of_k(i, 0)
            heads_of_v(i, 0)
            for c in range(1, CHUNKS):
                diagonal_x(i, c)
                heads_of_k(i, c)
                heads_of_v(i, c)
        end_of_phase1(pool)

        def split_x(i, c):
            k = (c % C2) // 2
            pool.wait_ge(acc_done.h, acc_done.upto(i, max(0, (c - 1) * E + 3)))
            if c % 2 == 0:
                pool.wait_ge(half_in[k].h, half_in[k].upto(i + (c == C2), 3))
            pool.wait_ge(a_mm.h, a_mm.upto(i, 2 * E * (c - 1)))
            cols = slice((c % 2) * CW, (c % 2) * CW + CW)
            settle()
            for j in range(2):
                p = slice(64 * j, 64 * j + 64)
                last = nc.gpsimd.tensor_copy(xs[p, c % 2, j, :], xnl[p, k, cols])
            last.then_inc(hi_done.h, 1)
            pool.wait_ge(hi_done.h, hi_done.upto(i, c + 1))
            for j in range(2):
                p, other = slice(64 * j, 64 * j + 64), slice(64 - 64 * j, 128 - 64 * j)
                last = nc.gpsimd.tensor_tensor(xs[other, c % 2, j, :], xnl[p, k, cols],
                                               xs[p, c % 2, j, :].bitcast(F32), ALU.subtract)
            last.then_inc(xs_done.h, 1)

        def m_iteration(i, following):
            for c in range(C2):
                for e in range(E):
                    n = c * E + e
                    pool.wait_ge(yw_done.h, yw_done.upto(i, n + 1))
                    if e == 0:
                        pool.wait_ge(ot_mm.h, ot_mm.upto(i, c - 1))
                        other = t2l[:, c // 2, (c % 2) * CW:(c % 2) * CW + CW]
                    else:
                        pool.wait_ge(acc_done.h, acc_done.upto(i, n))
                        if e == 3 and (c + 1 < C2 or following):
                            pool.wait_ge(xs_done.h, xs_done.upto(i, c + 2))
                        other = acc[:, c % 2, :]
                    nc.gpsimd.tensor_tensor(acc[:, c % 2, :], yw[:, n % 2, :], other, ALU.add
                                            ).then_inc(acc_done.h, 1)
                    if e == 2 and (c + 1 < C2 or following):
                        split_x(i, c + 1)

        split_x(0, 0)
        with pool.Fori(0, IMAGES - 1) as i:
            m_iteration(i, True)
        m_iteration(IMAGES - 1, False)

    @block.scalar
    def _(act):
        act.wait_ge(prepared.h, PRIME + PREP_STEPS)

        def evacuate_xT(i, n):
            m, u, wh = n // 4, (n // 2) % 2, n % 2
            act.wait_ge(xt_mm.h, xt_mm.upto(i, n + 1))
            if n == 0:
                act.wait_ge(t2_done.h, t2_done.upto(i, 0))
                act.wait_ge(d_mm[1].h, d_mm[1].upto(i, 0))
            src = bank(n % 2)[:, 0:CW].rearrange("p (w r t) -> p r w t", r=2, t=TOK)
            for r in range(2):
                last = nc.scalar.activation(xT[:, m, 2 * r + u, 4 * wh:4 * wh + 4, :], src[:, r], ACT.Copy)
            last.then_inc(xt_done.h, 1)

        def evacuate_qk(i, c):
            act.wait_ge(q_mm.h, q_mm.upto(i, c + 1))
            act.wait_ge(s_mm.h, s_mm.upto(i, 4 * (c - 1)))
            src = bank(0)[:, 0:CW].rearrange("p (w t) -> p w t", t=TOK)
            for s in range(2):
                p = slice(64 * s, 64 * s + 64)
                last = nc.scalar.activation(q_diag[p, c % 2, :, s, 0:TOK], src[p], ACT.Identity,
                                            bias=bq[p], scale=HD ** -0.5)
            last.then_inc(q_done.h, 1)
            act.wait_ge(k_mm.h, k_mm.upto(i, c + 1))
            act.wait_ge(kh_done.h, kh_done.upto(i, c))
            nc.scalar.activation(k_sb[:, 0].rearrange("p w t -> p (w t)"), bank(1)[:, 0:CW], ACT.Identity,
                                 bias=bk).then_inc(k_done.h, 1)

        def exponential(i, u):
            act.wait_ge(sub_done.h, sub_done.upto(i, u + 1))
            v = probs[:, u % 3].rearrange("p j h k -> p (j h) k")[:, :, 0:TOK]
            nc.scalar.activation(v, v, ACT.Exp).then_inc(exp_done.h, 1)

        def evacuate_pt(i, u):
            act.wait_ge(pt_mm.h, pt_mm.upto(i, u + 1))
            act.wait_ge(o_mm.h, o_mm.upto(i, u - 1))
            nc.scalar.activation(probsT[:, u % 2, :], bank(4 + u % 2), ACT.Copy).then_inc(pt_done.h, 1)

        def square(i, n, c):
            act.wait_ge(d_mm[n].h, d_mm[n].upto(i, c + 1))
            if c >= 2:
                act.wait_ge(var_mm[n].h, var_mm[n].upto(i, c - 1))
            else:
                act.wait_ge(var_mm[(n - 1) % 3].h, var_mm[(n - 1) % 3].upto(i, CHUNKS if n else 0))
            nc.scalar.activation(sq[:, c % 2, :], bank(c % 2)[:, 0:CW], ACT.Square).then_inc(sq_done[n].h, 1)

        def deviation(i, n, c):
            act.wait_ge(var_mm[n].h, var_mm[n].upto(i, c + 1))
            if n == 2:
                act.wait_ge(rs_done[2].h, rs_done[2].upto(i, c))
                act.wait_ge(rs_done[1].h, rs_done[1].upto(i, CHUNKS))
                nc.scalar.activation(sd[:, 0, :], bank(2 + c % 2)[:, 0:CW], ACT.Sqrt, bias=eps_c
                                     ).then_inc(sd_done[2].h, 1)
                act.wait_ge(rs2_done.h, rs2_done.upto(i, c))
                nc.scalar.activation(sd[:, 1, :], bank(2 + c % 2)[:, 0:CW], ACT.Sqrt, bias=eps2_c,
                                     scale=1.0 + LN_EPS).then_inc(sd2_done.h, 1)
                return
            if c >= 2:
                act.wait_ge(rs_done[n].h, rs_done[n].upto(i, c - 1))
            elif n == 1:
                act.wait_ge(rs_done[0].h, rs_done[0].upto(i, CHUNKS))
            else:
                act.wait_ge(rs2_done.h, rs2_done.upto(i, 0))
            nc.scalar.activation(sd[:, c % 2, :], bank(2 + c % 2)[:, 0:CW], ACT.Sqrt, bias=eps_c
                                 ).then_inc(sd_done[n].h, 1)

        def layernorm(i, n):
            square(i, n, 0)
            for c in range(CHUNKS):
                if c + 1 < CHUNKS:
                    square(i, n, c + 1)
                deviation(i, n, c)

        with act.Fori(0, ITERS) as i:
            for n in range(8):
                evacuate_xT(i, n)
            evacuate_qk(i, 0)
            for u in range(UNITS + 2):
                if u % 4 == 0 and u // 4 + 1 < CHUNKS:
                    evacuate_qk(i, u // 4 + 1)
                if u < UNITS:
                    exponential(i, u)
                if u >= 2:
                    evacuate_pt(i, u - 2)
            for c in range(CHUNKS):
                act.wait_ge(xot_mm.h, xot_mm.upto(i, c + 1))
                act.wait_ge(h_mm.h, h_mm.upto(i, 0))
                nc.scalar.activation(xoT[:, c * CW:c * CW + CW].rearrange("p (a t) -> p a t", t=TOK),
                                     bank(c % 2).rearrange("p (a t) -> p a t", t=PAD)[:, :, 0:TOK],
                                     ACT.Copy).then_inc(xot_done.h, 1)
            for c in range(CHUNKS):
                act.wait_ge(f_mm.h, f_mm.upto(i, c + 1))
                act.wait_ge(u_done.h, u_done.upto(i, c - 1))
                nc.scalar.activation(rs[:, c % 2, :], bank(4 + c % 2)[:, 0:CW], ACT.Tanh, scale=0.5
                                     ).then_inc(th_done.h, 1)
            layernorm(i, 0)
            layernorm(i, 1)
            for c in range(CHUNKS):
                act.wait_ge(h_mm.h, h_mm.upto(i, c + 1))
                act.wait_ge(t2_done.h, t2_done.upto(i, c - 3))
                nc.scalar.activation(hid[:, (c % 4) * CW:(c % 4) * CW + CW], bank(4 + c % 2)[:, 0:CW], ACT.Tanh,
                                     bias=brnn).then_inc(h_done.h, 1)
            layernorm(i, 2)
            act.wait_ge(dl_done.h, dl_done.upto(i, 1))
            nc.scalar.activation(r_small[0:ROWS2, 5, :], r_small[0:ROWS2, 4, :], ACT.Tanh, scale=0.5
                                 ).then_inc(gth_done.h, 1)
            for c in range(CHUNKS):
                act.wait_ge(gt_mm.h, gt_mm.upto(i, c + 1))
                act.wait_ge(gate_stored.h, gate_stored.upto(i, 0))
                nc.scalar.activation(gateT[:, c * CW:c * CW + CW], bank(6 + c % 2)[0:GROWS, :].bitcast(BF16)[:, 0:CW],
                                     ACT.Copy).then_inc(gt_done.h, 1)
        end_of_phase1(act)

        act.wait_ge(m_step.h, PRIME + M_STEPS)

        def m_iteration(i):
            for c in range(C2):
                for e in range(E):
                    for m in range(2):
                        n = (c * E + e) * 2 + m
                        act.wait_ge(a_mm.h, a_mm.upto(i, n + 1))
                        act.wait_ge(y_mm.h, y_mm.upto(i, c * E + e - 1))
                        nc.scalar.activation(g[:, n % 4], PS[:, 2 * m:2 * m + 2, 0:CW], ACT.Gelu,
                                             bias=b1[:, e, m:m + 1]).then_inc(g_done.h, 1)

        with act.Fori(0, IMAGES) as i:
            m_iteration(i)

    @block.vector
    def _(dve):
        steps = [0]

        def step(ins):
            steps[0] += 1
            ins.then_inc(prepared.h, 1)
            dve.wait_ge(prepared.h, PRIME + steps[0])

        dve.wait_ge(taps_in.h, PRIME + 48)
        grid = taps.rearrange("p (a b) -> p a b", b=OFF)
        nc.vector.memset(taps, 0.0).then_inc(taps_step.h, 1)
        for n, (raw, size) in enumerate(((raw7, 7), (raw5, 5), (raw3, 3))):
            lo = (OFF - size) // 2
            dve.wait_ge(taps_step.h, PRIME + n + 1)
            part = grid[:, lo:lo + size, lo:lo + size]
            nc.vector.scalar_tensor_tensor(part, raw.rearrange("p (a b) -> p a b", b=size), 0.25 * 0.2, part,
                                           ALU.mult, ALU.add).then_inc(taps_step.h, 1)
        dve.wait_ge(taps_step.h, PRIME + 4)
        mid = grid[:, WS - 1:WS, WS - 1:WS]
        nc.vector.tensor_scalar(mid, mid, 1.0, None, ALU.add).then_inc(taps_step.h, 1)
        dve.wait_ge(taps_step.h, PRIME + 5)
        for x in range(WS):
            last = nc.vector.tensor_copy(spread[:, x], grid[:, :, WS - 1 - x:2 * WS - 1 - x])
        last.then_inc(taps_step.h, 1)
        dve.wait_ge(wloaded.h, PRIME + 16 * WLOADS)
        for s in range(2):
            p = slice(64 * s, 64 * s + 64)
            step(nc.vector.scalar_tensor_tensor(wv[p], wv[p], 0.1, ident[p, p], ALU.mult, ALU.add))
        step(nc.vector.tensor_scalar(bv[:], bv[:], 0.1, None, ALU.mult))
        step(nc.vector.tensor_scalar(bq, bq, HD ** -0.5, None, ALU.mult))
        step(nc.vector.tensor_tensor(brnn, brnn, brnn2, ALU.add))
        step(nc.vector.memset(eps_c, LN_EPS))
        step(nc.vector.memset(eps2_c, LN_EPS * LN_EPS))
        step(nc.vector.tensor_copy(ident_b[:], ident))
        dve.wait_ge(outc_mm.h, PRIME + 1)
        step(nc.vector.tensor_scalar(w_outc[:], bank(7)[:, 0:128], 0.25, None, ALU.mult))
        assert steps[0] == PREP_STEPS

        def evacuate_v(i, c):
            dve.wait_ge(v_mm.h, v_mm.upto(i, c + 1))
            dve.wait_ge(conv_mm.h, conv_mm.upto(i, 0))
            dve.wait_ge(vh_done.h, vh_done.upto(i, 0))
            bias = bv[:].unsqueeze(1).broadcast_to([128, 8, CH])
            nc.vector.tensor_tensor(v_all[:, :, 8 * c:8 * c + 8].rearrange("p k n -> p n k"),
                                    bank(0).rearrange("p (n k) -> p n k", k=CH), bias, ALU.add
                                    ).then_inc(v_done.h, 1)
            dve.wait_ge(vs_mm.h, vs_mm.upto(i, c + 1))
            dve.wait_ge(vh_done.h, vh_done.upto(i, c))
            nc.vector.tensor_tensor(v_swap[:, 0], bank(1).rearrange("p (n k) -> p n k", k=CH), bias, ALU.add
                                    ).then_inc(vs_done.h, 1)

        def less_max(i, u):
            sc = bank(2 + u % 2)[:, 0:CW].rearrange("p (g k) -> p g k", k=TOK)
            dve.wait_ge(s_mm.h, s_mm.upto(i, u + 1))
            nc.vector.tensor_reduce(mx[:, u % 2, :], sc, AX.X, ALU.max).then_inc(max_done.h, 1)
            dve.wait_ge(max_done.h, max_done.upto(i, u + 1))
            dve.wait_ge(pt_mm.h, pt_mm.upto(i, u - 2))
            nc.vector.tensor_tensor(probs[:, u % 3].rearrange("p j h k -> p (j h) k")[:, :, 0:TOK], sc,
                                    mx[:, u % 2, :].unsqueeze(2).broadcast_to([128, 8, TOK]), ALU.subtract
                                    ).then_inc(sub_done.h, 1)

        def normalise(i, u):
            dve.wait_ge(o_mm.h, o_mm.upto(i, u + 1))
            o = bank(6 + u % 2)[:, 0:4 * 68].rearrange("p (g s i d) -> p g s i d", g=4, s=2, i=2)
            if u == 0:
                dve.wait_ge(xt_mm.h, xt_mm.upto(i, 8))
            for s in range(2):
                p = slice(64 * s, 64 * s + 64)
                last = nc.vector.reciprocal(rden[p, u % 2], o[p, :, s, :, HD])
            last.then_inc(rden_done.h, 1)
            dve.wait_ge(rden_done.h, rden_done.upto(i, u + 1))
            for s in range(2):
                p = slice(64 * s, 64 * s + 64)
                last = nc.vector.tensor_tensor(
                    xo[p, 2 * u:2 * u + 2, :].rearrange("p n (h i d) -> p (n h) i d", h=2, i=2), o[p, :, s, :, 0:HD],
                    rden[p, u % 2].unsqueeze(3).broadcast_to([64, 4, 2, HD]), ALU.mult)
            last.then_inc(o_done.h, 1)

        def evacuate_logits(i, c):
            dve.wait_ge(lg_mm.h, lg_mm.upto(i, c + 1))
            dve.wait_ge(gate_done.h, gate_done.upto(i, 0))
            nc.vector.tensor_tensor(
                lg[:, 8 * c:8 * c + 8, :].rearrange("p (q j) e -> p q (j e)", j=2),
                bank(6 + c % 2)[0:ROWS2, 0:64].rearrange("p (q n) -> p q n", q=4),
                b_r[:].unsqueeze(1).broadcast_to([ROWS2, 4, 2 * E]), ALU.add).then_inc(lg_done.h, 1)

        def layernorm(i, n):
            for c in range(CHUNKS):
                dve.wait_ge(sd_done[n].h, sd_done[n].upto(i, c + 1))
                if n == 2:
                    before = mul_done[2].upto(i, c) if c else mul_done[1].upto(i, CHUNKS)
                    dve.wait_ge(mul_done[2 if c else 1].h, before)
                elif c >= 2:
                    dve.wait_ge(mul_done[n].h, mul_done[n].upto(i, c - 1))
                elif n == 1:
                    dve.wait_ge(mul_done[0].h, mul_done[0].upto(i, CHUNKS))
                else:
                    dve.wait_ge(u_done.h, u_done.upto(i, CHUNKS))
                src = sd[:, 0 if n == 2 else c % 2, :]
                nc.vector.reciprocal(rs[:, 0 if n == 2 else c % 2, :], src).then_inc(rs_done[n].h, 1)
                dve.wait_ge(rs_done[n].h, rs_done[n].upto(i, c + 1))
                d = bank(c % 2)[:, 0:CW]
                if n == 0:
                    dve.wait_ge(t_done.h, t_done.upto(i, c - 1))
                    nc.vector.tensor_tensor(tmp[:, c % 2, :], d, rs[:, c % 2, :], ALU.mult
                                            ).then_inc(mul_done[0].h, 1)
                    dve.wait_ge(mul_done[0].h, mul_done[0].upto(i, c + 1))
                    nc.vector.tensor_scalar(tT[:, c * CW:c * CW + CW], tmp[:, c % 2, :], lng, lnb,
                                            ALU.mult, ALU.add).then_inc(t_done.h, 1)
                elif n == 1:
                    nc.vector.tensor_tensor(z1[:, c * CW:c * CW + CW], d, rs[:, c % 2, :], ALU.mult
                                            ).then_inc(mul_done[1].h, 1)
                else:
                    dve.wait_ge(lg_mm.h, lg_mm.upto(i, c - 1))
                    nc.vector.tensor_tensor(zz[:, c % 2, :], d, rs[:, 0, :], ALU.mult).then_inc(mul_done[2].h, 1)
                    dve.wait_ge(sd2_done.h, sd2_done.upto(i, c + 1))
                    dve.wait_ge(xn_done.h, xn_done.upto(i, c))
                    nc.vector.reciprocal(rs[:, 1, :], sd[:, 1, :]).then_inc(rs2_done.h, 1)
                    dve.wait_ge(rs2_done.h, rs2_done.upto(i, c + 1))
                    k = c // 2
                    dve.wait_ge(xn_stored[c % 2].h, xn_stored[c % 2].upto(i, k))
                    nc.vector.tensor_tensor(xn[:, c % 2, :], d, rs[:, 1, :], ALU.mult).then_inc(xn_done.h, 1)
                    if c >= 1:
                        evacuate_logits(i, c - 1)

        def route(i):
            n = [0]
            wide = [ROWS2, 2 * UNITS, E]

            def rstep(ins):
                n[0] += 1
                ins.then_inc(r_step.h, 1)
                dve.wait_ge(r_step.h, r_step.upto(i, n[0]))

            def over(x):
                return r_small[0:ROWS2, x, :].unsqueeze(2).broadcast_to(wide)

            rk = rank.unsqueeze(1).broadcast_to(wide)
            dve.wait_ge(lg_done.h, lg_done.upto(i, CHUNKS))
            dve.wait_ge(gt_mm.h, gt_mm.upto(i, 0))
            for k, oh in ((0, oh1), (1, oh2)):
                best, first = r_small[0:ROWS2, 2 * k, :], r_small[0:ROWS2, 2 * k + 1, :]
                rstep(nc.vector.tensor_reduce(best, lg[:], AX.X, ALU.max))
                rstep(nc.vector.tensor_tensor(oh[:], lg[:], over(2 * k), ALU.is_equal))
                rstep(nc.vector.tensor_tensor(oh[:], oh[:], rk, ALU.mult))
                rstep(nc.vector.tensor_reduce(first, oh[:], AX.X, ALU.max))
                rstep(nc.vector.tensor_tensor(oh[:], oh[:], over(2 * k + 1), ALU.is_equal))
                if k == 0:
                    rstep(nc.vector.scalar_tensor_tensor(lg[:], oh[:], -BIG, lg[:], ALU.mult, ALU.add))
            nc.vector.tensor_tensor(r_small[0:ROWS2, 4, :], r_small[0:ROWS2, 0, :], r_small[0:ROWS2, 2, :],
                                    ALU.subtract).then_inc(dl_done.h, 1)
            dve.wait_ge(gth_done.h, gth_done.upto(i, 1))
            rstep(nc.vector.tensor_scalar(r_small[0:ROWS2, 6, :], r_small[0:ROWS2, 5, :], 0.5, 0.5, ALU.mult, ALU.add))
            rstep(nc.vector.tensor_scalar(r_small[0:ROWS2, 7, :], r_small[0:ROWS2, 5, :], -0.5, 0.5, ALU.mult, ALU.add))
            rstep(nc.vector.tensor_tensor(oh1[:], oh1[:], over(6), ALU.mult))
            rstep(nc.vector.tensor_tensor(oh2[:], oh2[:], over(7), ALU.mult))
            rstep(nc.vector.tensor_tensor(gate[:], oh1[:], oh2[:], ALU.add))
            part = [gate3[:, :, k, :] for k in range(PARTS)]
            whole = gate[:].rearrange("p (u j) e -> p u (j e)", j=2)
            rest = gate_rest[:].rearrange("p (u j) e -> p u (j e)", j=2)
            rstep(nc.vector.tensor_copy(part[0], whole))
            rstep(nc.vector.tensor_tensor(rest, whole, part[0], ALU.subtract))
            rstep(nc.vector.tensor_copy(part[1], rest))
            assert n[0] == ROUTER_STEPS
            nc.vector.tensor_tensor(part[2], rest, part[1], ALU.subtract).then_inc(gate_done.h, 1)

        with dve.Fori(0, ITERS) as i:
            evacuate_v(i, 0)
            for u in range(UNITS + 3):
                if u < UNITS:
                    less_max(i, u)
                if u % 4 == 2 and u // 4 + 1 < CHUNKS:
                    evacuate_v(i, u // 4 + 1)
                if u >= 3:
                    normalise(i, u - 3)
            dve.wait_ge(o_done.h, o_done.upto(i, UNITS))
            for n in range(8):
                dve.wait_ge(conv_mm.h, conv_mm.upto(i, n + 1))
                part = xo[:, :, 8 * n:8 * n + 8].rearrange("p n k -> p k n")
                nc.vector.tensor_tensor(part, bank(n % 2).rearrange("p (k n) -> p k n", n=PAIRS), part, ALU.add
                                        ).then_inc(conv_done.h, 1)
            for c in range(CHUNKS):
                dve.wait_ge(th_done.h, th_done.upto(i, c + 1))
                dve.wait_ge(t2_stored.h, t2_stored.upto(i, 0))
                dve.wait_ge(d_mm[2].h, d_mm[2].upto(i, 0))
                nc.vector.scalar_tensor_tensor(ffn_u[:, c * CW:c * CW + CW], rs[:, c % 2, :], 1.0,
                                               bank(4 + c % 2)[:, 0:CW], ALU.add, ALU.mult).then_inc(u_done.h, 1)
            layernorm(i, 0)
            layernorm(i, 1)
            for c in range(CHUNKS):
                dve.wait_ge(h_done.h, h_done.upto(i, c + 1))
                dve.wait_ge(d_mm[0].h, d_mm[0].upto(i, CHUNKS))
                dve.wait_ge(t_done.h, t_done.upto(i, CHUNKS))
                nc.vector.tensor_tensor(t2[:, c * CW:c * CW + CW], tT[:, c * CW:c * CW + CW],
                                        hid[:, (c % 4) * CW:(c % 4) * CW + CW], ALU.add).then_inc(t2_done.h, 1)
            layernorm(i, 2)
            evacuate_logits(i, CHUNKS - 1)
            route(i)
        end_of_phase1(dve)

        m_steps = [0]

        def mstep(ins):
            m_steps[0] += 1
            ins.then_inc(m_step.h, 1)
            dve.wait_ge(m_step.h, PRIME + m_steps[0])

        dve.wait_ge(m_bias_mm.h, PRIME + 1)
        mstep(nc.vector.tensor_tensor(b1[:].rearrange("p e m -> p (e m)"), bank(7)[:, 0:2 * E],
                                      b1[:].rearrange("p e m -> p (e m)"), ALU.add))
        mstep(nc.vector.tensor_tensor(w1[:], w1[:], ge[:].unsqueeze(2).broadcast_to([128, E, HID]), ALU.mult))
        mstep(nc.vector.tensor_copy(w1hi[:], w1[:]))
        mstep(nc.vector.tensor_tensor(w1lo[:], w1[:], w1hi[:].bitcast(F32), ALU.subtract))
        mstep(nc.vector.tensor_copy(sel_b[:], sel[:]))
        assert m_steps[0] == M_STEPS

        def spread_gate(i, n):
            dve.wait_ge(wr_mm.h, wr_mm.upto(i, n + 1))
            nc.vector.tensor_copy(wrep[:, n % 2, :], bank(7)[:, 0:CW]).then_inc(wr_done.h, 1)

        def weigh(i, n):
            e = n % E
            dve.wait_ge(y_mm.h, y_mm.upto(i, n + 1))
            dve.wait_ge(wr_done.h, wr_done.upto(i, n + 1))
            dve.wait_ge(acc_done.h, acc_done.upto(i, n - 1))
            nc.vector.scalar_tensor_tensor(yw[:, n % 2, :], bank(4 + n % 2)[:, 0:CW], b2[:, e:e + 1],
                                           wrep[:, n % 2, :], ALU.add, ALU.mult).then_inc(yw_done.h, 1)

        def m_iteration(i):
            for n in range(C2 * E):
                spread_gate(i, n)
                weigh(i, n)
                if n % E == E - 1:
                    c = n // E
                    dve.wait_ge(ot_mm.h, ot_mm.upto(i, c + 1))
                    dve.wait_ge(out_stored[c % 2].h, out_stored[c % 2].upto(i, 2 * (c // 2)))
                    nc.vector.tensor_copy(ot[:, c % 2, :], bank(6)[0:ROWS2, :]).then_inc(ot_done.h, 1)

        with dve.Fori(0, IMAGES) as i:
            m_iteration(i)

    @block.tensor
    def _(pe):
        mm = nc.tensor.matmul
        pe.wait_ge(wloaded.h, PRIME + 16 * WLOADS)
        pe.wait_ge(zeroed.h, PRIME + 3)
        mm(bank(7)[:, 0:128], w_out[:], centre, start=True, stop=True).then_inc(outc_mm.h, 1)
        pe.wait_ge(prepared.h, PRIME + PREP_STEPS)

        def project_qk(i, c):
            m, rq = c // 4, c % 4
            x = xT[:, m, rq].rearrange("p w t -> p (w t)")
            if c == 0:
                pe.wait_ge(xt_done.h, xt_done.upto(i, 8))
            else:
                pe.wait_ge(v_done.h, v_done.upto(i, c))
            mm(bank(0)[:, 0:CW], wq[:], x, start=True, stop=True).then_inc(q_mm.h, 1)
            if c > 0:
                pe.wait_ge(vs_done.h, vs_done.upto(i, c))
            mm(bank(1)[:, 0:CW], wk[:], x, start=True, stop=True).then_inc(k_mm.h, 1)

        def project_v(i, c):
            pe.wait_ge(xd_done.h, xd_done.upto(i, c + 1))
            pe.wait_ge(q_done.h, q_done.upto(i, c + 1))
            for w in range(8):
                last = mm(bank(0)[:, CH * w:CH * w + CH], x_diag[:, c % 2, w, 0:2, :].rearrange("p a b -> p (a b)"),
                          wv[:], start=True, stop=True)
            last.then_inc(v_mm.h, 1)
            pe.wait_ge(k_done.h, k_done.upto(i, c + 1))
            for w in range(8):
                last = mm(bank(1)[:, CH * w:CH * w + CH], x_diag[:, c % 2, w, 1:3, :].rearrange("p a b -> p (a b)"),
                          wv[:], start=True, stop=True)
            last.then_inc(vs_mm.h, 1)

        def scores(i, u):
            c, q = u // 4, u % 4
            if q == 0:
                pe.wait_ge(q_done.h, q_done.upto(i, c + 1))
                pe.wait_ge(kh_done.h, kh_done.upto(i, c + 1))
            if u >= 2:
                pe.wait_ge(sub_done.h, sub_done.upto(i, u - 1))
            for j in range(2):
                w = 2 * q + j
                last = mm(bank(2 + u % 2)[:, 196 * j:196 * j + 196],
                          q_diag[:, c % 2, w].rearrange("p a b -> p (a b)"),
                          k_heads[:, c % 2, w].rearrange("p a b -> p (a b)"), start=True, stop=True)
            last.then_inc(s_mm.h, 1)

        def turn_probs(i, u):
            pe.wait_ge(exp_done.h, exp_done.upto(i, u + 1))
            if u >= 2:
                pe.wait_ge(pt_done.h, pt_done.upto(i, u - 1))
            for j in range(2):
                for hp in range(2):
                    k = 2 * j + hp
                    last = nc.tensor.transpose(
                        bank(4 + u % 2)[:, 128 * k:128 * k + 128],
                        probs[:, u % 3, j, 2 * hp:2 * hp + 2, :].rearrange("p a b -> p (a b)"), ident)
            last.then_inc(pt_mm.h, 1)

        def attend(i, u):
            c, q = u // 4, u % 4
            if q == 0:
                pe.wait_ge(vh_done.h, vh_done.upto(i, c + 1))
            pe.wait_ge(pt_done.h, pt_done.upto(i, u + 1))
            if u >= 2:
                pe.wait_ge(o_done.h, o_done.upto(i, u - 1))
            for j in range(2):
                for hp in range(2):
                    k = 2 * j + hp
                    last = mm(bank(6 + u % 2)[:, 68 * k:68 * k + 68], probsT[:, u % 2, 128 * k:128 * k + 128],
                              v_heads[:, c % 2, 2 * q + j, hp].rearrange("p s i d -> p (s i d)"),
                              start=True, stop=True)
            last.then_inc(o_mm.h, 1)

        def centred(i, n, c):
            cols = slice(c * CW, c * CW + CW)
            out = bank(c % 2)[:, 0:CW]
            if c >= 2:
                free = xn_done if n == 2 else mul_done[n]
                pe.wait_ge(free.h, free.upto(i, c - 1))
            if n == 0:
                pe.wait_ge(u_done.h, u_done.upto(i, c + 1))
                if c < 2:
                    pe.wait_ge(xot_done.h, xot_done.upto(i, CHUNKS))
                mm(out, w_outc[:], ffn_u[:, cols], start=True, stop=False)
                mm(out, centre, xoT[:, cols], start=False, stop=True).then_inc(d_mm[0].h, 1)
            elif n == 1:
                pe.wait_ge(t_done.h, t_done.upto(i, c + 1))
                if c < 2:
                    pe.wait_ge(mul_done[0].h, mul_done[0].upto(i, CHUNKS))
                mm(out, centre, tT[:, cols], start=True, stop=True).then_inc(d_mm[1].h, 1)
            else:
                pe.wait_ge(t2_done.h, t2_done.upto(i, c + 1))
                if c < 2:
                    pe.wait_ge(mul_done[1].h, mul_done[1].upto(i, CHUNKS))
                mm(out, centre, t2[:, cols], start=True, stop=True).then_inc(d_mm[2].h, 1)

        def variance(i, n, c):
            pe.wait_ge(sq_done[n].h, sq_done[n].upto(i, c + 1))
            if c >= 2:
                free = sd2_done if n == 2 else sd_done[n]
                pe.wait_ge(free.h, free.upto(i, c - 1))
            elif n == 0:
                pe.wait_ge(sub_done.h, sub_done.upto(i, UNITS))
            else:
                pe.wait_ge(sd_done[n - 1].h, sd_done[n - 1].upto(i, CHUNKS))
            mm(bank(2 + c % 2)[:, 0:CW], meanm, sq[:, c % 2, :], start=True, stop=True).then_inc(var_mm[n].h, 1)

        def logits(i, c):
            pe.wait_ge(mul_done[2].h, mul_done[2].upto(i, c + 1))
            if c >= 2:
                pe.wait_ge(lg_done.h, lg_done.upto(i, c - 1))
            else:
                pe.wait_ge(o_done.h, o_done.upto(i, UNITS))
            for q in range(4):
                last = mm(bank(6 + c % 2)[0:ROWS2, 16 * q:16 * q + 16], zz[:, c % 2, ROWS2 * q:ROWS2 * q + ROWS2],
                          w_r[:], start=True, stop=True)
            last.then_inc(lg_mm.h, 1)

        def layernorm(i, n):
            centred(i, n, 0)
            for c in range(CHUNKS):
                if c + 1 < CHUNKS:
                    centred(i, n, c + 1)
                variance(i, n, c)
                if n == 2 and c >= 1:
                    logits(i, c - 1)
            if n == 2:
                logits(i, CHUNKS - 1)

        with pe.Fori(0, ITERS) as i:
            pe.wait_ge(xn_done.h, xn_done.upto(i, 0))
            pe.wait_ge(sd2_done.h, sd2_done.upto(i, 0))
            pe.wait_ge(h_done.h, h_done.upto(i, 0))
            pe.wait_ge(lg_done.h, lg_done.upto(i, 0))
            pe.wait_ge(gt_done.h, gt_done.upto(i, 0))
            pe.wait_ge(rows_done.h, rows_done.upto(i, 1))
            for n in range(8):
                m, u, wh = n // 4, (n // 2) % 2, n % 2
                if n >= 2:
                    pe.wait_ge(xt_done.h, xt_done.upto(i, n - 1))
                for w in range(4):
                    last = nc.tensor.transpose(bank(n % 2)[:, ROWS2 * w:ROWS2 * w + ROWS2],
                                               x_rows[:, m, u, 4 * wh + w].rearrange("p s k -> p (s k)"), ident[0:ROWS2, 0:ROWS2])
                last.then_inc(xt_mm.h, 1)
            project_qk(i, 0)
            project_v(i, 0)
            for u in range(UNITS + 3):
                if u < UNITS:
                    scores(i, u)
                if u % 4 == 0 and u // 4 + 1 < CHUNKS:
                    project_qk(i, u // 4 + 1)
                if u % 4 == 2 and u // 4 + 1 < CHUNKS:
                    project_v(i, u // 4 + 1)
                if 2 <= u < UNITS + 2:
                    turn_probs(i, u - 2)
                if u >= 3:
                    attend(i, u - 3)
            pe.wait_ge(conv_w.h, PRIME + 16 * 2 * WS)
            pe.wait_ge(v_done.h, v_done.upto(i, CHUNKS))
            pe.wait_ge(vs_done.h, vs_done.upto(i, CHUNKS))
            for n in range(8):
                if n >= 2:
                    pe.wait_ge(conv_done.h, conv_done.upto(i, n - 1))
                for k in range(8):
                    last = mm(bank(n % 2)[:, PAIRS * k:PAIRS * k + PAIRS],
                              conv_m[:, 8 * n + k].rearrange("p a b -> p (a b)"), v_all[:, 8 * n + k, :],
                              start=True, stop=True)
                last.then_inc(conv_mm.h, 1)
            pe.wait_ge(conv_done.h, conv_done.upto(i, 8))
            for c in range(CHUNKS):
                if c >= 2:
                    pe.wait_ge(xot_done.h, xot_done.upto(i, c - 1))
                for q in range(4):
                    n = 8 * c + 2 * q
                    last = nc.tensor.transpose(bank(c % 2)[:, 128 * q:128 * q + 128],
                                               xo[:, n:n + 2, :].rearrange("p a b -> p (a b)"), ident)
                last.then_inc(xot_mm.h, 1)
            for c in range(CHUNKS):
                pe.wait_ge(xot_done.h, xot_done.upto(i, c + 1))
                if c >= 2:
                    pe.wait_ge(u_done.h, u_done.upto(i, c - 1))
                else:
                    pe.wait_ge(pt_done.h, pt_done.upto(i, UNITS))
                mm(bank(4 + c % 2)[:, 0:CW], w_in[:], xoT[:, c * CW:c * CW + CW], start=True, stop=True
                   ).then_inc(f_mm.h, 1)
            layernorm(i, 0)
            layernorm(i, 1)
            for c in range(CHUNKS):
                pe.wait_ge(mul_done[1].h, mul_done[1].upto(i, c + 1))
                pe.wait_ge(h_done.h, h_done.upto(i, c - 1 if c >= 2 else c - 3))
                if c < 2:
                    pe.wait_ge(u_done.h, u_done.upto(i, CHUNKS))
                out = bank(4 + c % 2)[:, 0:CW]
                mm(out, w_ih[:], z1[:, c * CW:c * CW + CW], start=True, stop=False)
                mm(out, w_hh[:], hid[:, (c % 4) * CW:(c % 4) * CW + CW], start=False, stop=True).then_inc(h_mm.h, 1)
            layernorm(i, 2)
            pe.wait_ge(gate_done.h, gate_done.upto(i, 1))
            for c in range(CHUNKS):
                pe.wait_ge(lg_done.h, lg_done.upto(i, CHUNKS))
                if c >= 2:
                    pe.wait_ge(gt_done.h, gt_done.upto(i, c - 1))
                pe.sem_inc(passed.h, 1)
                for q in range(4):
                    last = nc.tensor.transpose(
                        bank(6 + c % 2)[0:GROWS, :].bitcast(BF16)[:, ROWS2 * q:ROWS2 * q + ROWS2],
                        gate3[:, 4 * c + q].rearrange("p k n -> p (k n)"), ident_b[0:ROWS2, 0:ROWS2])
                last.then_inc(gt_mm.h, 1)
        end_of_phase1(pe)

        pe.wait_ge(m_wloaded.h, PRIME + 16 * MLOADS)
        for e in range(E):
            for m in range(2):
                last = mm(bank(7)[:, 2 * e + m:2 * e + m + 1], w1[0:CH, e, 128 * m:128 * m + 128], be[0:CH, e:e + 1],
                          start=True, stop=True)
        last.then_inc(m_bias_mm.h, 1)
        pe.wait_ge(m_step.h, PRIME + M_STEPS)

        def spread_gate(i, n):
            c, e = n // E, n % E
            if n % (2 * E) == 0:
                pe.wait_ge(half_in[c // 2].h, half_in[c // 2].upto(i, 3))
            pe.wait_ge(wr_done.h, wr_done.upto(i, n))
            mm(bank(7)[:, 0:CW], sel_b[:, e, :], gatel[:, c // 2, (c % 2) * CW:(c % 2) * CW + CW],
               start=True, stop=True).then_inc(wr_mm.h, 1)

        def expand(i, n, m):
            c, e = n // E, n % E
            if m == 0 and e == 0:
                pe.wait_ge(xs_done.h, xs_done.upto(i, c + 1))
            pe.wait_ge(g_done.h, g_done.upto(i, 2 * n + m - 1))
            hs = slice(128 * m, 128 * m + 128)
            for part, w in enumerate((w1hi, w1lo)):
                for j in range(2):
                    last = mm(bank(2 * m + j)[:, 0:CW], w[:, e, hs], xs[:, c % 2, j, :],
                              start=(part == 0), stop=(part == 1))
            last.then_inc(a_mm.h, 1)

        def contract(i, n):
            e = n % E
            pe.wait_ge(yw_done.h, yw_done.upto(i, n - 1))
            for m in range(2):
                pe.wait_ge(g_done.h, g_done.upto(i, 2 * n + m + 1))
                for j in range(2):
                    last = mm(bank(4 + n % 2)[64 * j:64 * j + 64, 0:CW], w2[:, e, m, :], g[:, (2 * n + m) % 4, j, :],
                              start=(m == 0), stop=(m == 1))
            last.then_inc(y_mm.h, 1)

        def turn_out(i, c):
            pe.wait_ge(acc_done.h, acc_done.upto(i, (c + 1) * E))
            pe.wait_ge(ot_done.h, ot_done.upto(i, c))
            for q in range(4):
                last = nc.tensor.transpose(bank(6)[0:ROWS2, 128 * q:128 * q + 128],
                                           acc[:, c % 2, ROWS2 * q:ROWS2 * q + ROWS2], ident)
            last.then_inc(ot_mm.h, 1)

        def m_iteration(i):
            for n in range(C2 * E + 1):
                if n < C2 * E:
                    spread_gate(i, n)
                    expand(i, n, 0)
                    expand(i, n, 1)
                if n >= 1:
                    contract(i, n - 1)
                if n >= 1 and n % E == 0:
                    turn_out(i, n // E - 1)

        with pe.Fori(0, IMAGES) as i:
            m_iteration(i)


_OUT = (IMAGES, SIDE, SIDE, CH)


def kernel(**inputs):
    import numpy as np
    import concourse.bacc as bacc
    from concourse import mybir as mb
    from concourse.bass_utils import run_bass_kernel_spmd

    a = {k: np.asarray(v) for k, v in inputs.items()}

    def flipped(w):
        return w[:, 0, ::-1, ::-1].reshape(w.shape[0], -1)

    arrays = {
        "x": a["x"],
        "const": constants(),
        "qkv_wT": a["L0_conv_qkv_w"].T,
        "qkv_b": a["L0_conv_qkv_b"],
        "conv3f": flipped(a["L0_conv_conv3_w"]),
        "conv5f": flipped(a["L0_conv_conv5_w"]),
        "conv7f": flipped(a["L0_conv_conv7_w"]),
        "ffn_in_wT": a["L0_conv_ffn_in_w"].T,
        "ffn_out_w": a["L0_conv_ffn_out_w"],
        "ln_g": a["L0_conv_ln_g"],
        "ln_b": a["L0_conv_ln_b"],
        "W_ihT": a["L1_attn_W_ih"].T,
        "W_hhT": a["L1_attn_W_hh"].T,
        "b_ih": a["L1_attn_b_ih"],
        "b_hh": a["L1_attn_b_hh"],
        "Wr": a["L1_ffn_Wr"],
        "br": a["L1_ffn_br"],
        "ln_geT": a["L1_ffn_ln_g"].T,
        "ln_beT": a["L1_ffn_ln_b"].T,
        "W1": a["L1_ffn_W1"],
        "b1P": a["L1_ffn_b1"].reshape(EXPERTS, 2, 128).transpose(2, 0, 1),
        "W2": a["L1_ffn_W2"],
        "sel": selectors(),
        "b2T": a["L1_ffn_b2"].T,
    }
    arrays = {k: np.ascontiguousarray(v) for k, v in arrays.items()}
    nc = bacc.Bacc("TRN2", target_bir_lowering=False, num_devices=1)
    aps = {k: nc.dram_tensor(f"in_{k}", v.shape, mb.dt.from_np(v.dtype), kind="ExternalInput").ap()
           for k, v in arrays.items()}
    aps["out"] = nc.dram_tensor("out_y", _OUT, mb.dt.float32, kind="ExternalOutput").ap()
    build(nc, aps)
    r = run_bass_kernel_spmd(nc, [{f"in_{k}": v for k, v in arrays.items()}], core_ids=[0])
    return r.results[0]["out_y"]
```

```python
from contextlib import ExitStack

import concourse.bass as bass
from concourse import mybir

F32 = mybir.dt.float32
F32R = mybir.dt.float32r
BF16 = mybir.dt.bfloat16
ALU = mybir.AluOpType
ACT = mybir.ActivationFunctionType
AX = mybir.AxisListType

IMAGES, SIDE, CH = 32, 56, 64
WS = 7
TOK = WS * WS
HEADS, HD = 4, 16
EXPERTS, HID = 8, 256
LN_EPS = 1e-5
PAD = 64
GROUP = 2
CHUNKS = 4 * GROUP
CW = 8 * TOK
UNITS = 4 * CHUNKS
PAIRS = 2 * UNITS
ROWS2 = 2 * TOK
HW2 = CW * 2
HALVES = IMAGES * 2
BIG = 3.0e38
OFF = 2 * WS - 1
ITERS = IMAGES // GROUP
WLOADS = 32
MLOADS = 12
PREP_STEPS = 11
M_STEPS = 5
ROUTER_STEPS = 22
GC = 4
GRP = CHUNKS // GC
PARTS = 3
GROWS = PARTS * 2 * EXPERTS
WINDOW = 128 + 2 * GC - 2
CONSTS = 2 * 128 + WINDOW + 128 * GC + HEADS + EXPERTS
PRIME = 40


class Sem:

    def __init__(self, handle, per, step=1):
        self.h, self.per, self.step = handle, per, step

    def upto(self, i, n):
        return i * (self.per * self.step) + (PRIME + n) * self.step


def constants():
    import numpy as np

    c = np.zeros((128, CONSTS), np.float32)
    eye = np.eye(128, dtype=np.float32)
    mean = np.kron(np.eye(2), np.full((CH, CH), 1.0 / CH)).astype(np.float32)
    c[:, 0:128] = eye
    c[:, 128:256] = eye - mean
    for part in range(2):
        for j in range(2):
            c[64 * j:64 * j + 64, 256 + 2 * GC - 2 + 32 * part + j] = 1.0 / CH
            for k in range(GC):
                lo = 256 + WINDOW + 128 * k + 64 * j
                c[32 * part + 2 * k + j, lo:lo + 64] = 1
    for h in range(HEADS):
        c[:, CONSTS - 12 + h] = (np.arange(128) % CH) // HD == h
    c[:, CONSTS - 8:] = EXPERTS - np.arange(EXPERTS)
    return c


def selectors():
    import numpy as np

    c = np.zeros((PARTS, 2, EXPERTS, EXPERTS, 2, CH), np.float32)
    for j in range(2):
        for e in range(EXPERTS):
            c[:, j, e, e, j, :] = 1
    return c.reshape(GROWS, EXPERTS, 128)


def build(nc, A):
    with ExitStack() as ctx:
        program(nc, A, ctx)


def program(nc, A, ctx):
    def sb(name, shape, dt=F32, to=ctx):
        return to.enter_context(nc.sbuf_tensor(name, shape, dt))

    all_sems = []

    def sem(name, per=1, step=1):
        s = Sem(ctx.enter_context(nc.semaphore(name)), per, step)
        all_sems.append(s)
        return s

    PS = ctx.enter_context(nc.psum_tensor("banks", [128, 8, 512], F32))

    def bank(b):
        return PS[:, b, :]

    t2_dram = nc.dram_tensor("t2_scratch", (HALVES, 128, HW2), F32, kind="Internal").ap()
    xn_dram = nc.dram_tensor("xn_scratch", (HALVES, 128, HW2), F32, kind="Internal").ap()
    gate_dram = nc.dram_tensor("gate_scratch", (HALVES, GROWS, HW2), BF16, kind="Internal").ap()
    taps_dram = nc.dram_tensor("taps_scratch", (WS, CH, OFF * WS), F32, kind="Internal").ap()

    const = sb("const", [128, CONSTS])
    ident = const[:, 0:128]
    centre = const[:, 128:256]
    mean_rows = const[:, 256:256 + WINDOW]
    rows_back = const[:, 256 + WINDOW:256 + WINDOW + 128 * GC]
    headmask = const[:, CONSTS - 12:CONSTS - 8]
    rank = const[0:ROWS2, CONSTS - 8:CONSTS]

    phase1 = ExitStack()

    def sa(name, shape, dt=F32):
        return sb(name, shape, dt, phase1)

    small = sa("small", [128, 16])
    bq, bk, lng, lnb, brnn, brnn2, eps_c, eps2_c, lnb_c = (small[:, k:k + 1] for k in range(9))
    wq = sa("wq", [128, 128])
    wk = sa("wk", [128, 128])
    wv = sa("wv", [128, 128])
    bv = sa("bv", [128, CH])
    w_in = sa("w_in", [128, 128])
    w_out = sa("w_out", [128, 128])
    w_outc = sa("w_outc", [128, 128])
    w_ih = sa("w_ih", [128, 128])
    w_hh = sa("w_hh", [128, 128])
    w_r = sa("w_r", [128, 2 * EXPERTS])
    wr_rows = sa("wr_rows", [128, 2 * 112 + 2 * EXPERTS])
    b_r = sa("b_r", [ROWS2, 2 * EXPERTS])
    conv_m = sa("conv_m", [128, CH, 2, PAD])
    x_in = sa("x_in", [ROWS2, GROUP, 2, 2, 8, CH])
    xT = sa("xT", [128, GROUP, 4, 8, PAD])
    q_diag = sa("q_diag", [128, 2, 8, 2, PAD])
    k_sb = sa("k_sb", [128, 1, 8, TOK])
    k_heads = sa("k_heads", [128, 2, 8, HEADS, TOK])
    v_tok = sa("v_tok", [128, 2, 4, 2, CH])
    v_all = sa("v_all", [128, PAIRS, CH])
    v_heads = sa("v_heads", [128, 2, 4, HEADS, 2, 2, HD + 1])
    probs = sa("probs", [128, 3, HEADS, 2, PAD])
    probsT = sa("probsT", [128, 2, 512])
    rden = sa("rden", [128, 2, 4, 2])
    xo = sa("xo", [128, PAIRS, CH])
    xoT = sa("xoT", [128, CHUNKS * CW])
    ffn_u = sa("ffn_u", [128, CHUNKS * CW])
    hid = sa("hid", [128, 4 * CW])
    sq = sa("sq", [128, 2, CW])
    sd = sa("sd", [128, GRP, CW])
    rs = sa("rs", [128, GRP, CW])
    rs_parts = sa("rs_parts", [128, GRP, CW], F32R)
    from_rows = sa("from_rows", [128, GC, 128], F32R)
    xn = sa("xn", [128, 2, CW])
    lg = sa("lg", [ROWS2, 2 * UNITS, EXPERTS])
    oh1 = sa("oh1", [ROWS2, 2 * UNITS, EXPERTS])
    gate3 = sa("gate3", [ROWS2, UNITS, PARTS, 2 * EXPERTS], BF16)
    ident_b = sa("ident_b", [128, 128], BF16)
    r_small = sa("r_small", [128, 8, 2 * UNITS])
    mx = sa("mx", [128, 2, 8])
    tT = [xT[:, c // 4, c % 4, :, 0:TOK] for c in range(CHUNKS)]
    z1 = xoT
    t2 = ffn_u
    dev = xoT
    th = xn
    lg_rows = sq[:, 0, :]
    var_rows = [t[0:2 * GC].rearrange("p a b -> p (a b)")[:, 0:CW] for t in (lg, oh1)]
    gate_rest = oh1
    gate = lg
    x_rows = xo[0:ROWS2].rearrange("p (m u w s) k -> p m u w s k", m=GROUP, u=2, w=8)
    gateT = k_heads[0:GROWS].rearrange("p a w h t -> p (a w h t)")[:, 0:CHUNKS * CW // 2].bitcast(BF16)
    oh2 = xo[0:ROWS2, 0:2 * UNITS * EXPERTS // CH, :].rearrange("p a b -> p (a b)").rearrange(
        "p (g e) -> p g e", e=EXPERTS)
    taps = xo[0:CH, 0:3, :].rearrange("p a b -> p (a b)")[:, 0:OFF * OFF]
    spread = xo[0:CH, 3:13, :].rearrange("p a b -> p (a b)")[:, 0:WS * OFF * WS].rearrange(
        "p (x u v) -> p x u v", x=WS, u=OFF)
    raw3, raw5, raw7 = lg[0:CH, 0:2, :], lg[0:CH, 8:12, :], lg[0:CH, 16:23, :]
    raw3 = raw3.rearrange("p a b -> p (a b)")[:, 0:9]
    raw5 = raw5.rearrange("p a b -> p (a b)")[:, 0:25]
    raw7 = raw7.rearrange("p a b -> p (a b)")[:, 0:49]
    phase1.close()

    phase2 = ExitStack()

    def sm(name, shape, dt=F32):
        return sb(name, shape, dt, phase2)

    w1 = sm("w1", [128, EXPERTS, HID])
    w1hi = sm("w1hi", [128, EXPERTS, HID], F32R)
    w1lo = sm("w1lo", [128, EXPERTS, HID], F32R)
    w2 = sm("w2", [128, EXPERTS, 2, CH])
    b1 = sm("b1", [128, EXPERTS, 2])
    b2 = sm("b2", [128, EXPERTS])
    ge = sm("ge", [128, EXPERTS])
    be = sm("be", [128, EXPERTS])
    xnl = sm("xnl", [128, 2, HW2])
    t2l = sm("t2l", [128, 2, HW2])
    gatel = sm("gatel", [GROWS, 2, HW2], BF16)
    sel = sm("sel", [GROWS, EXPERTS, 128])
    sel_b = sm("sel_b", [GROWS, EXPERTS, 128], BF16)
    xs = sm("xs", [128, 2, 2, CW], F32R)
    g = sm("g", [128, 4, 2, CW])
    wrep = sm("wrep", [128, 4, CW])
    yw = sm("yw", [128, 4, CW])
    acc = sm("acc", [128, 2, CW])
    ot = sm("ot", [ROWS2, 2, 512])
    phase2.close()

    zeroed = sem("zeroed")
    passed = sem("passed")
    wloaded = sem("wloaded")
    taps_in = sem("taps_in")
    taps_step = sem("taps_step")
    taps_saved = sem("taps_saved")
    conv_w = sem("conv_w")
    prepared = sem("prepared")
    outc_mm = sem("outc_mm")
    phase1_end = sem("phase1_end")

    x_loaded = sem("x_loaded", 8 * GROUP, 16)
    rows_done = sem("rows_done", 1)
    xt_mm = sem("xt_mm", 8)
    xt_done = sem("xt_done", 8)
    q_mm = sem("q_mm", CHUNKS)
    k_mm = sem("k_mm", CHUNKS)
    v_mm = sem("v_mm", CHUNKS)
    q_done = sem("q_done", CHUNKS)
    k_done = sem("k_done", CHUNKS)
    kh_done = sem("kh_done", CHUNKS)
    v_done = sem("v_done", CHUNKS)
    v_swapped = [sem(f"v_swapped{k}", CHUNKS, 16) for k in range(2)]
    vh_done = sem("vh_done", CHUNKS)
    s_mm = sem("s_mm", UNITS)
    max_done = sem("max_done", UNITS)
    sub_done = sem("sub_done", UNITS)
    exp_done = sem("exp_done", UNITS)
    pt_mm = sem("pt_mm", UNITS)
    pt_done = sem("pt_done", UNITS)
    o_mm = sem("o_mm", UNITS)
    rden_done = sem("rden_done", UNITS)
    o_done = sem("o_done", UNITS)
    conv_mm = sem("conv_mm", 8)
    conv_done = sem("conv_done", 8)
    xot_mm = sem("xot_mm", CHUNKS)
    xot_done = sem("xot_done", CHUNKS)
    f_mm = sem("f_mm", CHUNKS)
    th_done = sem("th_done", CHUNKS)
    u_done = sem("u_done", CHUNKS)
    d_mm = [sem(f"d_mm{n}", CHUNKS) for n in range(3)]
    sq_done = [sem(f"sq_done{n}", CHUNKS) for n in range(3)]
    dev_done = [sem(f"dev_done{n}", CHUNKS) for n in range(3)]
    var_mm = [sem(f"var_mm{n}", CHUNKS) for n in range(3)]
    sd_done = [sem(f"sd_done{n}", GRP) for n in range(3)]
    rs_done = [sem(f"rs_done{n}", GRP) for n in range(3)]
    hi_part_done = [sem(f"hi_part_done{n}", GRP) for n in range(3)]
    parts_done = [sem(f"parts_done{n}", GRP) for n in range(3)]
    bc_mm = [sem(f"bc_mm{n}", CHUNKS) for n in range(3)]
    mul_done = [sem(f"mul_done{n}", CHUNKS) for n in range(3)]
    h_mm = sem("h_mm", CHUNKS)
    h_done = sem("h_done", CHUNKS)
    t2_done = sem("t2_done", CHUNKS)
    vrow_done = sem("vrow_done", GRP)
    vt_mm = sem("vt_mm", 1)
    zsd_done = sem("zsd_done", 1)
    lgr_mm = sem("lgr_mm", 1)
    lgr_done = sem("lgr_done", 1)
    lgt_mm = sem("lgt_mm", 1)
    r_step = sem("r_step", ROUTER_STEPS)
    dl_done = sem("dl_done", 1)
    gth_done = sem("gth_done", 1)
    gate_done = sem("gate_done", 1)
    gt_mm = sem("gt_mm", CHUNKS)
    gt_done = sem("gt_done", CHUNKS)
    t2_stored = sem("t2_stored", CHUNKS, 16)
    xn_stored = [sem(f"xn_stored{k}", CHUNKS // 2, 16) for k in range(2)]
    gate_stored = sem("gate_stored", 4, 16)

    E = EXPERTS
    C2 = 4
    m_wloaded = sem("m_wloaded")
    m_step = sem("m_step")
    m_bias_mm = sem("m_bias_mm")
    half_in = [sem(f"half_in{k}", 3, 16) for k in range(2)]
    hi_done = sem("hi_done", C2)
    xs_done = sem("xs_done", C2)
    wr_mm = sem("wr_mm", C2 * E)
    wr_done = sem("wr_done", C2 * E)
    a_mm = sem("a_mm", C2 * E * 2)
    g_done = sem("g_done", C2 * E * 2)
    y_mm = sem("y_mm", C2 * E)
    yw_done = sem("yw_done", C2 * E)
    acc_done = sem("acc_done", C2 * E)
    ot_mm = sem("ot_mm", C2)
    ot_done = sem("ot_done", C2)
    out_stored = [sem(f"out_stored{k}", C2, 16) for k in range(2)]

    x_v = A["x"].rearrange("b (a s r u) (c w) k -> b s r u a c (w k)", a=WS, s=2, r=2, u=2, c=WS, w=8)
    out_v = A["out"].rearrange("b (a s r) (c w) k -> b r s a c (w k)", a=WS, s=2, r=4, c=WS, w=8)

    def by_window(ap):
        return ap.rearrange("p (w t) -> p w t", t=TOK)

    block = ctx.enter_context(nc.Block())

    def end_of_phase1(eng):
        eng.drain().then_inc(phase1_end.h, 1)
        eng.wait_ge(phase1_end.h, PRIME + 5)

    @block.sync
    def _(sp):
        count = [0]

        def load(dst, src):
            sp.dma_start(dst, src).then_inc(wloaded.h, 16)
            count[0] += 1

        load(const[:], A["const"])
        sp.wait_ge(zeroed.h, PRIME + 2)
        for s in range(2):
            lo, hi = 64 * s, 64 * s + 64
            load(wq[lo:hi, lo:hi], A["qkv_wT"][:, 0:64])
            load(wk[lo:hi, lo:hi], A["qkv_wT"][:, 64:128])
            load(wv[lo:hi, lo:hi], A["qkv_wT"][:, 128:192])
            load(w_in[lo:hi, lo:hi], A["ffn_in_wT"])
            load(w_out[lo:hi, lo:hi], A["ffn_out_w"])
            load(w_ih[lo:hi, lo:hi], A["W_ihT"])
            load(w_hh[lo:hi, lo:hi], A["W_hhT"])
            load(w_r[lo:hi, E * s:E * s + E], A["Wr"])
            load(b_r[:, E * s:E * s + E], A["br"].partition_broadcast(ROWS2))
            load(bq[lo:hi], A["qkv_b"][0:64].unsqueeze(1))
            load(bk[lo:hi], A["qkv_b"][64:128].unsqueeze(1))
            load(lng[lo:hi], A["ln_g"].unsqueeze(1))
            load(lnb[lo:hi], A["ln_b"].unsqueeze(1))
            load(brnn[lo:hi], A["b_ih"].unsqueeze(1))
            load(brnn2[lo:hi], A["b_hh"].unsqueeze(1))
        load(bv[:], A["qkv_b"][128:192].partition_broadcast(128))
        assert count[0] == WLOADS
        for dst, name in ((raw3, "conv3f"), (raw5, "conv5f"), (raw7, "conv7f")):
            sp.dma_start(dst, A[name]).then_inc(taps_in.h, 16)

        def load_x(image0):
            for m in range(GROUP):
                for s in range(2):
                    for r in range(2):
                        for u in range(2):
                            sp.dma_start(x_in[TOK * r:TOK * r + TOK, m, s, u].rearrange("p w k -> p (w k)"),
                                         x_v[image0 + m, s, r, u]).then_inc(x_loaded.h, 16)

        load_x(0)
        sp.wait_ge(taps_step.h, PRIME + 6)
        sp.dma_start(taps_dram.rearrange("x c n -> c x n"), spread.rearrange("p x u v -> p x (u v)")
                     ).then_inc(taps_saved.h, 16)
        sp.wait_ge(taps_saved.h, PRIME + 16)
        sp.wait_ge(zeroed.h, PRIME + 2)
        for s in range(2):
            for y in range(WS):
                p = 64 * s + WS * y
                sp.dma_start(conv_m[p:p + WS, :, s, 0:TOK],
                             taps_dram[:, :, WS * (WS - 1 - y):WS * (WS - 1 - y) + TOK]).then_inc(conv_w.h, 16)

        def iteration(i, following):
            if following:
                sp.wait_ge(rows_done.h, rows_done.upto(i, 1))
                load_x((i + 1) * GROUP)
            sp.wait_ge(conv_mm.h, conv_mm.upto(i, 0))
            sp.sem_inc(passed.h, 1)
            for c in range(CHUNKS):
                sp.wait_ge(v_done.h, v_done.upto(i, c + 1))
                for j in range(2):
                    to, fro = slice(64 - 64 * j, 128 - 64 * j), slice(64 * j, 64 * j + 64)
                    sp.dma_start(v_all[to, 8 * c:8 * c + 8, :].rearrange("p (q j) k -> p q j k", j=2)[:, :, j, :],
                                 v_tok[fro, c % 2, :, 1 - j, :]).then_inc(v_swapped[c % 2].h, 16)
            for c in range(CHUNKS):
                sp.wait_ge(t2_done.h, t2_done.upto(i, c + 1))
                sp.dma_start(t2_dram[i * 4 + c // 2, :, (c % 2) * CW:(c % 2) * CW + CW],
                             t2[:, c * CW:c * CW + CW]).then_inc(t2_stored.h, 16)
            for c in range(CHUNKS):
                sp.wait_ge(mul_done[2].h, mul_done[2].upto(i, c + 1))
                sp.dma_start(xn_dram[i * 4 + c // 2, :, (c % 2) * CW:(c % 2) * CW + CW],
                             xn[:, c % 2, :]).then_inc(xn_stored[c % 2].h, 16)
            for q in range(4):
                sp.wait_ge(gt_done.h, gt_done.upto(i, 2 * q + 2))
                sp.dma_start(gate_dram[i * 4 + q], gateT[:, q * HW2:q * HW2 + HW2]).then_inc(gate_stored.h, 16)

        with sp.Fori(0, ITERS - 1) as i:
            iteration(i, True)
        iteration(ITERS - 1, False)
        sp.wait_ge(t2_stored.h, t2_stored.upto(ITERS, 0))
        for k in range(2):
            sp.wait_ge(xn_stored[k].h, xn_stored[k].upto(ITERS, 0))
        sp.wait_ge(gate_stored.h, gate_stored.upto(ITERS, 0))
        end_of_phase1(sp)

        count[0] = 0

        def mload(dst, src):
            sp.dma_start(dst, src).then_inc(m_wloaded.h, 16)
            count[0] += 1

        for s in range(2):
            lo, hi = 64 * s, 64 * s + 64
            mload(w1[lo:hi], A["W1"].rearrange("e k h -> k e h"))
            mload(b2[lo:hi], A["b2T"])
            mload(ge[lo:hi], A["ln_geT"])
            mload(be[lo:hi], A["ln_beT"])
        for m in range(2):
            mload(w2[:, :, m, :], A["W2"].rearrange("e (m h) k -> m h e k", m=2)[m])
        mload(b1[:], A["b1P"])
        mload(sel[:], A["sel"])
        assert count[0] == MLOADS

        def load_half(image, k):
            half = image * 2 + k
            sp.dma_start(xnl[:, k, :], xn_dram[half]).then_inc(half_in[k].h, 16)
            sp.dma_start(gatel[:, k, :], gate_dram[half]).then_inc(half_in[k].h, 16)
            sp.dma_start(t2l[:, k, :], t2_dram[half]).then_inc(half_in[k].h, 16)

        for k in range(2):
            load_half(0, k)

        def m_iteration(i, following):
            for c in range(C2):
                sp.wait_ge(ot_done.h, ot_done.upto(i, c + 1))
                for s in range(2):
                    sp.dma_start(out_v[i, c, s], ot[TOK * s:TOK * s + TOK, c % 2, :]).then_inc(out_stored[c % 2].h, 16)
                if following and c % 2 == 1:
                    sp.wait_ge(wr_mm.h, wr_mm.upto(i, (c + 1) * E))
                    sp.sem_inc(passed.h, 1)
                    sp.wait_ge(xs_done.h, xs_done.upto(i, c + 2))
                    load_half(i + 1, c // 2)

        with sp.Fori(0, IMAGES - 1) as i:
            m_iteration(i, True)
        m_iteration(IMAGES - 1, False)
        for k in range(2):
            sp.wait_ge(out_stored[k].h, out_stored[k].upto(IMAGES, 0))

    @block.gpsimd
    def _(pool):
        for s in all_sems:
            pool.sem_inc(s.h, PRIME * s.step)
        for t in (wq, wk, wv, w_in, w_out, w_ih, w_hh, w_r, wr_rows):
            nc.gpsimd.memset(t[:], 0.0)
        nc.gpsimd.memset(conv_m[:], 0.0).then_inc(zeroed.h, 1)
        nc.gpsimd.memset(xT[:], 0.0)
        nc.gpsimd.memset(rs_parts[:].bitcast(F32), 0.0)
        nc.gpsimd.memset(q_diag[:], 0.0)
        nc.gpsimd.memset(probs[:], 0.0)
        nc.gpsimd.memset(hid[:], 0.0)
        nc.gpsimd.memset(v_heads[:], 0.0).then_inc(zeroed.h, 1)
        pool.wait_ge(zeroed.h, PRIME + 2)
        for k in range(2):
            part = v_heads[64 * k:64 * k + 64].rearrange("p a w h s i d -> p (a w h s) i d")
            last = nc.gpsimd.memset(part[:, :, k, HD:HD + 1], 20.0)
        last.then_inc(zeroed.h, 1)
        pool.wait_ge(zeroed.h, PRIME + 3)

        def settle():
            pool.sem_inc(passed.h, 1)

        def copy(out, src):
            return nc.gpsimd.tensor_scalar(out, src, 1.0, 1.0, ALU.mult, ALU.mult)

        def heads_of_k(i, c):
            if c:
                pool.wait_ge(vh_done.h, vh_done.upto(i, c))
            else:
                pool.wait_ge(rows_done.h, rows_done.upto(i, 1))
            pool.wait_ge(k_done.h, k_done.upto(i, c + 1))
            pool.wait_ge(gate_stored.h, gate_stored.upto(i, 0))
            pool.wait_ge(s_mm.h, s_mm.upto(i, 4 * (c - 1)))
            settle()
            for h in range(HEADS):
                last = nc.gpsimd.tensor_scalar(k_heads[:, c % 2, :, h, :], k_sb[:, 0], headmask[:, h:h + 1], 1.0,
                                               ALU.mult, ALU.mult)
            last.then_inc(kh_done.h, 1)

        def heads_of_v(i, c):
            pool.wait_ge(kh_done.h, kh_done.upto(i, c + 1))
            pool.wait_ge(v_done.h, v_done.upto(i, c + 1))
            pool.wait_ge(o_mm.h, o_mm.upto(i, 4 * (c - 1)))
            if c == 0:
                pool.wait_ge(conv_mm.h, conv_mm.upto(i, 0))
            settle()
            for j in range(2):
                p = slice(64 * j, 64 * j + 64)
                for s in range(2):
                    copy(v_heads[p, c % 2, :, :, s, j, 0:HD],
                         v_tok[p, c % 2, :, s, :].rearrange("p q (h d) -> p q h d", h=HEADS))
                own = v_all[p, 8 * c:8 * c + 8, :].rearrange("p (q j) k -> p q j k", j=2)[:, :, j, :]
                last = copy(own, v_tok[p, c % 2, :, j, :])
            last.then_inc(vh_done.h, 1)

        def regroup_x(i):
            pool.wait_ge(vh_done.h, vh_done.upto(i, 0))
            pool.wait_ge(x_loaded.h, x_loaded.upto(i, 8 * GROUP))
            pool.wait_ge(xot_mm.h, xot_mm.upto(i, 0))
            pool.wait_ge(gate_done.h, gate_done.upto(i, 0))
            settle()
            for m in range(GROUP):
                for s in range(2):
                    last = copy(x_rows[:, m, :, :, s, :], x_in[:, m, s])
            last.then_inc(rows_done.h, 1)

        pool.wait_ge(taps_saved.h, PRIME + 16)
        with pool.Fori(0, ITERS) as i:
            regroup_x(i)
            heads_of_k(i, 0)
            heads_of_v(i, 0)
            for c in range(1, CHUNKS):
                heads_of_k(i, c)
                heads_of_v(i, c)
        end_of_phase1(pool)

        def split_x(i, c):
            k = (c % C2) // 2
            pool.wait_ge(acc_done.h, acc_done.upto(i, max(0, (c - 1) * E + 3)))
            if c % 2 == 0:
                pool.wait_ge(half_in[k].h, half_in[k].upto(i + (c == C2), 3))
            pool.wait_ge(a_mm.h, a_mm.upto(i, 2 * E * (c - 1)))
            cols = slice((c % 2) * CW, (c % 2) * CW + CW)
            settle()
            for j in range(2):
                p = slice(64 * j, 64 * j + 64)
                last = copy(xs[p, c % 2, j, :], xnl[p, k, cols])
            last.then_inc(hi_done.h, 1)
            pool.wait_ge(hi_done.h, hi_done.upto(i, c + 1))
            for j in range(2):
                p, other = slice(64 * j, 64 * j + 64), slice(64 - 64 * j, 128 - 64 * j)
                last = nc.gpsimd.tensor_tensor(xs[other, c % 2, j, :], xnl[p, k, cols],
                                               xs[p, c % 2, j, :].bitcast(F32), ALU.subtract)
            last.then_inc(xs_done.h, 1)

        def m_iteration(i, following):
            for c in range(C2):
                for e in range(E):
                    n = c * E + e
                    pool.wait_ge(yw_done.h, yw_done.upto(i, n + 1))
                    if e == 0:
                        pool.wait_ge(ot_mm.h, ot_mm.upto(i, c - 1))
                        other = t2l[:, c // 2, (c % 2) * CW:(c % 2) * CW + CW]
                    else:
                        pool.wait_ge(acc_done.h, acc_done.upto(i, n))
                        if e == 3 and (c + 1 < C2 or following):
                            pool.wait_ge(xs_done.h, xs_done.upto(i, c + 2))
                        other = acc[:, c % 2, :]
                    nc.gpsimd.tensor_tensor(acc[:, c % 2, :], yw[:, n % 4, :], other, ALU.add
                                            ).then_inc(acc_done.h, 1)
                    if e == 2 and (c + 1 < C2 or following):
                        split_x(i, c + 1)

        split_x(0, 0)
        with pool.Fori(0, IMAGES - 1) as i:
            m_iteration(i, True)
        m_iteration(IMAGES - 1, False)

    @block.scalar
    def _(act):
        act.wait_ge(prepared.h, PRIME + PREP_STEPS)

        def evacuate_xT(i, n):
            m, u, wh = n // 4, (n // 2) % 2, n % 2
            act.wait_ge(xt_mm.h, xt_mm.upto(i, n + 1))
            if n == 0:
                act.wait_ge(t2_done.h, t2_done.upto(i, 0))
                act.wait_ge(d_mm[1].h, d_mm[1].upto(i, 0))
            src = bank(n % 2)[:, 0:CW].rearrange("p (w r t) -> p r w t", r=2, t=TOK)
            for r in range(2):
                last = nc.scalar.activation(xT[:, m, 2 * r + u, 4 * wh:4 * wh + 4, 0:TOK], src[:, r], ACT.Copy)
            last.then_inc(xt_done.h, 1)

        def evacuate_qk(i, c):
            act.wait_ge(q_mm.h, q_mm.upto(i, c + 1))
            act.wait_ge(s_mm.h, s_mm.upto(i, 4 * (c - 1)))
            src = bank(0)[:, 0:CW].rearrange("p (w t) -> p w t", t=TOK)
            for s in range(2):
                p = slice(64 * s, 64 * s + 64)
                last = nc.scalar.activation(q_diag[p, c % 2, :, s, 0:TOK], src[p], ACT.Identity,
                                            bias=bq[p], scale=HD ** -0.5)
            last.then_inc(q_done.h, 1)
            act.wait_ge(k_mm.h, k_mm.upto(i, c + 1))
            act.wait_ge(kh_done.h, kh_done.upto(i, c))
            nc.scalar.activation(k_sb[:, 0].rearrange("p w t -> p (w t)"), bank(1)[:, 0:CW], ACT.Identity,
                                 bias=bk).then_inc(k_done.h, 1)

        def exponential(i, u):
            act.wait_ge(sub_done.h, sub_done.upto(i, u + 1))
            v = probs[:, u % 3].rearrange("p h j k -> p (h j) k")[:, :, 0:TOK]
            nc.scalar.activation(v, v, ACT.Exp).then_inc(exp_done.h, 1)

        def evacuate_pt(i, u):
            act.wait_ge(pt_mm.h, pt_mm.upto(i, u + 1))
            act.wait_ge(o_mm.h, o_mm.upto(i, u - 1))
            nc.scalar.activation(probsT[:, u % 2, :], bank(4 + u % 2), ACT.Copy).then_inc(pt_done.h, 1)

        def deviations(i, n, c):
            bias = lnb_c if n == 1 else 0.0
            act.wait_ge(d_mm[n].h, d_mm[n].upto(i, c + 1))
            if c >= 2:
                act.wait_ge(var_mm[n].h, var_mm[n].upto(i, c - 1))
            else:
                act.wait_ge(var_mm[(n - 1) % 3].h, var_mm[(n - 1) % 3].upto(i, CHUNKS if n else 0))
            if n == 0 and c == 0:
                act.wait_ge(lgt_mm.h, lgt_mm.upto(i, 0))
            d = bank(c % 2)[:, 0:CW]
            nc.scalar.activation(sq[:, c % 2, :], d, ACT.Square, bias=bias).then_inc(sq_done[n].h, 1)
            nc.scalar.activation(dev[:, c * CW:c * CW + CW], d, ACT.Identity if n == 1 else ACT.Copy, bias=bias
                                 ).then_inc(dev_done[n].h, 1)

        def root(i, n, grp):
            act.wait_ge(var_mm[n].h, var_mm[n].upto(i, GC * grp + GC))
            act.wait_ge(rs_done[(n - 1) % 3].h, rs_done[(n - 1) % 3].upto(i, (grp + 1) if n else grp + 1 - GRP))
            v = bank(2 + grp)[:, 0:CW]
            if n < 2:
                nc.scalar.activation(sd[:, grp, :], v, ACT.Sqrt, bias=eps_c).then_inc(sd_done[n].h, 1)
                return
            nc.scalar.activation(sd[:, grp, :], v, ACT.Sqrt, bias=eps2_c, scale=1.0 + LN_EPS
                                 ).then_inc(sd_done[n].h, 1)
            act.wait_ge(gate_done.h, gate_done.upto(i, 0))
            nc.scalar.activation(var_rows[grp], v[0:2 * GC], ACT.Copy).then_inc(vrow_done.h, 1)

        with act.Fori(0, ITERS) as i:
            for n in range(8):
                evacuate_xT(i, n)
            evacuate_qk(i, 0)
            for u in range(UNITS + 2):
                if u % 4 == 0 and u // 4 + 1 < CHUNKS:
                    evacuate_qk(i, u // 4 + 1)
                if u < UNITS:
                    exponential(i, u)
                if u >= 2:
                    evacuate_pt(i, u - 2)
            for c in range(CHUNKS):
                act.wait_ge(xot_mm.h, xot_mm.upto(i, c + 1))
                act.wait_ge(mul_done[2].h, mul_done[2].upto(i, 0))
                nc.scalar.activation(xoT[:, c * CW:c * CW + CW].rearrange("p (a t) -> p a t", t=TOK),
                                     bank(c % 2).rearrange("p (a t) -> p a t", t=PAD)[:, :, 0:TOK],
                                     ACT.Copy).then_inc(xot_done.h, 1)
            for k in range(CHUNKS + 2):
                if k < CHUNKS:
                    act.wait_ge(f_mm.h, f_mm.upto(i, k + 1))
                    if k >= 2:
                        act.wait_ge(u_done.h, u_done.upto(i, k - 1))
                    else:
                        act.wait_ge(xn_stored[k].h, xn_stored[k].upto(i, 0))
                    nc.scalar.activation(th[:, k % 2, :], bank(4 + k % 2)[:, 0:CW], ACT.Tanh, scale=0.5
                                         ).then_inc(th_done.h, 1)
                if k >= 2:
                    deviations(i, 0, k - 2)
            root(i, 0, 0)
            root(i, 0, 1)
            for c in range(CHUNKS):
                deviations(i, 1, c)
            root(i, 1, 0)
            root(i, 1, 1)
            for k in range(CHUNKS + 3):
                if 1 <= k <= CHUNKS:
                    c = k - 1
                    act.wait_ge(h_mm.h, h_mm.upto(i, c + 1))
                    act.wait_ge(t2_done.h, t2_done.upto(i, c - 3))
                    nc.scalar.activation(hid[:, (c % 4) * CW:(c % 4) * CW + CW], bank(4 + c % 2)[:, 0:CW], ACT.Tanh,
                                         bias=brnn).then_inc(h_done.h, 1)
                if k >= 3:
                    deviations(i, 2, k - 3)
                if k == CHUNKS:
                    root(i, 2, 0)
            root(i, 2, 1)
            act.wait_ge(lgr_mm.h, lgr_mm.upto(i, 1))
            act.wait_ge(var_mm[2].h, var_mm[2].upto(i, CHUNKS))
            nc.scalar.activation(lg_rows, bank(4)[:, 0:CW], ACT.Copy).then_inc(lgr_done.h, 1)
            act.wait_ge(vt_mm.h, vt_mm.upto(i, 1))
            act.wait_ge(gate_done.h, gate_done.upto(i, 0))
            nc.scalar.activation(r_small[0:ROWS2, 7, :], bank(0)[0:ROWS2, 0:2 * UNITS], ACT.Sqrt,
                                 bias=eps_c[0:ROWS2]).then_inc(zsd_done.h, 1)
            act.wait_ge(dl_done.h, dl_done.upto(i, 1))
            nc.scalar.activation(r_small[0:ROWS2, 5, :], r_small[0:ROWS2, 4, :], ACT.Tanh, scale=0.5
                                 ).then_inc(gth_done.h, 1)
            for c in range(CHUNKS):
                act.wait_ge(gt_mm.h, gt_mm.upto(i, c + 1))
                act.wait_ge(gate_stored.h, gate_stored.upto(i, 0))
                nc.scalar.activation(gateT[:, c * CW:c * CW + CW], bank(6 + c % 2)[0:GROWS, :].bitcast(BF16)[:, 0:CW],
                                     ACT.Copy).then_inc(gt_done.h, 1)
        end_of_phase1(act)

        act.wait_ge(m_step.h, PRIME + M_STEPS)

        def m_iteration(i):
            for c in range(C2):
                for e in range(E):
                    for m in range(2):
                        n = (c * E + e) * 2 + m
                        act.wait_ge(a_mm.h, a_mm.upto(i, n + 1))
                        act.wait_ge(y_mm.h, y_mm.upto(i, c * E + e - 1))
                        nc.scalar.activation(g[:, n % 4], PS[:, 2 * m:2 * m + 2, 0:CW], ACT.Gelu,
                                             bias=b1[:, e, m:m + 1]).then_inc(g_done.h, 1)

        with act.Fori(0, IMAGES) as i:
            m_iteration(i)

    @block.vector
    def _(dve):
        steps = [0]

        def step(ins):
            steps[0] += 1
            ins.then_inc(prepared.h, 1)
            dve.wait_ge(prepared.h, PRIME + steps[0])

        dve.wait_ge(taps_in.h, PRIME + 48)
        grid = taps.rearrange("p (a b) -> p a b", b=OFF)
        nc.vector.memset(taps, 0.0).then_inc(taps_step.h, 1)
        for n, (raw, size) in enumerate(((raw7, 7), (raw5, 5), (raw3, 3))):
            lo = (OFF - size) // 2
            dve.wait_ge(taps_step.h, PRIME + n + 1)
            part = grid[:, lo:lo + size, lo:lo + size]
            nc.vector.scalar_tensor_tensor(part, raw.rearrange("p (a b) -> p a b", b=size), 0.25 * 0.2, part,
                                           ALU.mult, ALU.add).then_inc(taps_step.h, 1)
        dve.wait_ge(taps_step.h, PRIME + 4)
        mid = grid[:, WS - 1:WS, WS - 1:WS]
        nc.vector.tensor_scalar(mid, mid, 1.0, None, ALU.add).then_inc(taps_step.h, 1)
        dve.wait_ge(taps_step.h, PRIME + 5)
        for x in range(WS):
            last = nc.vector.tensor_copy(spread[:, x], grid[:, :, WS - 1 - x:2 * WS - 1 - x])
        last.then_inc(taps_step.h, 1)
        dve.wait_ge(wloaded.h, PRIME + 16 * WLOADS)
        step(nc.vector.scalar_tensor_tensor(wv[:], wv[:], 0.1, ident, ALU.mult, ALU.add))
        step(nc.vector.tensor_copy(from_rows[:].rearrange("p a b -> p (a b)"), rows_back))
        step(nc.vector.tensor_scalar(bv[:], bv[:], 0.1, None, ALU.mult))
        step(nc.vector.tensor_scalar(bq, bq, HD ** -0.5, None, ALU.mult))
        step(nc.vector.tensor_tensor(brnn, brnn, brnn2, ALU.add))
        step(nc.vector.memset(eps_c, LN_EPS))
        step(nc.vector.memset(eps2_c, LN_EPS * LN_EPS))
        step(nc.vector.tensor_copy(ident_b[:], ident))
        dve.wait_ge(outc_mm.h, PRIME + 1)
        step(nc.vector.tensor_scalar(w_outc[:], bank(7)[:, 0:128], 0.25, None, ALU.mult))
        step(nc.vector.tensor_copy(wr_rows[:, 112:112 + 2 * E], bank(7)[:, 128:128 + 2 * E]))
        step(nc.vector.tensor_copy(lnb_c, bank(7)[:, 144:145]))
        assert steps[0] == PREP_STEPS

        def evacuate_v(i, c):
            dve.wait_ge(v_mm.h, v_mm.upto(i, c + 1))
            dve.wait_ge(vh_done.h, vh_done.upto(i, c - 1))
            dve.wait_ge(v_swapped[c % 2].h, v_swapped[c % 2].upto(i, 2 * (c // 2)))
            nc.vector.tensor_tensor(v_tok[:, c % 2].rearrange("p q s k -> p (q s) k"),
                                    bank(0).rearrange("p (n k) -> p n k", k=CH),
                                    bv[:].unsqueeze(1).broadcast_to([128, 8, CH]), ALU.add).then_inc(v_done.h, 1)

        def less_max(i, u):
            sc = bank(2 + u % 2)[:, 0:CW].rearrange("p (g k) -> p g k", k=TOK)
            dve.wait_ge(s_mm.h, s_mm.upto(i, u + 1))
            nc.vector.tensor_reduce(mx[:, u % 2, :], sc, AX.X, ALU.max).then_inc(max_done.h, 1)
            dve.wait_ge(max_done.h, max_done.upto(i, u + 1))
            dve.wait_ge(pt_mm.h, pt_mm.upto(i, u - 2))
            nc.vector.tensor_tensor(probs[:, u % 3].rearrange("p h j k -> p (h j) k")[:, :, 0:TOK], sc,
                                    mx[:, u % 2, :].unsqueeze(2).broadcast_to([128, 8, TOK]), ALU.subtract
                                    ).then_inc(sub_done.h, 1)

        def normalise(i, u):
            dve.wait_ge(o_mm.h, o_mm.upto(i, u + 1))
            o = bank(6 + u % 2)[:, 0:4 * 68].rearrange("p (h s j d) -> p h s j d", h=HEADS, s=2, j=2)
            if u == 0:
                dve.wait_ge(xt_mm.h, xt_mm.upto(i, 8))
            for s in range(2):
                p = slice(64 * s, 64 * s + 64)
                last = nc.vector.reciprocal(rden[p, u % 2], o[p, :, s, :, HD])
            last.then_inc(rden_done.h, 1)
            dve.wait_ge(rden_done.h, rden_done.upto(i, u + 1))
            for s in range(2):
                p = slice(64 * s, 64 * s + 64)
                last = nc.vector.tensor_tensor(
                    xo[p, 2 * u:2 * u + 2, :].rearrange("p j (h d) -> p h j d", h=HEADS), o[p, :, s, :, 0:HD],
                    rden[p, u % 2].unsqueeze(3).broadcast_to([64, 4, 2, HD]), ALU.mult)
            last.then_inc(o_done.h, 1)

        def inverse_deviation(i, n, grp):
            dve.wait_ge(sd_done[n].h, sd_done[n].upto(i, grp + 1))
            nc.vector.reciprocal(rs[:, grp, :], sd[:, grp, :]).then_inc(rs_done[n].h, 1)
            dve.wait_ge(rs_done[n].h, rs_done[n].upto(i, grp + 1))
            if n:
                dve.wait_ge(bc_mm[n - 1].h, bc_mm[n - 1].upto(i, GC * grp + GC))
            else:
                dve.wait_ge(bc_mm[2].h, bc_mm[2].upto(i, GC * (grp + 1 - GRP)))
            nc.vector.tensor_copy(rs_parts[0:64, grp, :], rs[0:64, grp, :]).then_inc(hi_part_done[n].h, 1)
            dve.wait_ge(hi_part_done[n].h, hi_part_done[n].upto(i, grp + 1))
            low = rs_parts[32:64, grp, :]
            nc.vector.tensor_tensor(low, rs[32:64, grp, :], low.bitcast(F32), ALU.subtract
                                    ).then_inc(parts_done[n].h, 1)

        def scale(i, n, c):
            cols = slice(c * CW, c * CW + CW)
            dve.wait_ge(bc_mm[n].h, bc_mm[n].upto(i, c + 1))
            dve.wait_ge(dev_done[n].h, dev_done[n].upto(i, c + 1))
            r = bank(6 + c % 2)[:, 0:CW]
            if n == 0:
                nc.vector.scalar_tensor_tensor(tT[c], by_window(dev[:, cols]), lng, by_window(r), ALU.mult, ALU.mult
                                               ).then_inc(mul_done[0].h, 1)
            elif n == 1:
                nc.vector.tensor_tensor(z1[:, cols], dev[:, cols], r, ALU.mult).then_inc(mul_done[1].h, 1)
            else:
                dve.wait_ge(xn_stored[c % 2].h, xn_stored[c % 2].upto(i, c // 2))
                nc.vector.tensor_tensor(xn[:, c % 2, :], dev[:, cols], r, ALU.mult).then_inc(mul_done[2].h, 1)

        def residual(i, c):
            cols = slice(c * CW, c * CW + CW)
            dve.wait_ge(h_done.h, h_done.upto(i, c + 1))
            dve.wait_ge(d_mm[0].h, d_mm[0].upto(i, CHUNKS))
            dve.wait_ge(mul_done[0].h, mul_done[0].upto(i, CHUNKS))
            nc.vector.scalar_tensor_tensor(by_window(t2[:, cols]), tT[c], lnb,
                                           by_window(hid[:, (c % 4) * CW:(c % 4) * CW + CW]), ALU.add, ALU.add).then_inc(t2_done.h, 1)

        def route(i):
            n = [0]
            wide = [ROWS2, 2 * UNITS, E]

            def rstep(ins):
                n[0] += 1
                ins.then_inc(r_step.h, 1)
                dve.wait_ge(r_step.h, r_step.upto(i, n[0]))

            def over(x):
                return r_small[0:ROWS2, x, :].unsqueeze(2).broadcast_to(wide)

            rk = rank.unsqueeze(1).broadcast_to(wide)
            dve.wait_ge(zsd_done.h, zsd_done.upto(i, 1))
            rstep(nc.vector.reciprocal(r_small[0:ROWS2, 6, :], r_small[0:ROWS2, 7, :]))
            dve.wait_ge(lgt_mm.h, lgt_mm.upto(i, 1))
            rstep(nc.vector.tensor_tensor(lg[:], bank(5)[0:ROWS2].rearrange("p (n e) -> p n e", e=E), over(6), ALU.mult))
            by_pair = lg[:].rearrange("p (n j) e -> p n (j e)", j=2)
            rstep(nc.vector.tensor_tensor(by_pair, by_pair, b_r[:].unsqueeze(1).broadcast_to([ROWS2, UNITS, 2 * E]),
                                          ALU.add))
            dve.wait_ge(gt_mm.h, gt_mm.upto(i, 0))
            for k, oh in ((0, oh1), (1, oh2)):
                best, first = r_small[0:ROWS2, 2 * k, :], r_small[0:ROWS2, 2 * k + 1, :]
                rstep(nc.vector.tensor_reduce(best, lg[:], AX.X, ALU.max))
                rstep(nc.vector.tensor_tensor(oh[:], lg[:], over(2 * k), ALU.is_equal))
                rstep(nc.vector.tensor_tensor(oh[:], oh[:], rk, ALU.mult))
                rstep(nc.vector.tensor_reduce(first, oh[:], AX.X, ALU.max))
                rstep(nc.vector.tensor_tensor(oh[:], oh[:], over(2 * k + 1), ALU.is_equal))
                if k == 0:
                    rstep(nc.vector.scalar_tensor_tensor(lg[:], oh[:], -BIG, lg[:], ALU.mult, ALU.add))
            nc.vector.tensor_tensor(r_small[0:ROWS2, 4, :], r_small[0:ROWS2, 0, :], r_small[0:ROWS2, 2, :],
                                    ALU.subtract).then_inc(dl_done.h, 1)
            dve.wait_ge(gth_done.h, gth_done.upto(i, 1))
            rstep(nc.vector.tensor_scalar(r_small[0:ROWS2, 6, :], r_small[0:ROWS2, 5, :], 0.5, 0.5, ALU.mult, ALU.add))
            rstep(nc.vector.tensor_scalar(r_small[0:ROWS2, 7, :], r_small[0:ROWS2, 5, :], -0.5, 0.5, ALU.mult, ALU.add))
            rstep(nc.vector.tensor_tensor(oh1[:], oh1[:], over(6), ALU.mult))
            rstep(nc.vector.tensor_tensor(oh2[:], oh2[:], over(7), ALU.mult))
            rstep(nc.vector.tensor_tensor(gate[:], oh1[:], oh2[:], ALU.add))
            part = [gate3[:, :, k, :] for k in range(PARTS)]
            whole = gate[:].rearrange("p (u j) e -> p u (j e)", j=2)
            rest = gate_rest[:].rearrange("p (u j) e -> p u (j e)", j=2)
            rstep(nc.vector.tensor_copy(part[0], whole))
            rstep(nc.vector.tensor_tensor(rest, whole, part[0], ALU.subtract))
            rstep(nc.vector.tensor_copy(part[1], rest))
            assert n[0] == ROUTER_STEPS
            nc.vector.tensor_tensor(part[2], rest, part[1], ALU.subtract).then_inc(gate_done.h, 1)

        with dve.Fori(0, ITERS) as i:
            evacuate_v(i, 0)
            for u in range(UNITS + 3):
                if u < UNITS:
                    less_max(i, u)
                if u % 4 == 2 and u // 4 + 1 < CHUNKS:
                    evacuate_v(i, u // 4 + 1)
                if u >= 3:
                    normalise(i, u - 3)
            dve.wait_ge(o_done.h, o_done.upto(i, UNITS))
            for n in range(8):
                dve.wait_ge(conv_mm.h, conv_mm.upto(i, n + 1))
                part = xo[:, :, 8 * n:8 * n + 8].rearrange("p n k -> p k n")
                nc.vector.tensor_tensor(part, bank(n % 2).rearrange("p (k n) -> p k n", n=PAIRS), part, ALU.add
                                        ).then_inc(conv_done.h, 1)
            for c in range(CHUNKS):
                dve.wait_ge(th_done.h, th_done.upto(i, c + 1))
                dve.wait_ge(t2_stored.h, t2_stored.upto(i, 0))
                dve.wait_ge(lgr_mm.h, lgr_mm.upto(i, 0))
                nc.vector.scalar_tensor_tensor(ffn_u[:, c * CW:c * CW + CW], th[:, c % 2, :], 1.0,
                                               bank(4 + c % 2)[:, 0:CW], ALU.add, ALU.mult).then_inc(u_done.h, 1)
            inverse_deviation(i, 0, 0)
            for c in range(CHUNKS):
                scale(i, 0, c)
                if c == 0:
                    inverse_deviation(i, 0, 1)
            inverse_deviation(i, 1, 0)
            for k in range(CHUNKS + 2):
                if k < CHUNKS:
                    scale(i, 1, k)
                if k == 0:
                    inverse_deviation(i, 1, 1)
                if k >= 2:
                    residual(i, k - 2)
            inverse_deviation(i, 2, 0)
            for c in range(CHUNKS):
                scale(i, 2, c)
                if c == 0:
                    inverse_deviation(i, 2, 1)
            route(i)
        end_of_phase1(dve)

        m_steps = [0]

        def mstep(ins):
            m_steps[0] += 1
            ins.then_inc(m_step.h, 1)
            dve.wait_ge(m_step.h, PRIME + m_steps[0])

        dve.wait_ge(m_bias_mm.h, PRIME + 1)
        mstep(nc.vector.tensor_tensor(b1[:].rearrange("p e m -> p (e m)"), bank(7)[:, 0:2 * E],
                                      b1[:].rearrange("p e m -> p (e m)"), ALU.add))
        mstep(nc.vector.tensor_tensor(w1[:], w1[:], ge[:].unsqueeze(2).broadcast_to([128, E, HID]), ALU.mult))
        mstep(nc.vector.tensor_copy(w1hi[:], w1[:]))
        mstep(nc.vector.tensor_tensor(w1lo[:], w1[:], w1hi[:].bitcast(F32), ALU.subtract))
        mstep(nc.vector.tensor_copy(sel_b[:], sel[:]))
        assert m_steps[0] == M_STEPS

        def spread_gate(i, n):
            dve.wait_ge(wr_mm.h, wr_mm.upto(i, n + 1))
            dve.wait_ge(yw_done.h, yw_done.upto(i, n - 3))
            nc.vector.tensor_copy(wrep[:, n % 4, :], bank(7)[:, 0:CW]).then_inc(wr_done.h, 1)

        def weigh(i, n):
            e = n % E
            dve.wait_ge(y_mm.h, y_mm.upto(i, n + 1))
            dve.wait_ge(wr_done.h, wr_done.upto(i, n + 1))
            dve.wait_ge(acc_done.h, acc_done.upto(i, n - 3))
            nc.vector.scalar_tensor_tensor(yw[:, n % 4, :], bank(4 + n % 2)[:, 0:CW], b2[:, e:e + 1],
                                           wrep[:, n % 4, :], ALU.add, ALU.mult).then_inc(yw_done.h, 1)

        def evacuate_out(i, c):
            dve.wait_ge(ot_mm.h, ot_mm.upto(i, c + 1))
            dve.wait_ge(out_stored[c % 2].h, out_stored[c % 2].upto(i, 2 * (c // 2)))
            nc.vector.tensor_copy(ot[:, c % 2, :], bank(6)[0:ROWS2, :]).then_inc(ot_done.h, 1)

        def m_iteration(i, preceded):
            for n in range(C2 * E):
                spread_gate(i, n)
                if n >= 1 or preceded:
                    weigh(i, n - 1)
                if n % E == 3 and (n > E or preceded):
                    evacuate_out(i, n // E - 1)

        m_iteration(0, False)
        with dve.Fori(1, IMAGES) as i:
            m_iteration(i, True)
        weigh(IMAGES, -1)
        evacuate_out(IMAGES, -1)

    @block.tensor
    def _(pe):
        mm = nc.tensor.matmul
        pe.wait_ge(wloaded.h, PRIME + 16 * WLOADS)
        pe.wait_ge(zeroed.h, PRIME + 3)
        mm(bank(7)[:, 0:128], w_out[:], centre, start=True, stop=True)
        mm(bank(7)[:, 128:128 + 2 * E], centre, w_r[:], start=True, stop=True)
        mm(bank(7)[:, 144:145], centre, lnb, start=True, stop=True).then_inc(outc_mm.h, 1)
        pe.wait_ge(prepared.h, PRIME + PREP_STEPS)

        def project_qk(i, c):
            x = xT[:, c // 4, c % 4, :, 0:TOK]
            if c == 0:
                pe.wait_ge(xt_done.h, xt_done.upto(i, 8))
            else:
                pe.wait_ge(v_done.h, v_done.upto(i, c))
            mm(by_window(bank(0)[:, 0:CW]), wq[:], x, start=True, stop=True).then_inc(q_mm.h, 1)
            if c > 0:
                pe.wait_ge(k_done.h, k_done.upto(i, c))
            mm(by_window(bank(1)[:, 0:CW]), wk[:], x, start=True, stop=True).then_inc(k_mm.h, 1)

        def project_v(i, c):
            pe.wait_ge(q_done.h, q_done.upto(i, c + 1))
            for q in range(4):
                last = mm(bank(0)[:, 128 * q:128 * q + 128],
                          xT[:, c // 4, c % 4, 2 * q:2 * q + 2, :].rearrange("p a b -> p (a b)"),
                          wv[:], start=True, stop=True)
            last.then_inc(v_mm.h, 1)

        def scores(i, u):
            c, q = u // 4, u % 4
            if q == 0:
                pe.wait_ge(q_done.h, q_done.upto(i, c + 1))
                pe.wait_ge(kh_done.h, kh_done.upto(i, c + 1))
            if u >= 2:
                pe.wait_ge(sub_done.h, sub_done.upto(i, u - 1))
            for j in range(2):
                w = 2 * q + j
                out = bank(2 + u % 2)[:, 0:CW].rearrange("p (h j k) -> p h j k", h=HEADS, j=2)
                last = mm(out[:, :, j, :], q_diag[:, c % 2, w].rearrange("p a b -> p (a b)"),
                          k_heads[:, c % 2, w], start=True, stop=True)
            last.then_inc(s_mm.h, 1)

        def turn_probs(i, u):
            pe.wait_ge(exp_done.h, exp_done.upto(i, u + 1))
            if u >= 2:
                pe.wait_ge(pt_done.h, pt_done.upto(i, u - 1))
            for h in range(HEADS):
                last = nc.tensor.transpose(bank(4 + u % 2)[:, 128 * h:128 * h + 128],
                                           probs[:, u % 3, h].rearrange("p a b -> p (a b)"), ident)
            last.then_inc(pt_mm.h, 1)

        def attend(i, u):
            c, q = u // 4, u % 4
            if q == 0:
                pe.wait_ge(vh_done.h, vh_done.upto(i, c + 1))
            pe.wait_ge(pt_done.h, pt_done.upto(i, u + 1))
            if u >= 2:
                pe.wait_ge(o_done.h, o_done.upto(i, u - 1))
            for h in range(HEADS):
                last = mm(bank(6 + u % 2)[:, 68 * h:68 * h + 68], probsT[:, u % 2, 128 * h:128 * h + 128],
                          v_heads[:, c % 2, q, h].rearrange("p s j d -> p (s j d)"), start=True, stop=True)
            last.then_inc(o_mm.h, 1)

        def ffn(i, c):
            pe.wait_ge(xot_done.h, xot_done.upto(i, c + 1))
            if c >= 2:
                pe.wait_ge(u_done.h, u_done.upto(i, c - 1))
            else:
                pe.wait_ge(pt_done.h, pt_done.upto(i, UNITS))
            mm(bank(4 + c % 2)[:, 0:CW], w_in[:], xoT[:, c * CW:c * CW + CW], start=True, stop=True
               ).then_inc(f_mm.h, 1)

        def centred(i, n, c):
            cols = slice(c * CW, c * CW + CW)
            out = bank(c % 2)[:, 0:CW]
            if c >= 2:
                pe.wait_ge(sq_done[n].h, sq_done[n].upto(i, c - 1))
                pe.wait_ge(dev_done[n].h, dev_done[n].upto(i, c - 1))
            elif n == 0:
                pe.wait_ge(xot_done.h, xot_done.upto(i, CHUNKS))
            else:
                pe.wait_ge(sq_done[n - 1].h, sq_done[n - 1].upto(i, CHUNKS))
                pe.wait_ge(dev_done[n - 1].h, dev_done[n - 1].upto(i, CHUNKS))
            if n == 0:
                pe.wait_ge(u_done.h, u_done.upto(i, c + 1))
                mm(out, w_outc[:], ffn_u[:, cols], start=True, stop=False)
                mm(out, centre, xoT[:, cols], start=False, stop=True).then_inc(d_mm[0].h, 1)
            elif n == 1:
                pe.wait_ge(mul_done[0].h, mul_done[0].upto(i, c + 1))
                mm(by_window(out), centre, tT[c], start=True, stop=True).then_inc(d_mm[1].h, 1)
            else:
                pe.wait_ge(t2_done.h, t2_done.upto(i, c + 1))
                mm(out, centre, t2[:, cols], start=True, stop=True).then_inc(d_mm[2].h, 1)

        def variance(i, n, c):
            grp, k = c // GC, c % GC
            pe.wait_ge(sq_done[n].h, sq_done[n].upto(i, c + 1))
            if k == 0 and n == 0:
                pe.wait_ge(sub_done.h, sub_done.upto(i, UNITS))
            elif k == 0:
                pe.wait_ge(sd_done[n - 1].h, sd_done[n - 1].upto(i, grp + 1))
            lo = 2 * GC - 2 - 2 * k
            mm(bank(2 + grp)[:, 0:CW], mean_rows[:, lo:lo + 128], sq[:, c % 2, :], start=(k == 0), stop=(k == GC - 1)
               ).then_inc(var_mm[n].h, 1)

        def spread_rows(i, n, c):
            grp = c // GC
            pe.wait_ge(parts_done[n].h, parts_done[n].upto(i, grp + 1))
            if c >= 2:
                pe.wait_ge(mul_done[n].h, mul_done[n].upto(i, c - 1))
            elif n == 0:
                pe.wait_ge(o_done.h, o_done.upto(i, UNITS))
            else:
                pe.wait_ge(mul_done[n - 1].h, mul_done[n - 1].upto(i, CHUNKS))
            mm(bank(6 + c % 2)[:, 0:CW], from_rows[:, c % GC, :], rs_parts[:, grp, :], start=True, stop=True
               ).then_inc(bc_mm[n].h, 1)

        def recur(i, c):
            pe.wait_ge(mul_done[1].h, mul_done[1].upto(i, c + 1))
            pe.wait_ge(h_done.h, h_done.upto(i, c - 1 if c >= 2 else c - 3))
            if c < 2:
                pe.wait_ge(u_done.h, u_done.upto(i, CHUNKS))
            out = bank(4 + c % 2)[:, 0:CW]
            mm(out, w_ih[:], z1[:, c * CW:c * CW + CW], start=True, stop=False)
            mm(out, w_hh[:], hid[:, (c % 4) * CW:(c % 4) * CW + CW], start=False, stop=True).then_inc(h_mm.h, 1)

        def logits(i):
            pe.wait_ge(h_done.h, h_done.upto(i, CHUNKS))
            for c in range(CHUNKS):
                lo = 112 - 16 * c
                last = mm(bank(4)[:, 0:CW], wr_rows[:, lo:lo + 128], t2[:, c * CW:c * CW + CW],
                          start=(c == 0), stop=(c == CHUNKS - 1))
            last.then_inc(lgr_mm.h, 1)

        def turn_variances(i):
            pe.wait_ge(sq_done[2].h, sq_done[2].upto(i, CHUNKS))
            pe.wait_ge(dev_done[2].h, dev_done[2].upto(i, CHUNKS))
            pe.wait_ge(vrow_done.h, vrow_done.upto(i, GRP))
            pe.sem_inc(passed.h, 1)
            for q in range(4):
                for grp in range(GRP):
                    lo = (GRP * q + grp) * 2 * GC
                    last = nc.tensor.transpose(bank(0)[0:ROWS2, lo:lo + 2 * GC],
                                               var_rows[grp][:, ROWS2 * q:ROWS2 * q + ROWS2],
                                               ident[0:2 * GC, 0:2 * GC])
            last.then_inc(vt_mm.h, 1)

        def turn_logits(i):
            pe.wait_ge(lgr_done.h, lgr_done.upto(i, 1))
            for q in range(4):
                last = nc.tensor.transpose(bank(5)[0:ROWS2, 128 * q:128 * q + 128],
                                           lg_rows[:, ROWS2 * q:ROWS2 * q + ROWS2], ident)
            last.then_inc(lgt_mm.h, 1)

        with pe.Fori(0, ITERS) as i:
            pe.wait_ge(zsd_done.h, zsd_done.upto(i, 0))
            pe.wait_ge(dev_done[2].h, dev_done[2].upto(i, 0))
            pe.wait_ge(sd_done[2].h, sd_done[2].upto(i, 0))
            pe.wait_ge(vrow_done.h, vrow_done.upto(i, 0))
            pe.wait_ge(lgr_done.h, lgr_done.upto(i, 0))
            pe.wait_ge(gate_done.h, gate_done.upto(i, 0))
            pe.wait_ge(gt_done.h, gt_done.upto(i, 0))
            pe.wait_ge(rows_done.h, rows_done.upto(i, 1))
            for n in range(8):
                m, u, wh = n // 4, (n // 2) % 2, n % 2
                if n >= 2:
                    pe.wait_ge(xt_done.h, xt_done.upto(i, n - 1))
                for w in range(4):
                    last = nc.tensor.transpose(bank(n % 2)[:, ROWS2 * w:ROWS2 * w + ROWS2],
                                               x_rows[:, m, u, 4 * wh + w].rearrange("p s k -> p (s k)"), ident[0:ROWS2, 0:ROWS2])
                last.then_inc(xt_mm.h, 1)
            project_qk(i, 0)
            project_v(i, 0)
            for u in range(UNITS + 3):
                if u < UNITS:
                    scores(i, u)
                if u % 4 == 0 and u // 4 + 1 < CHUNKS:
                    project_qk(i, u // 4 + 1)
                if u % 4 == 2 and u // 4 + 1 < CHUNKS:
                    project_v(i, u // 4 + 1)
                if 2 <= u < UNITS + 2:
                    turn_probs(i, u - 2)
                if u >= 3:
                    attend(i, u - 3)
            pe.wait_ge(conv_w.h, PRIME + 16 * 2 * WS)
            pe.wait_ge(v_done.h, v_done.upto(i, CHUNKS))
            pe.wait_ge(k_done.h, k_done.upto(i, CHUNKS))
            pe.wait_ge(vh_done.h, vh_done.upto(i, CHUNKS))
            for k in range(2):
                pe.wait_ge(v_swapped[k].h, v_swapped[k].upto(i, CHUNKS))
            for n in range(8):
                if n >= 2:
                    pe.wait_ge(conv_done.h, conv_done.upto(i, n - 1))
                for k in range(8):
                    last = mm(bank(n % 2)[:, PAIRS * k:PAIRS * k + PAIRS],
                              conv_m[:, 8 * n + k].rearrange("p a b -> p (a b)"), v_all[:, :, 8 * n + k],
                              start=True, stop=True)
                last.then_inc(conv_mm.h, 1)
            pe.wait_ge(conv_done.h, conv_done.upto(i, 8))
            for c in range(CHUNKS):
                if c >= 2:
                    pe.wait_ge(xot_done.h, xot_done.upto(i, c - 1))
                for q in range(4):
                    n = 8 * c + 2 * q
                    last = nc.tensor.transpose(bank(c % 2)[:, 128 * q:128 * q + 128],
                                               xo[:, n:n + 2, :].rearrange("p a b -> p (a b)"), ident)
                last.then_inc(xot_mm.h, 1)
            for k in range(CHUNKS + 3):
                if k < CHUNKS:
                    ffn(i, k)
                if 2 <= k < CHUNKS + 2:
                    centred(i, 0, k - 2)
                if k >= 3:
                    variance(i, 0, k - 3)
            for k in range(CHUNKS + 3):
                if k < CHUNKS:
                    spread_rows(i, 0, k)
                if 2 <= k < CHUNKS + 2:
                    centred(i, 1, k - 2)
                if k >= 3:
                    variance(i, 1, k - 3)
            for k in range(CHUNKS + 4):
                if k < CHUNKS:
                    spread_rows(i, 1, k)
                if 1 <= k < CHUNKS + 1:
                    recur(i, k - 1)
                if 3 <= k < CHUNKS + 3:
                    centred(i, 2, k - 3)
                if k >= 4:
                    variance(i, 2, k - 4)
            logits(i)
            for c in range(CHUNKS):
                spread_rows(i, 2, c)
                if c == GC - 1:
                    turn_variances(i)
                    turn_logits(i)
            pe.wait_ge(gate_done.h, gate_done.upto(i, 1))
            for c in range(CHUNKS):
                if c >= 2:
                    pe.wait_ge(gt_done.h, gt_done.upto(i, c - 1))
                else:
                    pe.wait_ge(mul_done[2].h, mul_done[2].upto(i, CHUNKS))
                pe.sem_inc(passed.h, 1)
                for q in range(4):
                    last = nc.tensor.transpose(
                        bank(6 + c % 2)[0:GROWS, :].bitcast(BF16)[:, ROWS2 * q:ROWS2 * q + ROWS2],
                        gate3[:, CHUNKS * q + c].rearrange("p k n -> p (k n)"), ident_b[0:ROWS2, 0:ROWS2])
                last.then_inc(gt_mm.h, 1)
        end_of_phase1(pe)

        pe.wait_ge(m_wloaded.h, PRIME + 16 * MLOADS)
        for e in range(E):
            for m in range(2):
                last = mm(bank(7)[:, 2 * e + m:2 * e + m + 1], w1[0:CH, e, 128 * m:128 * m + 128], be[0:CH, e:e + 1],
                          start=True, stop=True)
        last.then_inc(m_bias_mm.h, 1)
        pe.wait_ge(m_step.h, PRIME + M_STEPS)

        def spread_gate(i, n):
            c, e = n // E, n % E
            if n % (2 * E) == 0:
                pe.wait_ge(half_in[c // 2].h, half_in[c // 2].upto(i, 3))
            pe.wait_ge(wr_done.h, wr_done.upto(i, n))
            mm(bank(7)[:, 0:CW], sel_b[:, e, :], gatel[:, c // 2, (c % 2) * CW:(c % 2) * CW + CW],
               start=True, stop=True).then_inc(wr_mm.h, 1)

        def expand(i, n, m):
            c, e = n // E, n % E
            if m == 0 and e == 0:
                pe.wait_ge(xs_done.h, xs_done.upto(i, c + 1))
            pe.wait_ge(g_done.h, g_done.upto(i, 2 * n + m - 1))
            hs = slice(128 * m, 128 * m + 128)
            for part, w in enumerate((w1hi, w1lo)):
                for j in range(2):
                    last = mm(bank(2 * m + j)[:, 0:CW], w[:, e, hs], xs[:, c % 2, j, :],
                              start=(part == 0), stop=(part == 1))
            last.then_inc(a_mm.h, 1)

        def contract(i, n):
            e = n % E
            pe.wait_ge(yw_done.h, yw_done.upto(i, n - 1))
            for m in range(2):
                pe.wait_ge(g_done.h, g_done.upto(i, 2 * n + m + 1))
                for j in range(2):
                    last = mm(bank(4 + n % 2)[64 * j:64 * j + 64, 0:CW], w2[:, e, m, :], g[:, (2 * n + m) % 4, j, :],
                              start=(m == 0), stop=(m == 1))
            last.then_inc(y_mm.h, 1)

        def turn_out(i, c):
            pe.wait_ge(acc_done.h, acc_done.upto(i, (c + 1) * E))
            pe.wait_ge(ot_done.h, ot_done.upto(i, c))
            for q in range(4):
                last = nc.tensor.transpose(bank(6)[0:ROWS2, 128 * q:128 * q + 128],
                                           acc[:, c % 2, ROWS2 * q:ROWS2 * q + ROWS2], ident)
            last.then_inc(ot_mm.h, 1)

        def m_iteration(i, preceded):
            for n in range(C2 * E):
                spread_gate(i, n)
                expand(i, n, 0)
                expand(i, n, 1)
                if n >= 1 or preceded:
                    contract(i, n - 1)
                if n % E == 2 and (n > E or preceded):
                    turn_out(i, n // E - 1)

        m_iteration(0, False)
        with pe.Fori(1, IMAGES) as i:
            m_iteration(i, True)
        contract(IMAGES, -1)
        turn_out(IMAGES, -1)


_OUT = (IMAGES, SIDE, SIDE, CH)


def kernel(**inputs):
    import numpy as np
    import concourse.bacc as bacc
    from concourse import mybir as mb
    from concourse.bass_utils import run_bass_kernel_spmd

    a = {k: np.asarray(v) for k, v in inputs.items()}

    def flipped(w):
        return w[:, 0, ::-1, ::-1].reshape(w.shape[0], -1)

    arrays = {
        "x": a["x"],
        "const": constants(),
        "qkv_wT": a["L0_conv_qkv_w"].T,
        "qkv_b": a["L0_conv_qkv_b"],
        "conv3f": flipped(a["L0_conv_conv3_w"]),
        "conv5f": flipped(a["L0_conv_conv5_w"]),
        "conv7f": flipped(a["L0_conv_conv7_w"]),
        "ffn_in_wT": a["L0_conv_ffn_in_w"].T,
        "ffn_out_w": a["L0_conv_ffn_out_w"],
        "ln_g": a["L0_conv_ln_g"],
        "ln_b": a["L0_conv_ln_b"],
        "W_ihT": a["L1_attn_W_ih"].T,
        "W_hhT": a["L1_attn_W_hh"].T,
        "b_ih": a["L1_attn_b_ih"],
        "b_hh": a["L1_attn_b_hh"],
        "Wr": a["L1_ffn_Wr"],
        "br": a["L1_ffn_br"],
        "ln_geT": a["L1_ffn_ln_g"].T,
        "ln_beT": a["L1_ffn_ln_b"].T,
        "W1": a["L1_ffn_W1"],
        "b1P": a["L1_ffn_b1"].reshape(EXPERTS, 2, 128).transpose(2, 0, 1),
        "W2": a["L1_ffn_W2"],
        "sel": selectors(),
        "b2T": a["L1_ffn_b2"].T,
    }
    arrays = {k: np.ascontiguousarray(v) for k, v in arrays.items()}
    nc = bacc.Bacc("TRN2", target_bir_lowering=False, num_devices=1)
    aps = {k: nc.dram_tensor(f"in_{k}", v.shape, mb.dt.from_np(v.dtype), kind="ExternalInput").ap()
           for k, v in arrays.items()}
    aps["out"] = nc.dram_tensor("out_y", _OUT, mb.dt.float32, kind="ExternalOutput").ap()
    build(nc, aps)
    r = run_bass_kernel_spmd(nc, [{f"in_{k}": v for k, v in arrays.items()}], core_ids=[0])
    return r.results[0]["out_y"]
```

```python
from contextlib import ExitStack

import concourse.bass as bass
from concourse import mybir

F32 = mybir.dt.float32
F32R = mybir.dt.float32r
BF16 = mybir.dt.bfloat16
ALU = mybir.AluOpType
ACT = mybir.ActivationFunctionType
AX = mybir.AxisListType

IMAGES, SIDE, CH = 32, 56, 64
WS = 7
TOK = WS * WS
HEADS, HD = 4, 16
EXPERTS, HID = 8, 256
LN_EPS = 1e-5
PAD = 64
GROUP = 2
CHUNKS = 4 * GROUP
CW = 8 * TOK
UNITS = 4 * CHUNKS
PAIRS = 2 * UNITS
ROWS2 = 2 * TOK
HW2 = CW * 2
HALVES = IMAGES * 2
BIG = 3.0e38
OFF = 2 * WS - 1
ITERS = IMAGES // GROUP
WLOADS = 32
MLOADS = 7
PREP_STEPS = 11
M_STEPS = 5
ROUTER_STEPS = 21
TH_STEP = 12
GC = 4
GRP = CHUNKS // GC
PARTS = 3
GROWS = PARTS * 2 * EXPERTS
HC = CW // 2
WINDOW = 64 + 2 * GC - 2
CONSTS = 2 * 128 + WINDOW + 128 * 2 * GC + HEADS + EXPERTS
PRIME = 40


class Sem:

    def __init__(self, handle, per, step=1):
        self.h, self.per, self.step = handle, per, step

    def upto(self, i, n):
        return i * (self.per * self.step) + (PRIME + n) * self.step


def row_of(k):
    return (k % 2) * (GC // 2) + k // 2


def constants():
    import numpy as np

    c = np.zeros((128, CONSTS), np.float32)
    eye = np.eye(128, dtype=np.float32)
    mean = np.kron(np.eye(2), np.full((CH, CH), 1.0 / CH)).astype(np.float32)
    c[:, 0:128] = eye
    c[:, 128:256] = eye - mean
    for copy in range(2):
        for j in range(2):
            c[64 * j:64 * j + 64, 256 + 2 * GC - 2 + 32 * copy + j] = 1.0 / CH
            for part in range(2):
                for k in range(GC):
                    lo = 256 + WINDOW + 128 * (2 * k + part) + 64 * j
                    c[64 * part + 32 * copy + 2 * row_of(k) + j, lo:lo + 64] = 1
    for h in range(HEADS):
        c[:, CONSTS - 12 + h] = (np.arange(128) % CH) // HD == h
    c[:, CONSTS - 8:] = EXPERTS - np.arange(EXPERTS)
    return c


def selectors():
    import numpy as np

    c = np.zeros((PARTS, 2, EXPERTS, EXPERTS, 2, CH), np.float32)
    for j in range(2):
        for e in range(EXPERTS):
            c[:, j, e, e, j, :] = 1
    return c.reshape(GROWS, EXPERTS, 128)


def build(nc, A):
    with ExitStack() as ctx:
        program(nc, A, ctx)


def program(nc, A, ctx):
    def sb(name, shape, dt=F32, to=ctx):
        return to.enter_context(nc.sbuf_tensor(name, shape, dt))

    all_sems = []

    def sem(name, per=1, step=1):
        s = Sem(ctx.enter_context(nc.semaphore(name)), per, step)
        all_sems.append(s)
        return s

    PS = ctx.enter_context(nc.psum_tensor("banks", [128, 8, 512], F32))

    def bank(b):
        return PS[:, b, :]

    t2_dram = nc.dram_tensor("t2_scratch", (HALVES, 128, HW2), F32, kind="Internal").ap()
    xn_dram = nc.dram_tensor("xn_scratch", (HALVES, 128, HW2), F32, kind="Internal").ap()
    gate_dram = nc.dram_tensor("gate_scratch", (HALVES + CHUNKS // 2, GROWS, HW2), BF16, kind="Internal").ap()
    taps_dram = nc.dram_tensor("taps_scratch", (WS, CH, OFF * WS), F32, kind="Internal").ap()

    const = sb("const", [128, CONSTS])
    ident = const[:, 0:128]
    centre = const[:, 128:256]
    mean_rows = const[:, 256:256 + WINDOW]
    rows_back = const[:, 256 + WINDOW:256 + WINDOW + 128 * 2 * GC]
    headmask = const[:, CONSTS - 12:CONSTS - 8]
    rank = const[0:ROWS2, CONSTS - 8:CONSTS]

    b1 = sb("b1", [128, EXPERTS, 2])
    b2 = sb("b2", [128, EXPERTS])
    ge = sb("ge", [128, EXPERTS])
    be = sb("be", [128, EXPERTS])

    phase1 = ExitStack()

    def sa(name, shape, dt=F32):
        return sb(name, shape, dt, phase1)

    small = sa("small", [128, 16])
    bq, bk, lng, lnb, brnn, brnn2, eps_c, eps2_c, lnb_c = (small[:, k:k + 1] for k in range(9))
    wq = sa("wq", [128, 128])
    wk = sa("wk", [128, 128])
    wv = sa("wv", [128, 128])
    bv = sa("bv", [128, CH])
    w_in = sa("w_in", [128, 128])
    w_out = sa("w_out", [128, 128])
    w_outc = sa("w_outc", [128, 128])
    w_ih = sa("w_ih", [128, 128])
    w_hh = sa("w_hh", [128, 128])
    w_r = sa("w_r", [128, 2 * EXPERTS])
    wr_rows = sa("wr_rows", [128, 2 * 48 + 2 * EXPERTS])
    b_r = sa("b_r", [ROWS2, 2 * EXPERTS])
    conv_m = sa("conv_m", [128, CH, 2, PAD])
    x_in = sa("x_in", [ROWS2, GROUP, 2, 2, 8, CH])
    xT = sa("xT", [128, GROUP, 4, 8, PAD])
    q_diag = sa("q_diag", [128, 2, 8, 2, PAD])
    k_sb = sa("k_sb", [128, 1, 8, TOK])
    k_heads = sa("k_heads", [128, 2, 8, HEADS, TOK])
    v_tok = sa("v_tok", [128, 2, 4, 2, CH])
    v_all = sa("v_all", [128, PAIRS, CH])
    v_heads = sa("v_heads", [128, 2, 4, HEADS, 2, 2, HD + 1])
    probs = sa("probs", [128, 3, HEADS, 2, PAD])
    probsT = sa("probsT", [128, 2, 512])
    rden = sa("rden", [128, 2, 4, 2])
    xo = sa("xo", [128, PAIRS, CH])
    xoT = sa("xoT", [128, CHUNKS * CW])
    ffn_u = sa("ffn_u", [128, CHUNKS * CW])
    hid = sa("hid", [128, 4 * CW])
    sq = sa("sq", [128, 2, CW])
    sd = sa("sd", [128, GRP, HC])
    var_rows = sa("var_rows", [128, GRP, HC])
    rs = sa("rs", [128, GRP, HC])
    rs_parts = sa("rs_parts", [128, GRP, HC], F32R)
    from_rows = sa("from_rows", [128, 2 * GC, 128], F32R)
    th = sa("th", [128, 2, CW])
    lg = sa("lg", [ROWS2, 2 * UNITS, EXPERTS])
    oh1 = sa("oh1", [ROWS2, 2 * UNITS, EXPERTS])
    gate3 = sa("gate3", [ROWS2, UNITS, PARTS, 2 * EXPERTS], BF16)
    ident_b = sa("ident_b", [128, 128], BF16)
    r_small = sa("r_small", [128, 8, 2 * UNITS])
    mx = sa("mx", [128, 2, 8])
    tT = [xT[:, c // 4, c % 4, :, 0:TOK] for c in range(CHUNKS)]
    z1 = xoT
    t2 = ffn_u
    dev = xoT
    lg_rows = sq[:, 0, :]
    gate_rest = oh1
    gate = lg
    x_rows = xo[0:ROWS2].rearrange("p (m u w s) k -> p m u w s k", m=GROUP, u=2, w=8)
    gateT = xoT[0:GROWS, 0:CHUNKS * CW // 2].bitcast(BF16)
    oh2 = xoT[0:ROWS2, CHUNKS * CW // 2:CHUNKS * CW // 2 + 2 * UNITS * EXPERTS].rearrange("p (g e) -> p g e", e=EXPERTS)
    taps = ffn_u[0:CH, 0:OFF * OFF]
    spread = ffn_u[0:CH, OFF * OFF:OFF * OFF + WS * OFF * WS].rearrange("p (x u v) -> p x u v", x=WS, u=OFF)
    raw3, raw5, raw7 = lg[0:CH, 0:2, :], lg[0:CH, 8:12, :], lg[0:CH, 16:23, :]
    raw3 = raw3.rearrange("p a b -> p (a b)")[:, 0:9]
    raw5 = raw5.rearrange("p a b -> p (a b)")[:, 0:25]
    raw7 = raw7.rearrange("p a b -> p (a b)")[:, 0:49]
    phase1.close()

    phase2 = ExitStack()

    def sm(name, shape, dt=F32):
        return sb(name, shape, dt, phase2)

    w1 = sm("w1", [128, EXPERTS, HID])
    w2 = sm("w2", [128, EXPERTS, 2, CH])
    w1hi = sm("w1hi", [128, EXPERTS, HID], F32R)
    w1lo = sm("w1lo", [128, EXPERTS, HID], F32R)
    xnl = sm("xnl", [128, 2, HW2])
    t2l = sm("t2l", [128, 2, HW2])
    gatel = sm("gatel", [GROWS, 2, HW2], BF16)
    sel = sm("sel", [GROWS, EXPERTS, 128])
    sel_b = sm("sel_b", [GROWS, EXPERTS, 128], BF16)
    xs = sm("xs", [128, 2, 2, CW], F32R)
    g = sm("g", [128, 4, 2, CW])
    wrep = sm("wrep", [128, 4, CW])
    yw = sm("yw", [128, 4, CW])
    acc = sm("acc", [128, 2, CW])
    ot = sm("ot", [ROWS2, 2, 512])
    phase2.close()

    zeroed = sem("zeroed")
    passed = sem("passed")
    wloaded = sem("wloaded")
    taps_in = sem("taps_in")
    dve_zeroed = sem("dve_zeroed")
    w1_loaded = sem("w1_loaded")
    w2_loaded = sem("w2_loaded")
    sel_loaded = sem("sel_loaded")
    taps_step = sem("taps_step")
    taps_saved = sem("taps_saved")
    conv_w = sem("conv_w")
    prepared = sem("prepared")
    outc_mm = sem("outc_mm")
    phase1_end = sem("phase1_end")

    x_loaded = sem("x_loaded", 8 * GROUP, 16)
    rows_done = sem("rows_done", 1)
    xt_mm = sem("xt_mm", 8)
    xt_done = sem("xt_done", 8)
    q_mm = sem("q_mm", CHUNKS)
    k_mm = sem("k_mm", CHUNKS)
    v_mm = sem("v_mm", CHUNKS)
    q_done = sem("q_done", CHUNKS)
    k_done = sem("k_done", CHUNKS)
    kh_done = sem("kh_done", CHUNKS)
    v_done = sem("v_done", CHUNKS)
    v_swapped = [sem(f"v_swapped{k}", CHUNKS, 16) for k in range(2)]
    vh_done = sem("vh_done", CHUNKS)
    s_mm = sem("s_mm", UNITS)
    max_done = sem("max_done", UNITS)
    sub_done = sem("sub_done", UNITS)
    exp_done = sem("exp_done", UNITS)
    pt_mm = sem("pt_mm", UNITS)
    pt_done = sem("pt_done", UNITS)
    o_mm = sem("o_mm", UNITS)
    rden_done = sem("rden_done", UNITS)
    o_done = sem("o_done", UNITS)
    conv_mm = sem("conv_mm", 8)
    conv_done = sem("conv_done", 8)
    xot_mm = sem("xot_mm", CHUNKS)
    xot_done = sem("xot_done", CHUNKS)
    f_mm = sem("f_mm", CHUNKS)
    th_done = sem("th_done", CHUNKS)
    u_done = sem("u_done", CHUNKS)
    d_mm = [sem(f"d_mm{n}", CHUNKS) for n in range(3)]
    sq_done = [sem(f"sq_done{n}", CHUNKS) for n in range(3)]
    dev_done = [sem(f"dev_done{n}", CHUNKS) for n in range(3)]
    var_mm = [sem(f"var_mm{n}", CHUNKS) for n in range(3)]
    sd_done = [sem(f"sd_done{n}", GRP) for n in range(3)]
    rs_done = [sem(f"rs_done{n}", GRP) for n in range(3)]
    hi_part_done = [sem(f"hi_part_done{n}", GRP) for n in range(3)]
    parts_done = [sem(f"parts_done{n}", GRP) for n in range(3)]
    bc_mm = [sem(f"bc_mm{n}", CHUNKS) for n in range(3)]
    mul_done = [sem(f"mul_done{n}", CHUNKS) for n in range(3)]
    h_mm = sem("h_mm", CHUNKS)
    h_done = sem("h_done", CHUNKS)
    t2_done = sem("t2_done", CHUNKS)
    vrow_done = sem("vrow_done", GRP)
    vt_mm = sem("vt_mm", 1)
    zsd_done = sem("zsd_done", 1)
    lgr_mm = sem("lgr_mm", 1)
    lgr_done = sem("lgr_done", 1)
    lgt_mm = sem("lgt_mm", 1)
    r_step = sem("r_step", ROUTER_STEPS)
    z_step = sem("z_step", 3)
    gth_done = sem("gth_done", 1)
    gate_done = sem("gate_done", 1)
    gt_mm = sem("gt_mm", CHUNKS)
    gt_done = sem("gt_done", CHUNKS)
    t2_stored = sem("t2_stored", CHUNKS, 16)
    xn_stored = sem("xn_stored", CHUNKS, 16)
    gate_stored = sem("gate_stored", 4, 16)

    E = EXPERTS
    C2 = 4
    m_wloaded = sem("m_wloaded")
    m_step = sem("m_step")
    m_bias_mm = sem("m_bias_mm")
    half_in = [sem(f"half_in{k}", 3, 16) for k in range(2)]
    hi_done = sem("hi_done", C2)
    xs_done = sem("xs_done", C2)
    wr_mm = sem("wr_mm", C2 * E)
    wr_done = sem("wr_done", C2 * E)
    a_mm = sem("a_mm", C2 * E * 2)
    g_done = sem("g_done", C2 * E * 2)
    y_mm = sem("y_mm", C2 * E)
    yw_done = sem("yw_done", C2 * E)
    acc_done = sem("acc_done", C2 * E)
    ot_mm = sem("ot_mm", C2)
    ot_done = sem("ot_done", C2)
    out_stored = [sem(f"out_stored{k}", C2, 16) for k in range(2)]

    x_v = A["x"].rearrange("b (a s r u) (c w) k -> b s r u a c (w k)", a=WS, s=2, r=2, u=2, c=WS, w=8)
    out_v = A["out"].rearrange("b (a s r) (c w) k -> b r s a c (w k)", a=WS, s=2, r=4, c=WS, w=8)

    def unit_of_step(n):
        return n + 2 if n < TH_STEP else n + 3

    TH_UNIT = unit_of_step(TH_STEP - 1) + 1
    GATE_UNITS = range(UNITS - CHUNKS // 2, UNITS)
    assert unit_of_step(ROUTER_STEPS) < GATE_UNITS[0]

    def gate_bank(c):
        return bank(c % 2)[0:GROWS, 0:CW // 2].bitcast(BF16)

    def by_window(ap):
        return ap.rearrange("p (w t) -> p w t", t=TOK)

    block = ctx.enter_context(nc.Block())

    def end_of_phase1(eng):
        eng.drain().then_inc(phase1_end.h, 1)
        eng.wait_ge(phase1_end.h, PRIME + 5)

    @block.sync
    def _(sp):
        count = [0]

        def load(dst, src):
            sp.dma_start(dst, src).then_inc(wloaded.h, 16)
            count[0] += 1

        def load_x(image0):
            for m in range(GROUP):
                for s in range(2):
                    for r in range(2):
                        for u in range(2):
                            sp.dma_start(x_in[TOK * r:TOK * r + TOK, m, s, u].rearrange("p w k -> p (w k)"),
                                         x_v[image0 + m, s, r, u]).then_inc(x_loaded.h, 16)

        load(const[:], A["const"])
        load_x(0)
        sp.wait_ge(zeroed.h, PRIME + 1)
        for dst, name in ((raw3, "conv3f"), (raw5, "conv5f"), (raw7, "conv7f")):
            sp.dma_start(dst, A[name]).then_inc(taps_in.h, 16)
        for s in range(2):
            lo, hi = 64 * s, 64 * s + 64
            load(wq[lo:hi, lo:hi], A["qkv_wT"][:, 0:64])
            load(wk[lo:hi, lo:hi], A["qkv_wT"][:, 64:128])
            load(wv[lo:hi, lo:hi], A["qkv_wT"][:, 128:192])
            load(w_in[lo:hi, lo:hi], A["ffn_in_wT"])
            load(w_out[lo:hi, lo:hi], A["ffn_out_w"])
            load(w_ih[lo:hi, lo:hi], A["W_ihT"])
            load(w_hh[lo:hi, lo:hi], A["W_hhT"])
            load(w_r[lo:hi, E * s:E * s + E], A["Wr"])
            load(b_r[:, E * s:E * s + E], A["br"].partition_broadcast(ROWS2))
            load(bq[lo:hi], A["qkv_b"][0:64].unsqueeze(1))
            load(bk[lo:hi], A["qkv_b"][64:128].unsqueeze(1))
            load(lng[lo:hi], A["ln_g"].unsqueeze(1))
            load(lnb[lo:hi], A["ln_b"].unsqueeze(1))
            load(brnn[lo:hi], A["b_ih"].unsqueeze(1))
            load(brnn2[lo:hi], A["b_hh"].unsqueeze(1))
        load(bv[:], A["qkv_b"][128:192].partition_broadcast(128))
        assert count[0] == WLOADS

        def mload(dst, src):
            sp.dma_start(dst, src).then_inc(m_wloaded.h, 16)
            count[0] += 1

        sp.wait_ge(taps_step.h, PRIME + 6)
        sp.dma_start(taps_dram.rearrange("x c n -> c x n"), spread.rearrange("p x u v -> p x (u v)")
                     ).then_inc(taps_saved.h, 16)
        sp.wait_ge(taps_saved.h, PRIME + 16)
        sp.wait_ge(dve_zeroed.h, PRIME + 2)
        for s in range(2):
            for y in range(WS):
                p = 64 * s + WS * y
                sp.dma_start(conv_m[p:p + WS, :, s, 0:TOK],
                             taps_dram[:, :, WS * (WS - 1 - y):WS * (WS - 1 - y) + TOK]).then_inc(conv_w.h, 16)

        count[0] = 0
        for s in range(2):
            lo, hi = 64 * s, 64 * s + 64
            mload(b2[lo:hi], A["b2T"])
            mload(ge[lo:hi], A["ln_geT"])
            mload(be[lo:hi], A["ln_beT"])
        mload(b1[:], A["b1P"])
        assert count[0] == MLOADS

        def swap_values(i, c):
            sp.wait_ge(v_done.h, v_done.upto(i, c + 1))
            row = 8 * (c % CHUNKS)
            for j in range(2):
                to, fro = slice(64 - 64 * j, 128 - 64 * j), slice(64 * j, 64 * j + 64)
                sp.dma_start(v_all[to, row:row + 8, :].rearrange("p (q j) k -> p q j k", j=2)[:, :, j, :],
                             v_tok[fro, c % 2, :, 1 - j, :]).then_inc(v_swapped[c % 2].h, 16)

        def store_gates(i):
            for q in range(4):
                sp.wait_ge(gt_done.h, gt_done.upto(i, 2 * q + 2))
                sp.dma_start(gate_dram[i * 4 + q], gateT[:, q * HW2:q * HW2 + HW2]).then_inc(gate_stored.h, 16)

        def iteration(i, following):
            sp.wait_ge(rows_done.h, rows_done.upto(i, 1))
            load_x((i + 1 if following else i) * GROUP)
            for c in range(1, CHUNKS):
                swap_values(i, c)
            store_gates(i)
            for c in range(CHUNKS):
                sp.wait_ge(t2_done.h, t2_done.upto(i, c + 1))
                sp.dma_start(t2_dram[i * 4 + c // 2, :, (c % 2) * CW:(c % 2) * CW + CW],
                             t2[:, c * CW:c * CW + CW]).then_inc(t2_stored.h, 16)
            for c in range(CHUNKS):
                sp.wait_ge(mul_done[2].h, mul_done[2].upto(i, c + 1))
                sp.dma_start(xn_dram[i * 4 + c // 2, :, (c % 2) * CW:(c % 2) * CW + CW],
                             dev[:, c * CW:c * CW + CW]).then_inc(xn_stored.h, 16)
            swap_values(i, CHUNKS)

        swap_values(0, 0)
        with sp.Fori(0, ITERS - 1) as i:
            iteration(i, True)
        iteration(ITERS - 1, False)
        store_gates(ITERS)
        sp.wait_ge(t2_stored.h, t2_stored.upto(ITERS, 0))
        sp.wait_ge(xn_stored.h, xn_stored.upto(ITERS, 0))
        sp.wait_ge(gate_stored.h, gate_stored.upto(ITERS, 4))
        sp.wait_ge(v_swapped[0].h, v_swapped[0].upto(ITERS, 2))
        end_of_phase1(sp)

        for s in range(2):
            sp.dma_start(w1[64 * s:64 * s + 64], A["W1"].rearrange("e k h -> k e h")).then_inc(w1_loaded.h, 16)
        for m in range(2):
            sp.dma_start(w2[:, :, m, :], A["W2"].rearrange("e (m h) k -> m h e k", m=2)[m]).then_inc(w2_loaded.h, 16)
        sp.dma_start(sel[:], A["sel"]).then_inc(sel_loaded.h, 16)

        def load_half(image, k):
            half = image * 2 + k
            sp.dma_start(xnl[:, k, :], xn_dram[half]).then_inc(half_in[k].h, 16)
            sp.dma_start(gatel[:, k, :], gate_dram[image * 2 + (k + CHUNKS // 2)]).then_inc(half_in[k].h, 16)
            sp.dma_start(t2l[:, k, :], t2_dram[half]).then_inc(half_in[k].h, 16)

        for k in range(2):
            load_half(0, k)

        def m_iteration(i, following):
            for c in range(C2):
                sp.wait_ge(ot_done.h, ot_done.upto(i, c + 1))
                for s in range(2):
                    sp.dma_start(out_v[i, c, s], ot[TOK * s:TOK * s + TOK, c % 2, :]).then_inc(out_stored[c % 2].h, 16)
                if following and c % 2 == 1:
                    sp.wait_ge(wr_mm.h, wr_mm.upto(i, (c + 1) * E))
                    sp.sem_inc(passed.h, 1)
                    sp.wait_ge(xs_done.h, xs_done.upto(i, c + 2))
                    load_half(i + 1, c // 2)

        with sp.Fori(0, IMAGES - 1) as i:
            m_iteration(i, True)
        m_iteration(IMAGES - 1, False)
        for k in range(2):
            sp.wait_ge(out_stored[k].h, out_stored[k].upto(IMAGES, 0))

    @block.gpsimd
    def _(pool):
        for s in all_sems:
            pool.sem_inc(s.h, PRIME * s.step)
        for t in (wq, wk, wv, w_in, w_out, w_ih, w_hh, w_r, wr_rows):
            nc.gpsimd.memset(t[:], 0.0)
        nc.gpsimd.memset(lg[:], 0.0).then_inc(zeroed.h, 1)
        nc.gpsimd.memset(q_diag[:], 0.0)
        nc.gpsimd.memset(rs_parts[:].bitcast(F32), 0.0)
        nc.gpsimd.memset(probs[:], 0.0)
        nc.gpsimd.memset(hid[:], 0.0)
        nc.gpsimd.memset(v_heads[:], 0.0).then_inc(zeroed.h, 1)
        pool.wait_ge(zeroed.h, PRIME + 2)
        for k in range(2):
            part = v_heads[64 * k:64 * k + 64].rearrange("p a w h s i d -> p (a w h s) i d")
            last = nc.gpsimd.memset(part[:, :, k, HD:HD + 1], 20.0)
        last.then_inc(zeroed.h, 1)
        pool.wait_ge(zeroed.h, PRIME + 3)

        def settle():
            pool.sem_inc(passed.h, 1)

        def copy(out, src):
            return nc.gpsimd.tensor_scalar(out, src, 1.0, 1.0, ALU.mult, ALU.mult)

        def heads_of_k(i, c):
            if c % CHUNKS:
                pool.wait_ge(vh_done.h, vh_done.upto(i, c))
            else:
                pool.wait_ge(rows_done.h, rows_done.upto(i, 1 + c // CHUNKS))
            pool.wait_ge(k_done.h, k_done.upto(i, c + 1))
            pool.wait_ge(s_mm.h, s_mm.upto(i, 4 * (c - 1)))
            settle()
            for h in range(HEADS):
                last = nc.gpsimd.tensor_scalar(k_heads[:, c % 2, :, h, :], k_sb[:, 0], headmask[:, h:h + 1], 1.0,
                                               ALU.mult, ALU.mult)
            last.then_inc(kh_done.h, 1)

        def heads_of_v(i, c):
            pool.wait_ge(kh_done.h, kh_done.upto(i, c + 1))
            pool.wait_ge(v_done.h, v_done.upto(i, c + 1))
            pool.wait_ge(o_mm.h, o_mm.upto(i, 4 * (c - 1)))
            if c == CHUNKS:
                pool.wait_ge(conv_mm.h, conv_mm.upto(i, 8))
            settle()
            for j in range(2):
                p = slice(64 * j, 64 * j + 64)
                for s in range(2):
                    copy(v_heads[p, c % 2, :, :, s, j, 0:HD],
                         v_tok[p, c % 2, :, s, :].rearrange("p q (h d) -> p q h d", h=HEADS))
                row = 8 * (c % CHUNKS)
                own = v_all[p, row:row + 8, :].rearrange("p (q j) k -> p q j k", j=2)[:, :, j, :]
                last = copy(own, v_tok[p, c % 2, :, j, :])
            last.then_inc(vh_done.h, 1)

        def regroup_x(i, ahead):
            pool.wait_ge(vh_done.h, vh_done.upto(i, CHUNKS * ahead))
            pool.wait_ge(x_loaded.h, x_loaded.upto(i, 8 * GROUP * (1 + ahead)))
            pool.wait_ge(xot_mm.h, xot_mm.upto(i, CHUNKS * ahead))
            settle()
            for m in range(GROUP):
                for s in range(2):
                    last = copy(x_rows[:, m, :, :, s, :], x_in[:, m, s])
            last.then_inc(rows_done.h, 1)

        regroup_x(0, 0)
        heads_of_k(0, 0)
        heads_of_v(0, 0)
        with pool.Fori(0, ITERS) as i:
            for c in range(1, CHUNKS):
                heads_of_k(i, c)
                heads_of_v(i, c)
            regroup_x(i, 1)
            heads_of_k(i, CHUNKS)
            heads_of_v(i, CHUNKS)
        end_of_phase1(pool)

        def split_x(i, c):
            k = (c % C2) // 2
            pool.wait_ge(acc_done.h, acc_done.upto(i, max(0, (c - 1) * E + 3)))
            if c % 2 == 0:
                pool.wait_ge(half_in[k].h, half_in[k].upto(i + (c == C2), 3))
            pool.wait_ge(a_mm.h, a_mm.upto(i, 2 * E * (c - 1)))
            cols = slice((c % 2) * CW, (c % 2) * CW + CW)
            settle()
            for j in range(2):
                p = slice(64 * j, 64 * j + 64)
                last = copy(xs[p, c % 2, j, :], xnl[p, k, cols])
            last.then_inc(hi_done.h, 1)
            pool.wait_ge(hi_done.h, hi_done.upto(i, c + 1))
            for j in range(2):
                p, other = slice(64 * j, 64 * j + 64), slice(64 - 64 * j, 128 - 64 * j)
                last = nc.gpsimd.tensor_tensor(xs[other, c % 2, j, :], xnl[p, k, cols],
                                               xs[p, c % 2, j, :].bitcast(F32), ALU.subtract)
            last.then_inc(xs_done.h, 1)

        def m_iteration(i, following):
            for c in range(C2):
                for e in range(E):
                    n = c * E + e
                    pool.wait_ge(yw_done.h, yw_done.upto(i, n + 1))
                    if e == 0:
                        pool.wait_ge(ot_mm.h, ot_mm.upto(i, c - 1))
                        other = t2l[:, c // 2, (c % 2) * CW:(c % 2) * CW + CW]
                    else:
                        pool.wait_ge(acc_done.h, acc_done.upto(i, n))
                        if e == 3 and (c + 1 < C2 or following):
                            pool.wait_ge(xs_done.h, xs_done.upto(i, c + 2))
                        other = acc[:, c % 2, :]
                    nc.gpsimd.tensor_tensor(acc[:, c % 2, :], yw[:, n % 4, :], other, ALU.add
                                            ).then_inc(acc_done.h, 1)
                    if e == 2 and (c + 1 < C2 or following):
                        split_x(i, c + 1)

        split_x(0, 0)
        with pool.Fori(0, IMAGES - 1) as i:
            m_iteration(i, True)
        m_iteration(IMAGES - 1, False)

    @block.scalar
    def _(act):
        act.wait_ge(dve_zeroed.h, PRIME + 2)
        act.wait_ge(zeroed.h, PRIME + 3)
        act.wait_ge(prepared.h, PRIME + PREP_STEPS)

        def evacuate_xT(i, ahead, n):
            m, u, wh = n // 4, (n // 2) % 2, n % 2
            act.wait_ge(xt_mm.h, xt_mm.upto(i, 8 * ahead + n + 1))
            if n == 0:
                act.wait_ge(t2_done.h, t2_done.upto(i, CHUNKS * ahead))
                act.wait_ge(d_mm[1].h, d_mm[1].upto(i, CHUNKS * ahead))
            src = bank(n % 4)[:, 0:CW].rearrange("p (w r t) -> p r w t", r=2, t=TOK)
            for r in range(2):
                last = nc.scalar.activation(xT[:, m, 2 * r + u, 4 * wh:4 * wh + 4, 0:TOK], src[:, r], ACT.Copy)
            last.then_inc(xt_done.h, 1)

        def evacuate_qk(i, c):
            act.wait_ge(q_mm.h, q_mm.upto(i, c + 1))
            act.wait_ge(s_mm.h, s_mm.upto(i, 4 * (c - 1)))
            src = bank(0)[:, 0:CW].rearrange("p (w t) -> p w t", t=TOK)
            for s in range(2):
                p = slice(64 * s, 64 * s + 64)
                last = nc.scalar.activation(q_diag[p, c % 2, :, s, 0:TOK], src[p], ACT.Identity,
                                            bias=bq[p], scale=HD ** -0.5)
            last.then_inc(q_done.h, 1)
            act.wait_ge(k_mm.h, k_mm.upto(i, c + 1))
            act.wait_ge(kh_done.h, kh_done.upto(i, c))
            nc.scalar.activation(k_sb[:, 0].rearrange("p w t -> p (w t)"), bank(1)[:, 0:CW], ACT.Identity,
                                 bias=bk).then_inc(k_done.h, 1)

        def exponential(i, u):
            act.wait_ge(sub_done.h, sub_done.upto(i, u + 1))
            v = probs[:, u % 3].rearrange("p h j k -> p (h j) k")[:, :, 0:TOK]
            nc.scalar.activation(v, v, ACT.Exp).then_inc(exp_done.h, 1)

        def evacuate_pt(i, u):
            act.wait_ge(pt_mm.h, pt_mm.upto(i, u + 1))
            act.wait_ge(o_mm.h, o_mm.upto(i, u - 1))
            nc.scalar.activation(probsT[:, u % 2, :], bank(4 + u % 2), ACT.Copy).then_inc(pt_done.h, 1)

        def deviations(i, n, c):
            bias = lnb_c if n == 1 else 0.0
            act.wait_ge(d_mm[n].h, d_mm[n].upto(i, c + 1))
            if c >= 2:
                act.wait_ge(var_mm[n].h, var_mm[n].upto(i, c - 1))
            else:
                act.wait_ge(var_mm[(n - 1) % 3].h, var_mm[(n - 1) % 3].upto(i, CHUNKS if n else 0))
            if n == 0 and c == 0:
                act.wait_ge(lgt_mm.h, lgt_mm.upto(i, 0))
            d = bank(c % 2)[:, 0:CW]
            nc.scalar.activation(sq[:, c % 2, :], d, ACT.Square, bias=bias).then_inc(sq_done[n].h, 1)
            nc.scalar.activation(dev[:, c * CW:c * CW + CW], d, ACT.Identity if n == 1 else ACT.Copy, bias=bias
                                 ).then_inc(dev_done[n].h, 1)

        def root(i, n, grp):
            act.wait_ge(var_mm[n].h, var_mm[n].upto(i, GC * grp + GC))
            act.wait_ge(rs_done[(n - 1) % 3].h, rs_done[(n - 1) % 3].upto(i, (grp + 1) if n else grp + 1 - GRP))
            v = bank(2 + grp)[:, 0:HC]
            if n < 2:
                nc.scalar.activation(sd[:, grp, :], v, ACT.Sqrt, bias=eps_c).then_inc(sd_done[n].h, 1)
                return
            nc.scalar.activation(sd[:, grp, :], v, ACT.Sqrt, bias=eps2_c, scale=1.0 + LN_EPS
                                 ).then_inc(sd_done[n].h, 1)
            act.wait_ge(vt_mm.h, vt_mm.upto(i, 0))
            nc.scalar.activation(var_rows[:, grp, :], v, ACT.Copy).then_inc(vrow_done.h, 1)

        def second_gate(i):
            act.wait_ge(r_step.h, r_step.upto(i, TH_STEP))
            nc.scalar.activation(r_small[0:ROWS2, 5, :], r_small[0:ROWS2, 4, :], ACT.Exp, scale=-1.0
                                 ).then_inc(gth_done.h, 1)

        def evacuate_gates(i, c):
            act.wait_ge(gt_mm.h, gt_mm.upto(i, c + 1))
            act.wait_ge(xn_stored.h, xn_stored.upto(i, 0))
            nc.scalar.activation(gateT[:, c * CW:c * CW + CW], gate_bank(c), ACT.Copy).then_inc(gt_done.h, 1)

        for n in range(8):
            evacuate_xT(0, 0, n)
        evacuate_qk(0, 0)
        with act.Fori(0, ITERS) as i:
            for u in range(UNITS + 2):
                if u % 4 == 0 and u // 4 + 1 < CHUNKS:
                    evacuate_qk(i, u // 4 + 1)
                if u < UNITS:
                    exponential(i, u)
                if u >= 2:
                    evacuate_pt(i, u - 2)
                if u == TH_UNIT:
                    second_gate(i)
                if u in GATE_UNITS:
                    for c in range(2):
                        evacuate_gates(i, 2 * (u - GATE_UNITS[0]) + c)
            for c in range(CHUNKS):
                act.wait_ge(xot_mm.h, xot_mm.upto(i, c + 1))
                act.wait_ge(xn_stored.h, xn_stored.upto(i, 0))
                act.wait_ge(gate_stored.h, gate_stored.upto(i, 4))
                act.wait_ge(gate_done.h, gate_done.upto(i, 1))
                nc.scalar.activation(xoT[:, c * CW:c * CW + CW].rearrange("p (a t) -> p a t", t=TOK),
                                     bank(c % 2).rearrange("p (a t) -> p a t", t=PAD)[:, :, 0:TOK],
                                     ACT.Copy).then_inc(xot_done.h, 1)
            for k in range(CHUNKS + 2):
                if k < CHUNKS:
                    act.wait_ge(f_mm.h, f_mm.upto(i, k + 1))
                    act.wait_ge(u_done.h, u_done.upto(i, k - 1))
                    nc.scalar.activation(th[:, k % 2, :], bank(4 + k % 2)[:, 0:CW], ACT.Tanh, scale=0.5
                                         ).then_inc(th_done.h, 1)
                if k == CHUNKS:
                    root(i, 0, 0)
                if k >= 2:
                    deviations(i, 0, k - 2)
            root(i, 0, 1)
            for c in range(CHUNKS):
                if c == CHUNKS - 3:
                    root(i, 1, 0)
                deviations(i, 1, c)
            root(i, 1, 1)
            for k in range(CHUNKS + 3):
                if 1 <= k <= CHUNKS:
                    c = k - 1
                    act.wait_ge(h_mm.h, h_mm.upto(i, c + 1))
                    act.wait_ge(t2_done.h, t2_done.upto(i, c - 3))
                    nc.scalar.activation(hid[:, (c % 4) * CW:(c % 4) * CW + CW], bank(4 + c % 2)[:, 0:CW], ACT.Tanh,
                                         bias=brnn).then_inc(h_done.h, 1)
                if k == CHUNKS:
                    root(i, 2, 0)
                if k >= 3:
                    deviations(i, 2, k - 3)
            root(i, 2, 1)
            act.wait_ge(lgr_mm.h, lgr_mm.upto(i, 1))
            act.wait_ge(var_mm[2].h, var_mm[2].upto(i, CHUNKS))
            nc.scalar.activation(lg_rows, bank(4)[:, 0:CW], ACT.Copy).then_inc(lgr_done.h, 1)
            for n in range(8):
                evacuate_xT(i, 1, n)
            evacuate_qk(i, CHUNKS)
            act.wait_ge(vt_mm.h, vt_mm.upto(i, 1))
            act.wait_ge(gate_done.h, gate_done.upto(i, 1))
            turned = bank(4)[0:ROWS2].rearrange("p (b g a r) -> p b g a r", b=2, g=GRP, a=2)[:, :, :, :, 0:2 * GC]
            wanted = r_small[0:ROWS2, 7, :].rearrange("p (a b c g k) -> p b g a c k", a=2, b=2, c=2, g=GRP)
            for b in range(2):
                for grp in range(GRP):
                    last = nc.scalar.activation(wanted[:, b, grp],
                                                turned[:, b, grp].rearrange("p a (c k) -> p a c k", c=2),
                                                ACT.Sqrt, bias=eps_c[0:ROWS2])
            last.then_inc(zsd_done.h, 1)
        second_gate(ITERS)
        for c in range(CHUNKS):
            evacuate_gates(ITERS, c)
        end_of_phase1(act)

        act.wait_ge(m_step.h, PRIME + M_STEPS)

        def m_iteration(i):
            for c in range(C2):
                for e in range(E):
                    for m in range(2):
                        n = (c * E + e) * 2 + m
                        act.wait_ge(a_mm.h, a_mm.upto(i, n + 1))
                        act.wait_ge(y_mm.h, y_mm.upto(i, c * E + e - 1))
                        nc.scalar.activation(g[:, n % 4], PS[:, 2 * m:2 * m + 2, 0:CW], ACT.Gelu,
                                             bias=b1[:, e, m:m + 1]).then_inc(g_done.h, 1)

        with act.Fori(0, IMAGES) as i:
            m_iteration(i)

    @block.vector
    def _(dve):
        steps = [0]

        def step(ins):
            steps[0] += 1
            ins.then_inc(prepared.h, 1)
            dve.wait_ge(prepared.h, PRIME + steps[0])

        nc.vector.memset(xT[:], 0.0).then_inc(dve_zeroed.h, 1)
        nc.vector.memset(conv_m[:], 0.0).then_inc(dve_zeroed.h, 1)
        dve.wait_ge(taps_in.h, PRIME + 48)
        grid = taps.rearrange("p (a b) -> p a b", b=OFF)
        nc.vector.memset(taps, 0.0).then_inc(taps_step.h, 1)
        for n, (raw, size) in enumerate(((raw7, 7), (raw5, 5), (raw3, 3))):
            lo = (OFF - size) // 2
            dve.wait_ge(taps_step.h, PRIME + n + 1)
            part = grid[:, lo:lo + size, lo:lo + size]
            nc.vector.scalar_tensor_tensor(part, raw.rearrange("p (a b) -> p a b", b=size), 0.25 * 0.2, part,
                                           ALU.mult, ALU.add).then_inc(taps_step.h, 1)
        dve.wait_ge(taps_step.h, PRIME + 4)
        mid = grid[:, WS - 1:WS, WS - 1:WS]
        nc.vector.tensor_scalar(mid, mid, 1.0, None, ALU.add).then_inc(taps_step.h, 1)
        dve.wait_ge(taps_step.h, PRIME + 5)
        for x in range(WS):
            last = nc.vector.tensor_copy(spread[:, x], grid[:, :, WS - 1 - x:2 * WS - 1 - x])
        last.then_inc(taps_step.h, 1)
        dve.wait_ge(wloaded.h, PRIME + 16 * WLOADS)
        step(nc.vector.scalar_tensor_tensor(wv[:], wv[:], 0.1, ident, ALU.mult, ALU.add))
        step(nc.vector.tensor_copy(from_rows[:].rearrange("p a b -> p (a b)"), rows_back))
        step(nc.vector.tensor_scalar(bv[:], bv[:], 0.1, None, ALU.mult))
        step(nc.vector.tensor_scalar(bq, bq, HD ** -0.5, None, ALU.mult))
        step(nc.vector.tensor_tensor(brnn, brnn, brnn2, ALU.add))
        step(nc.vector.memset(eps_c, LN_EPS))
        step(nc.vector.memset(eps2_c, LN_EPS * LN_EPS))
        step(nc.vector.tensor_copy(ident_b[:], ident))
        dve.wait_ge(outc_mm.h, PRIME + 1)
        step(nc.vector.tensor_scalar(w_outc[:], bank(7)[:, 0:128], 0.25, None, ALU.mult))
        step(nc.vector.tensor_copy(wr_rows[:, 48:48 + 2 * E], bank(7)[:, 128:128 + 2 * E]))
        step(nc.vector.tensor_copy(lnb_c, bank(7)[:, 144:145]))
        assert steps[0] == PREP_STEPS

        def evacuate_v(i, c):
            dve.wait_ge(v_mm.h, v_mm.upto(i, c + 1))
            dve.wait_ge(vh_done.h, vh_done.upto(i, c - 1))
            dve.wait_ge(v_swapped[c % 2].h, v_swapped[c % 2].upto(i, 2 * (c // 2)))
            nc.vector.tensor_tensor(v_tok[:, c % 2].rearrange("p q s k -> p (q s) k"),
                                    bank(0).rearrange("p (n k) -> p n k", k=CH),
                                    bv[:].unsqueeze(1).broadcast_to([128, 8, CH]), ALU.add).then_inc(v_done.h, 1)

        def less_max(i, u):
            sc = bank(2 + u % 2)[:, 0:CW].rearrange("p (g k) -> p g k", k=TOK)
            dve.wait_ge(s_mm.h, s_mm.upto(i, u + 1))
            nc.vector.tensor_reduce(mx[:, u % 2, :], sc, AX.X, ALU.max).then_inc(max_done.h, 1)
            dve.wait_ge(max_done.h, max_done.upto(i, u + 1))
            dve.wait_ge(pt_mm.h, pt_mm.upto(i, u - 2))
            nc.vector.tensor_tensor(probs[:, u % 3].rearrange("p h j k -> p (h j) k")[:, :, 0:TOK], sc,
                                    mx[:, u % 2, :].unsqueeze(2).broadcast_to([128, 8, TOK]), ALU.subtract
                                    ).then_inc(sub_done.h, 1)

        def normalise(i, u):
            dve.wait_ge(o_mm.h, o_mm.upto(i, u + 1))
            o = bank(6 + u % 2)[:, 0:4 * 34].rearrange("p (h j d) -> p h j d", h=HEADS, j=2)
            nc.vector.reciprocal(rden[:, u % 2], o[:, :, :, HD]).then_inc(rden_done.h, 1)
            dve.wait_ge(rden_done.h, rden_done.upto(i, u + 1))
            if u == 0:
                dve.wait_ge(xt_mm.h, xt_mm.upto(i, 8))
            nc.vector.tensor_tensor(
                xo[:, 2 * u:2 * u + 2, :].rearrange("p j (h d) -> p h j d", h=HEADS), o[:, :, :, 0:HD],
                rden[:, u % 2].unsqueeze(3).broadcast_to([128, 4, 2, HD]), ALU.mult).then_inc(o_done.h, 1)

        def inverse_deviation(i, n, grp):
            dve.wait_ge(sd_done[n].h, sd_done[n].upto(i, grp + 1))
            nc.vector.reciprocal(rs[:, grp, :], sd[:, grp, :]).then_inc(rs_done[n].h, 1)
            dve.wait_ge(rs_done[n].h, rs_done[n].upto(i, grp + 1))
            if n:
                dve.wait_ge(bc_mm[n - 1].h, bc_mm[n - 1].upto(i, GC * grp + GC))
            else:
                dve.wait_ge(bc_mm[2].h, bc_mm[2].upto(i, GC * (grp + 1 - GRP)))
            nc.vector.tensor_copy(rs_parts[:, grp, :], rs[:, grp, :]).then_inc(hi_part_done[n].h, 1)
            dve.wait_ge(hi_part_done[n].h, hi_part_done[n].upto(i, grp + 1))
            for lo in (32, 96):
                low = rs_parts[lo:lo + 32, grp, :]
                last = nc.vector.tensor_tensor(low, rs[lo:lo + 32, grp, :], low.bitcast(F32), ALU.subtract)
            last.then_inc(parts_done[n].h, 1)

        def scale(i, n, c):
            cols = slice(c * CW, c * CW + CW)
            dve.wait_ge(bc_mm[n].h, bc_mm[n].upto(i, c + 1))
            dve.wait_ge(dev_done[n].h, dev_done[n].upto(i, c + 1))
            r = bank(6 + c % 2)[:, 0:CW]
            if n == 0:
                nc.vector.scalar_tensor_tensor(tT[c], by_window(dev[:, cols]), lng, by_window(r), ALU.mult, ALU.mult
                                               ).then_inc(mul_done[0].h, 1)
            elif n == 1:
                nc.vector.tensor_tensor(z1[:, cols], dev[:, cols], r, ALU.mult).then_inc(mul_done[1].h, 1)
            else:
                nc.vector.tensor_tensor(dev[:, cols], dev[:, cols], r, ALU.mult).then_inc(mul_done[2].h, 1)

        def residual(i, c):
            cols = slice(c * CW, c * CW + CW)
            dve.wait_ge(h_done.h, h_done.upto(i, c + 1))
            dve.wait_ge(d_mm[0].h, d_mm[0].upto(i, CHUNKS))
            dve.wait_ge(mul_done[0].h, mul_done[0].upto(i, CHUNKS))
            nc.vector.scalar_tensor_tensor(by_window(t2[:, cols]), tT[c], lnb,
                                           by_window(hid[:, (c % 4) * CW:(c % 4) * CW + CW]), ALU.add, ALU.add).then_inc(t2_done.h, 1)

        def scale_logits(i):
            wide = [ROWS2, 2 * UNITS, E]
            dve.wait_ge(zsd_done.h, zsd_done.upto(i, 1))
            nc.vector.reciprocal(r_small[0:ROWS2, 6, :], r_small[0:ROWS2, 7, :]).then_inc(z_step.h, 1)
            dve.wait_ge(z_step.h, z_step.upto(i, 1))
            dve.wait_ge(lgt_mm.h, lgt_mm.upto(i, 1))
            nc.vector.tensor_tensor(lg[:], bank(5)[0:ROWS2].rearrange("p (n e) -> p n e", e=E),
                                    r_small[0:ROWS2, 6, :].unsqueeze(2).broadcast_to(wide), ALU.mult
                                    ).then_inc(z_step.h, 1)
            dve.wait_ge(z_step.h, z_step.upto(i, 2))
            by_pair = lg[:].rearrange("p (n j) e -> p n (j e)", j=2)
            nc.vector.tensor_tensor(by_pair, by_pair, b_r[:].unsqueeze(1).broadcast_to([ROWS2, UNITS, 2 * E]), ALU.add
                                    ).then_inc(z_step.h, 1)

        def route(i, n):
            wide = [ROWS2, 2 * UNITS, E]

            def row(x):
                return r_small[0:ROWS2, x, :]

            def over(x):
                return row(x).unsqueeze(2).broadcast_to(wide)

            if n:
                dve.wait_ge(r_step.h, r_step.upto(i, n))
            else:
                dve.wait_ge(z_step.h, z_step.upto(i, 0))
            oh = oh1 if n < 6 else oh2
            best, first = (0, 1) if n < 6 else (2, 3)
            part = [gate3[:, :, k, :] for k in range(PARTS)]
            whole = gate[:].rearrange("p (u j) e -> p u (j e)", j=2)
            rest = gate_rest[:].rearrange("p (u j) e -> p u (j e)", j=2)
            v = nc.vector
            if n in (0, 6):
                ins = v.tensor_reduce(row(best), lg[:], AX.X, ALU.max)
            elif n in (1, 7):
                if n == 7:
                    dve.wait_ge(xn_stored.h, xn_stored.upto(i, 0))
                ins = v.tensor_tensor(oh[:], lg[:], over(best), ALU.is_equal)
            elif n in (2, 8):
                ins = v.tensor_tensor(oh[:], oh[:], rank.unsqueeze(1).broadcast_to(wide), ALU.mult)
            elif n in (3, 9):
                ins = v.tensor_reduce(row(first), oh[:], AX.X, ALU.max)
            elif n in (4, 10):
                ins = v.tensor_tensor(oh[:], oh[:], over(first), ALU.is_equal)
            elif n == 5:
                ins = v.scalar_tensor_tensor(lg[:], oh[:], -BIG, lg[:], ALU.mult, ALU.add)
            elif n == 11:
                ins = v.tensor_tensor(row(4), row(0), row(2), ALU.subtract)
            elif n == 12:
                dve.wait_ge(gth_done.h, gth_done.upto(i, 1))
                ins = v.tensor_scalar(row(6), row(5), 1.0, None, ALU.add)
            elif n == 13:
                ins = v.reciprocal(row(6), row(6))
            elif n == 14:
                ins = v.tensor_tensor(row(7), row(5), row(6), ALU.mult)
            elif n == 15:
                ins = v.tensor_tensor(oh1[:], oh1[:], over(6), ALU.mult)
            elif n == 16:
                ins = v.tensor_tensor(oh2[:], oh2[:], over(7), ALU.mult)
            elif n == 17:
                ins = v.tensor_tensor(gate[:], oh1[:], oh2[:], ALU.add)
            elif n == 18:
                dve.wait_ge(gt_mm.h, gt_mm.upto(i, 0))
                ins = v.tensor_copy(part[0], whole)
            elif n == 19:
                ins = v.tensor_tensor(rest, whole, part[0], ALU.subtract)
            elif n == 20:
                ins = v.tensor_copy(part[1], rest)
            else:
                ins = v.tensor_tensor(part[2], rest, part[1], ALU.subtract)
            ins.then_inc(r_step.h if n < ROUTER_STEPS else gate_done.h, 1)

        evacuate_v(0, 0)
        with dve.Fori(0, ITERS) as i:
            for u in range(UNITS + 3):
                if u < UNITS:
                    less_max(i, u)
                for n in range(ROUTER_STEPS + 1):
                    if unit_of_step(n) == u:
                        route(i, n)
                if u % 4 == 2 and u // 4 + 1 < CHUNKS:
                    evacuate_v(i, u // 4 + 1)
                if u >= 3:
                    normalise(i, u - 3)
            dve.wait_ge(o_done.h, o_done.upto(i, UNITS))
            for n in range(8):
                dve.wait_ge(conv_mm.h, conv_mm.upto(i, n + 1))
                part = xo[:, :, 8 * n:8 * n + 8].rearrange("p n k -> p k n")
                nc.vector.tensor_tensor(part, bank(n % 2).rearrange("p (k n) -> p k n", n=PAIRS), part, ALU.add
                                        ).then_inc(conv_done.h, 1)
            for c in range(CHUNKS):
                dve.wait_ge(th_done.h, th_done.upto(i, c + 1))
                dve.wait_ge(t2_stored.h, t2_stored.upto(i, 0))
                dve.wait_ge(lgr_mm.h, lgr_mm.upto(i, 0))
                nc.vector.scalar_tensor_tensor(ffn_u[:, c * CW:c * CW + CW], th[:, c % 2, :], 1.0,
                                               bank(4 + c % 2)[:, 0:CW], ALU.add, ALU.mult).then_inc(u_done.h, 1)
            inverse_deviation(i, 0, 0)
            for c in range(CHUNKS):
                scale(i, 0, c)
                if c == 2:
                    inverse_deviation(i, 0, 1)
            inverse_deviation(i, 1, 0)
            for k in range(CHUNKS + 2):
                if k < CHUNKS:
                    scale(i, 1, k)
                if k == 1:
                    inverse_deviation(i, 1, 1)
                if k >= 2:
                    residual(i, k - 2)
            inverse_deviation(i, 2, 0)
            for c in range(CHUNKS):
                scale(i, 2, c)
                if c == 1:
                    inverse_deviation(i, 2, 1)
            evacuate_v(i, CHUNKS)
            scale_logits(i)
        for n in range(ROUTER_STEPS + 1):
            route(ITERS, n)
        end_of_phase1(dve)

        m_steps = [0]

        def mstep(ins):
            m_steps[0] += 1
            ins.then_inc(m_step.h, 1)
            dve.wait_ge(m_step.h, PRIME + m_steps[0])

        dve.wait_ge(m_bias_mm.h, PRIME + 1)
        mstep(nc.vector.tensor_tensor(b1[:].rearrange("p e m -> p (e m)"), bank(7)[:, 0:2 * E],
                                      b1[:].rearrange("p e m -> p (e m)"), ALU.add))
        mstep(nc.vector.tensor_tensor(w1[:], w1[:], ge[:].unsqueeze(2).broadcast_to([128, E, HID]), ALU.mult))
        mstep(nc.vector.tensor_copy(w1hi[:], w1[:]))
        mstep(nc.vector.tensor_tensor(w1lo[:], w1[:], w1hi[:].bitcast(F32), ALU.subtract))
        dve.wait_ge(sel_loaded.h, PRIME + 16)
        mstep(nc.vector.tensor_copy(sel_b[:], sel[:]))
        assert m_steps[0] == M_STEPS

        def spread_gate(i, n):
            dve.wait_ge(wr_mm.h, wr_mm.upto(i, n + 1))
            dve.wait_ge(yw_done.h, yw_done.upto(i, n - 3))
            nc.vector.tensor_copy(wrep[:, n % 4, :], bank(7)[:, 0:CW]).then_inc(wr_done.h, 1)

        def weigh(i, n):
            e = n % E
            dve.wait_ge(y_mm.h, y_mm.upto(i, n + 1))
            dve.wait_ge(wr_done.h, wr_done.upto(i, n + 1))
            dve.wait_ge(acc_done.h, acc_done.upto(i, n - 3))
            nc.vector.scalar_tensor_tensor(yw[:, n % 4, :], bank(4 + n % 2)[:, 0:CW], b2[:, e:e + 1],
                                           wrep[:, n % 4, :], ALU.add, ALU.mult).then_inc(yw_done.h, 1)

        def evacuate_out(i, c):
            dve.wait_ge(ot_mm.h, ot_mm.upto(i, c + 1))
            dve.wait_ge(out_stored[c % 2].h, out_stored[c % 2].upto(i, 2 * (c // 2)))
            nc.vector.tensor_copy(ot[:, c % 2, :], bank(6)[0:ROWS2, :]).then_inc(ot_done.h, 1)

        def m_iteration(i, preceded):
            for n in range(C2 * E):
                spread_gate(i, n)
                if n >= 1 or preceded:
                    weigh(i, n - 1)
                if n % E == 3 and (n > E or preceded):
                    evacuate_out(i, n // E - 1)

        m_iteration(0, False)
        with dve.Fori(1, IMAGES) as i:
            m_iteration(i, True)
        weigh(IMAGES, -1)
        evacuate_out(IMAGES, -1)

    @block.tensor
    def _(pe):
        mm = nc.tensor.matmul
        pe.wait_ge(wloaded.h, PRIME + 16 * WLOADS)
        pe.wait_ge(zeroed.h, PRIME + 3)
        pe.wait_ge(dve_zeroed.h, PRIME + 2)
        mm(bank(7)[:, 0:128], w_out[:], centre, start=True, stop=True)
        mm(bank(7)[:, 128:128 + 2 * E], centre, w_r[:], start=True, stop=True)
        mm(bank(7)[:, 144:145], centre, lnb, start=True, stop=True).then_inc(outc_mm.h, 1)
        pe.wait_ge(prepared.h, PRIME + PREP_STEPS)

        def project_qk(i, c):
            x = xT[:, (c // 4) % GROUP, c % 4, :, 0:TOK]
            if c % CHUNKS == 0:
                pe.wait_ge(xt_done.h, xt_done.upto(i, c + 8))
            else:
                pe.wait_ge(v_done.h, v_done.upto(i, c))
            mm(by_window(bank(0)[:, 0:CW]), wq[:], x, start=True, stop=True).then_inc(q_mm.h, 1)
            if c > 0:
                pe.wait_ge(k_done.h, k_done.upto(i, c))
            mm(by_window(bank(1)[:, 0:CW]), wk[:], x, start=True, stop=True).then_inc(k_mm.h, 1)

        def project_v(i, c):
            pe.wait_ge(q_done.h, q_done.upto(i, c + 1))
            for q in range(4):
                last = mm(bank(0)[:, 128 * q:128 * q + 128],
                          xT[:, (c // 4) % GROUP, c % 4, 2 * q:2 * q + 2, :].rearrange("p a b -> p (a b)"),
                          wv[:], start=True, stop=True)
            last.then_inc(v_mm.h, 1)

        def scores(i, u):
            c, q = u // 4, u % 4
            if q == 0:
                pe.wait_ge(q_done.h, q_done.upto(i, c + 1))
                pe.wait_ge(kh_done.h, kh_done.upto(i, c + 1))
            if u >= 2:
                pe.wait_ge(sub_done.h, sub_done.upto(i, u - 1))
            for j in range(2):
                w = 2 * q + j
                out = bank(2 + u % 2)[:, 0:CW].rearrange("p (h j k) -> p h j k", h=HEADS, j=2)
                last = mm(out[:, :, j, :], q_diag[:, c % 2, w].rearrange("p a b -> p (a b)"),
                          k_heads[:, c % 2, w], start=True, stop=True)
            last.then_inc(s_mm.h, 1)

        def turn_probs(i, u):
            if u == 0:
                pe.wait_ge(z_step.h, z_step.upto(i, 0))
            pe.wait_ge(exp_done.h, exp_done.upto(i, u + 1))
            if u >= 2:
                pe.wait_ge(pt_done.h, pt_done.upto(i, u - 1))
            for h in range(HEADS):
                last = nc.tensor.transpose(bank(4 + u % 2)[:, 128 * h:128 * h + 128],
                                           probs[:, u % 3, h].rearrange("p a b -> p (a b)"), ident)
            last.then_inc(pt_mm.h, 1)

        def attend(i, u):
            c, q = u // 4, u % 4
            if q == 0:
                pe.wait_ge(vh_done.h, vh_done.upto(i, c + 1))
            pe.wait_ge(pt_done.h, pt_done.upto(i, u + 1))
            if u >= 2:
                pe.wait_ge(o_done.h, o_done.upto(i, u - 1))
            else:
                pe.wait_ge(mul_done[2].h, mul_done[2].upto(i, 0))
            for h in range(HEADS):
                for s in range(2):
                    col = 128 * h + 64 * s
                    last = mm(bank(6 + u % 2)[64 * s:64 * s + 64, 34 * h:34 * h + 34], probsT[:, u % 2, col:col + 64],
                              v_heads[:, c % 2, q, h, s].rearrange("p j d -> p (j d)"), start=True, stop=True)
            last.then_inc(o_mm.h, 1)

        def ffn(i, c):
            pe.wait_ge(xot_done.h, xot_done.upto(i, c + 1))
            if c >= 2:
                pe.wait_ge(u_done.h, u_done.upto(i, c - 1))
            else:
                pe.wait_ge(pt_done.h, pt_done.upto(i, UNITS))
            mm(bank(4 + c % 2)[:, 0:CW], w_in[:], xoT[:, c * CW:c * CW + CW], start=True, stop=True
               ).then_inc(f_mm.h, 1)

        def centred(i, n, c):
            cols = slice(c * CW, c * CW + CW)
            out = bank(c % 2)[:, 0:CW]
            if c >= 2:
                pe.wait_ge(sq_done[n].h, sq_done[n].upto(i, c - 1))
                pe.wait_ge(dev_done[n].h, dev_done[n].upto(i, c - 1))
            elif n == 0:
                pe.wait_ge(xot_done.h, xot_done.upto(i, CHUNKS))
            else:
                pe.wait_ge(sq_done[n - 1].h, sq_done[n - 1].upto(i, CHUNKS))
                pe.wait_ge(dev_done[n - 1].h, dev_done[n - 1].upto(i, CHUNKS))
            if n == 0:
                pe.wait_ge(u_done.h, u_done.upto(i, c + 1))
                mm(out, w_outc[:], ffn_u[:, cols], start=True, stop=False)
                mm(out, centre, xoT[:, cols], start=False, stop=True).then_inc(d_mm[0].h, 1)
            elif n == 1:
                pe.wait_ge(mul_done[0].h, mul_done[0].upto(i, c + 1))
                mm(by_window(out), centre, tT[c], start=True, stop=True).then_inc(d_mm[1].h, 1)
            else:
                pe.wait_ge(t2_done.h, t2_done.upto(i, c + 1))
                mm(out, centre, t2[:, cols], start=True, stop=True).then_inc(d_mm[2].h, 1)

        def variance(i, n, c):
            grp, k = c // GC, c % GC
            pe.wait_ge(sq_done[n].h, sq_done[n].upto(i, c + 1))
            if k == 0 and n == 0:
                pe.wait_ge(sub_done.h, sub_done.upto(i, UNITS))
            elif k == 0:
                pe.wait_ge(sd_done[n - 1].h, sd_done[n - 1].upto(i, grp + 1))
            lo = 2 * (GC - 1 - row_of(k))
            for part in range(2):
                last = mm(bank(2 + grp)[64 * part:64 * part + 64, 0:HC], mean_rows[:, lo:lo + 64],
                          sq[:, c % 2, HC * part:HC * part + HC], start=(k == 0), stop=(k == GC - 1))
            last.then_inc(var_mm[n].h, 1)

        def spread_rows(i, n, c):
            grp = c // GC
            pe.wait_ge(parts_done[n].h, parts_done[n].upto(i, grp + 1))
            if c >= 2:
                pe.wait_ge(mul_done[n].h, mul_done[n].upto(i, c - 1))
            elif n == 0:
                pe.wait_ge(o_done.h, o_done.upto(i, UNITS))
            else:
                pe.wait_ge(mul_done[n - 1].h, mul_done[n - 1].upto(i, CHUNKS))
            for part in range(2):
                last = mm(bank(6 + c % 2)[:, HC * part:HC * part + HC], from_rows[:, 2 * (c % GC) + part, :],
                          rs_parts[:, grp, :], start=True, stop=True)
            last.then_inc(bc_mm[n].h, 1)

        def recur(i, c):
            pe.wait_ge(mul_done[1].h, mul_done[1].upto(i, c + 1))
            pe.wait_ge(h_done.h, h_done.upto(i, c - 1 if c >= 2 else c - 3))
            if c < 2:
                pe.wait_ge(u_done.h, u_done.upto(i, CHUNKS))
            out = bank(4 + c % 2)[:, 0:CW]
            mm(out, w_ih[:], z1[:, c * CW:c * CW + CW], start=True, stop=False)
            mm(out, w_hh[:], hid[:, (c % 4) * CW:(c % 4) * CW + CW], start=False, stop=True).then_inc(h_mm.h, 1)

        def logits(i):
            pe.wait_ge(h_done.h, h_done.upto(i, CHUNKS))
            for c in range(CHUNKS):
                lo, p = 16 * (3 - c // 2), 64 * (c % 2)
                last = mm(bank(4)[p:p + 64, 0:CW], wr_rows[:, lo:lo + 64], t2[:, c * CW:c * CW + CW],
                          start=(c < 2), stop=(c >= CHUNKS - 2))
            last.then_inc(lgr_mm.h, 1)

        def turn_variances(i):
            pe.wait_ge(lgr_done.h, lgr_done.upto(i, 1))
            pe.wait_ge(vrow_done.h, vrow_done.upto(i, GRP))
            pe.sem_inc(passed.h, 1)
            for piece in range(2):
                for grp in range(GRP):
                    lo = (GRP * piece + grp) * 128
                    last = nc.tensor.transpose(bank(4)[0:ROWS2, lo:lo + 128],
                                               var_rows[:, grp, ROWS2 * piece:ROWS2 * piece + ROWS2], ident)
            last.then_inc(vt_mm.h, 1)

        def turn_logits(i):
            pe.wait_ge(lgr_done.h, lgr_done.upto(i, 1))
            for q in range(4):
                last = nc.tensor.transpose(bank(5)[0:ROWS2, 128 * q:128 * q + 128],
                                           lg_rows[:, ROWS2 * q:ROWS2 * q + ROWS2], ident)
            last.then_inc(lgt_mm.h, 1)

        def turn_x(i, ahead, n):
            m, u, wh = n // 4, (n // 2) % 2, n % 2
            if n == 0:
                pe.wait_ge(rows_done.h, rows_done.upto(i, 1 + ahead))
                if ahead:
                    pe.wait_ge(sq_done[2].h, sq_done[2].upto(i, CHUNKS))
                    pe.wait_ge(dev_done[2].h, dev_done[2].upto(i, CHUNKS))
            if n == 2 and ahead:
                pe.wait_ge(sd_done[2].h, sd_done[2].upto(i, GRP))
                pe.wait_ge(vrow_done.h, vrow_done.upto(i, GRP))
            if n >= 4:
                pe.wait_ge(xt_done.h, xt_done.upto(i, 8 * ahead + n - 3))
            for w in range(4):
                last = nc.tensor.transpose(bank(n % 4)[:, ROWS2 * w:ROWS2 * w + ROWS2],
                                           x_rows[:, m, u, 4 * wh + w].rearrange("p s k -> p (s k)"),
                                           ident[0:ROWS2, 0:ROWS2])
            last.then_inc(xt_mm.h, 1)

        def turn_gates(i, c):
            if c >= 2:
                pe.wait_ge(gt_done.h, gt_done.upto(i, c - 1))
            else:
                pe.wait_ge(gate_done.h, gate_done.upto(i, 1))
            pe.sem_inc(passed.h, 1)
            for q in range(4):
                last = nc.tensor.transpose(gate_bank(c)[:, ROWS2 * q:ROWS2 * q + ROWS2],
                                           gate3[:, CHUNKS * q + 4 * (c % 2) + c // 2].rearrange("p k n -> p (k n)"),
                                           ident_b[0:ROWS2, 0:ROWS2])
            last.then_inc(gt_mm.h, 1)

        for n in range(8):
            turn_x(0, 0, n)
        project_qk(0, 0)
        project_v(0, 0)
        with pe.Fori(0, ITERS) as i:
            pe.wait_ge(xt_done.h, xt_done.upto(i, 8))
            for u in range(UNITS + 3):
                if u < UNITS:
                    scores(i, u)
                if u % 4 == 0 and u // 4 + 1 < CHUNKS:
                    project_qk(i, u // 4 + 1)
                if u % 4 == 2 and u // 4 + 1 < CHUNKS:
                    project_v(i, u // 4 + 1)
                if 2 <= u < UNITS + 2:
                    turn_probs(i, u - 2)
                if u >= 3:
                    attend(i, u - 3)
                if u == GATE_UNITS[0]:
                    pe.wait_ge(v_done.h, v_done.upto(i, CHUNKS))
                    pe.wait_ge(k_done.h, k_done.upto(i, CHUNKS))
                if u in GATE_UNITS:
                    for c in range(2):
                        turn_gates(i, 2 * (u - GATE_UNITS[0]) + c)
            pe.wait_ge(conv_w.h, PRIME + 16 * 2 * WS)
            pe.wait_ge(gt_done.h, gt_done.upto(i, CHUNKS))
            pe.wait_ge(vh_done.h, vh_done.upto(i, CHUNKS))
            for k in range(2):
                pe.wait_ge(v_swapped[k].h, v_swapped[k].upto(i, CHUNKS))
            for n in range(8):
                if n >= 2:
                    pe.wait_ge(conv_done.h, conv_done.upto(i, n - 1))
                pe.sem_inc(passed.h, 1)
                for k in range(8):
                    for s in range(2):
                        last = mm(bank(n % 2)[64 * s:64 * s + 64, PAIRS * k:PAIRS * k + PAIRS],
                                  conv_m[:, 8 * n + k, s, :], v_all[:, :, 8 * n + k], start=True, stop=True)
                last.then_inc(conv_mm.h, 1)
            pe.wait_ge(conv_done.h, conv_done.upto(i, 8))
            for c in range(CHUNKS):
                if c >= 2:
                    pe.wait_ge(xot_done.h, xot_done.upto(i, c - 1))
                for q in range(4):
                    n = 8 * c + 2 * q
                    last = nc.tensor.transpose(bank(c % 2)[:, 128 * q:128 * q + 128],
                                               xo[:, n:n + 2, :].rearrange("p a b -> p (a b)"), ident)
                last.then_inc(xot_mm.h, 1)
            for k in range(CHUNKS + 3):
                if k < CHUNKS:
                    ffn(i, k)
                if 2 <= k < CHUNKS + 2:
                    centred(i, 0, k - 2)
                if k >= 3:
                    variance(i, 0, k - 3)
            for k in range(CHUNKS + 3):
                if k < CHUNKS:
                    spread_rows(i, 0, k)
                if 2 <= k < CHUNKS + 2:
                    centred(i, 1, k - 2)
                if k >= 3:
                    variance(i, 1, k - 3)
            for k in range(CHUNKS + 4):
                if k < CHUNKS:
                    spread_rows(i, 1, k)
                if 1 <= k < CHUNKS + 1:
                    recur(i, k - 1)
                if 3 <= k < CHUNKS + 3:
                    centred(i, 2, k - 3)
                if k >= 4:
                    variance(i, 2, k - 4)
            for c in range(CHUNKS):
                spread_rows(i, 2, c)
                if c == 1:
                    logits(i)
                if c in (1, 3):
                    for n in range(4):
                        turn_x(i, 1, 2 * (c - 1) + n)
                if c == GC + 1:
                    project_qk(i, CHUNKS)
                    turn_logits(i)
                    turn_variances(i)
            project_v(i, CHUNKS)
        pe.wait_ge(v_done.h, v_done.upto(ITERS, 1))
        pe.wait_ge(k_done.h, k_done.upto(ITERS, 1))
        for c in range(CHUNKS):
            turn_gates(ITERS, c)
        end_of_phase1(pe)

        pe.wait_ge(m_wloaded.h, PRIME + 16 * MLOADS)
        pe.wait_ge(w1_loaded.h, PRIME + 32)
        pe.wait_ge(w2_loaded.h, PRIME + 32)
        for e in range(E):
            for m in range(2):
                last = mm(bank(7)[:, 2 * e + m:2 * e + m + 1], w1[0:CH, e, 128 * m:128 * m + 128], be[0:CH, e:e + 1],
                          start=True, stop=True)
        last.then_inc(m_bias_mm.h, 1)
        pe.wait_ge(m_step.h, PRIME + M_STEPS)

        def spread_gate(i, n):
            c, e = n // E, n % E
            if n % (2 * E) == 0:
                pe.wait_ge(half_in[c // 2].h, half_in[c // 2].upto(i, 3))
            pe.wait_ge(wr_done.h, wr_done.upto(i, n))
            mm(bank(7)[:, 0:CW], sel_b[:, e, :], gatel[:, c // 2, (c % 2) * CW:(c % 2) * CW + CW],
               start=True, stop=True).then_inc(wr_mm.h, 1)

        def expand(i, n, m):
            c, e = n // E, n % E
            if m == 0 and e == 0:
                pe.wait_ge(xs_done.h, xs_done.upto(i, c + 1))
            pe.wait_ge(g_done.h, g_done.upto(i, 2 * n + m - 1))
            hs = slice(128 * m, 128 * m + 128)
            for part, w in enumerate((w1hi, w1lo)):
                for j in range(2):
                    last = mm(bank(2 * m + j)[:, 0:CW], w[:, e, hs], xs[:, c % 2, j, :],
                              start=(part == 0), stop=(part == 1))
            last.then_inc(a_mm.h, 1)

        def contract(i, n):
            e = n % E
            pe.wait_ge(yw_done.h, yw_done.upto(i, n - 1))
            for m in range(2):
                pe.wait_ge(g_done.h, g_done.upto(i, 2 * n + m + 1))
                for j in range(2):
                    last = mm(bank(4 + n % 2)[64 * j:64 * j + 64, 0:CW], w2[:, e, m, :], g[:, (2 * n + m) % 4, j, :],
                              start=(m == 0), stop=(m == 1))
            last.then_inc(y_mm.h, 1)

        def turn_out(i, c):
            pe.wait_ge(acc_done.h, acc_done.upto(i, (c + 1) * E))
            pe.wait_ge(ot_done.h, ot_done.upto(i, c))
            for q in range(4):
                last = nc.tensor.transpose(bank(6)[0:ROWS2, 128 * q:128 * q + 128],
                                           acc[:, c % 2, ROWS2 * q:ROWS2 * q + ROWS2], ident)
            last.then_inc(ot_mm.h, 1)

        def m_iteration(i, preceded):
            for n in range(C2 * E):
                spread_gate(i, n)
                expand(i, n, 0)
                expand(i, n, 1)
                if n >= 1 or preceded:
                    contract(i, n - 1)
                if n % E == 2 and (n > E or preceded):
                    turn_out(i, n // E - 1)

        m_iteration(0, False)
        with pe.Fori(1, IMAGES) as i:
            m_iteration(i, True)
        contract(IMAGES, -1)
        turn_out(IMAGES, -1)


_OUT = (IMAGES, SIDE, SIDE, CH)


def kernel(**inputs):
    import numpy as np
    import concourse.bacc as bacc
    from concourse import mybir as mb
    from concourse.bass_utils import run_bass_kernel_spmd

    a = {k: np.asarray(v) for k, v in inputs.items()}

    def flipped(w):
        return w[:, 0, ::-1, ::-1].reshape(w.shape[0], -1)

    arrays = {
        "x": a["x"],
        "const": constants(),
        "qkv_wT": a["L0_conv_qkv_w"].T,
        "qkv_b": a["L0_conv_qkv_b"],
        "conv3f": flipped(a["L0_conv_conv3_w"]),
        "conv5f": flipped(a["L0_conv_conv5_w"]),
        "conv7f": flipped(a["L0_conv_conv7_w"]),
        "ffn_in_wT": a["L0_conv_ffn_in_w"].T,
        "ffn_out_w": a["L0_conv_ffn_out_w"],
        "ln_g": a["L0_conv_ln_g"],
        "ln_b": a["L0_conv_ln_b"],
        "W_ihT": a["L1_attn_W_ih"].T,
        "W_hhT": a["L1_attn_W_hh"].T,
        "b_ih": a["L1_attn_b_ih"],
        "b_hh": a["L1_attn_b_hh"],
        "Wr": a["L1_ffn_Wr"],
        "br": a["L1_ffn_br"],
        "ln_geT": a["L1_ffn_ln_g"].T,
        "ln_beT": a["L1_ffn_ln_b"].T,
        "W1": a["L1_ffn_W1"],
        "b1P": a["L1_ffn_b1"].reshape(EXPERTS, 2, 128).transpose(2, 0, 1),
        "W2": a["L1_ffn_W2"],
        "sel": selectors(),
        "b2T": a["L1_ffn_b2"].T,
    }
    arrays = {k: np.ascontiguousarray(v) for k, v in arrays.items()}
    nc = bacc.Bacc("TRN2", target_bir_lowering=False, num_devices=1)
    aps = {k: nc.dram_tensor(f"in_{k}", v.shape, mb.dt.from_np(v.dtype), kind="ExternalInput").ap()
           for k, v in arrays.items()}
    aps["out"] = nc.dram_tensor("out_y", _OUT, mb.dt.float32, kind="ExternalOutput").ap()
    build(nc, aps)
    r = run_bass_kernel_spmd(nc, [{f"in_{k}": v for k, v in arrays.items()}], core_ids=[0])
    return r.results[0]["out_y"]
```
